# Optimizing a Trainium2 kernel written in Bass

```python
import numpy as np
import jax
import jax.numpy as jnp

def _softmax(x, axis=-1):
    return jax.nn.softmax(x, axis=axis)

def _gelu(x):
    return jax.nn.gelu(x, approximate=True)

def _silu(x):
    return jax.nn.silu(x)

def _sigmoid(x):
    return jax.nn.sigmoid(x)

def _layernorm(x, axis=-1, eps=1e-05):
    m = jnp.mean(x, axis=axis, keepdims=True)
    v = jnp.var(x, axis=axis, keepdims=True)
    return (x - m) / jnp.sqrt(v + eps)

def _scatter_add(tgt, idx, src, axis=0):
    return tgt.at[idx].add(src)

def _segment_sum(src, seg, n):
    return jax.ops.segment_sum(src, seg, n)
kernel_name = 'mk_perceiver_d4_seqx_r8_adf748'

def setup_inputs(seed: int=0):
    np.random.seed(seed)
    _w = jnp.asarray

    def _rec_inputs():
        import jax
        import jax.numpy as jnp
        _rk = jax.random.key(seed)
        x = -0.0002928 + 1 * jax.random.normal(jax.random.fold_in(_rk, 1), (1, 128, 128), jnp.float32)
        _lenS = 128 - jax.random.randint(jax.random.fold_in(_rk, 7), (1,), 0, max(1, 128 // 4) + 1, jnp.int32)
        _lenS2 = 2048 - jax.random.randint(jax.random.fold_in(_rk, 8), (1,), 0, max(1, 2048 // 4) + 1, jnp.int32)
        _ctx_768P = jax.random.normal(jax.random.fold_in(_rk, 11), (1, 16, 96), jnp.float32)
        _ctx_768c = jax.random.dirichlet(jax.random.fold_in(_rk, 511), 0.3 * jnp.ones((16,), jnp.float32), (1, 2048))
        _ctx_768t = jnp.einsum('bsk,bkd->bsd', _ctx_768c, _ctx_768P)
        _ctx_768t = _ctx_768t * jax.lax.rsqrt(jnp.mean(jnp.square(_ctx_768t)) + 1e-12) * 0.953939
        ctx_768 = -0.00055796 + 0.999787 * (_ctx_768t + 0.3 * jax.random.normal(jax.random.fold_in(_rk, 611), (1, 2048, 96), jnp.float32))
        _validS = jnp.arange(128)[None, :] < _lenS[:, None]
        _validS2 = jnp.arange(2048)[None, :] < _lenS2[:, None]
        _causal = jnp.tril(jnp.ones((128, 128), dtype=bool))
        mask_BxS2_bk0 = jnp.logical_not(jnp.broadcast_to(_validS2[:, :], (1, 2048)))
        mask_BxS2_bf1 = jnp.ones((1, 2048), dtype=bool)
        return (x, ctx_768, mask_BxS2_bk0, mask_BxS2_bf1)
    x, ctx_768, mask_BxS2_bk0, mask_BxS2_bf1 = _rec_inputs()

    def _L0_xattn_setup():
        import jax, jax.numpy as jnp
        import numpy as np
        HEADS = 16
        DIM_HEAD = 64
        key = jax.random.key(seed)
        ks = jax.random.split(key, 7)
        b, n, m = (2, 256, 128)
        query_dim, context_dim = (128, 96)
        inner = HEADS * DIM_HEAD
        s_q = 1.0 / np.sqrt(query_dim)
        s_c = 1.0 / np.sqrt(context_dim)
        s_i = 1.0 / np.sqrt(inner)
        return {'x': jax.random.normal(ks[0], (b, n, query_dim), jnp.float32), 'context': jax.random.normal(ks[1], (b, m, context_dim), jnp.float32), 'Wq': jax.random.normal(ks[2], (query_dim, inner), jnp.float32) * s_q, 'Wk': jax.random.normal(ks[3], (context_dim, inner), jnp.float32) * s_c, 'Wv': jax.random.normal(ks[4], (context_dim, inner), jnp.float32) * s_c, 'Wo': jax.random.normal(ks[5], (inner, query_dim), jnp.float32) * s_i, 'bo': jax.random.normal(ks[6], (query_dim,), jnp.float32) * 0.01}
    _L0_xattn_all = _L0_xattn_setup()
    _L0_xattn_in = {k: v for k, v in _L0_xattn_all.items() if k in ('Wq', 'Wk', 'Wv', 'Wo', 'bo')}
    del _L0_xattn_all

    def _L0_attn_setup():
        import jax, jax.numpy as jnp
        import numpy as np
        D_MODEL = 128
        STATE_DIM = 32
        key = jax.random.key(seed)
        ks = jax.random.split(key, 6)
        x = jax.random.normal(ks[0], (8, 512, D_MODEL), dtype=jnp.float32)
        Wa_w = jax.random.normal(ks[1], (STATE_DIM, D_MODEL), dtype=jnp.float32) * 0.01
        Wa_b = jnp.full((STATE_DIM,), 2.2, dtype=jnp.float32)
        B_w = jax.random.uniform(ks[2], (STATE_DIM, D_MODEL), jnp.float32, -1, 1) / np.sqrt(D_MODEL)
        C_w = jax.random.uniform(ks[3], (D_MODEL, STATE_DIM), jnp.float32, -1, 1) / np.sqrt(STATE_DIM)
        D_w = jax.random.uniform(ks[4], (D_MODEL, D_MODEL), jnp.float32, -1, 1) / np.sqrt(D_MODEL)
        return {'x': x, 'Wa_w': Wa_w, 'Wa_b': Wa_b, 'B_w': B_w, 'C_w': C_w, 'D_w': D_w}
    _L0_attn_all = _L0_attn_setup()
    _L0_attn_in = {k: v for k, v in _L0_attn_all.items() if k in ('Wa_w', 'Wa_b', 'B_w', 'C_w', 'D_w')}
    del _L0_attn_all

    def _L0_ffn_setup():
        import jax, jax.numpy as jnp
        import numpy as np
        HIDDEN = 128
        FFN = 4 * HIDDEN
        NUM_EXPERTS = 8
        TOP_K = 2
        B, S = (4, 256)
        key = jax.random.key(seed)
        ks = jax.random.split(key, 7)
        scale = 0.02
        return {'x': jax.random.normal(ks[0], (B, S, HIDDEN), dtype=jnp.float32), 'gate_w': jax.random.normal(ks[1], (HIDDEN, NUM_EXPERTS), dtype=jnp.float32) * scale, 'gate_b': jnp.zeros((NUM_EXPERTS,), dtype=jnp.float32), 'w1': jax.random.normal(ks[2], (NUM_EXPERTS, HIDDEN, FFN), dtype=jnp.float32) * scale, 'b1': jnp.zeros((NUM_EXPERTS, FFN), dtype=jnp.float32), 'w2': jax.random.normal(ks[3], (NUM_EXPERTS, FFN, HIDDEN), dtype=jnp.float32) * scale, 'b2': jnp.zeros((NUM_EXPERTS, HIDDEN), dtype=jnp.float32)}
    _L0_ffn_all = _L0_ffn_setup()
    _L0_ffn_in = {k: v for k, v in _L0_ffn_all.items() if k in ('gate_w', 'gate_b', 'w1', 'b1', 'w2', 'b2')}
    del _L0_ffn_all

    def _L1_xattn_setup():
        import jax, jax.numpy as jnp
        import numpy as np
        NUM_HEADS = 16
        CLAMP = 10000.0
        key = jax.random.key(seed)
        ks = jax.random.split(key, 8)
        B, Nq, Nkv, Cq, Ckv = (4, 256, 256, 128, 96)
        s_q = 1.0 / np.sqrt(Cq)
        s_kv = 1.0 / np.sqrt(Ckv)
        return {'query': jax.random.normal(ks[0], (B, Nq, Cq), jnp.float32), 'key_value': jax.random.normal(ks[1], (B, Nkv, Ckv), jnp.float32), 'Wq': jax.random.normal(ks[2], (Cq, Cq), jnp.float32) * s_q, 'bq': jnp.zeros((Cq,), jnp.float32), 'Wk': jax.random.normal(ks[3], (Ckv, Cq), jnp.float32) * s_kv, 'bk': jnp.zeros((Cq,), jnp.float32), 'Wv': jax.random.normal(ks[4], (Ckv, Cq), jnp.float32) * s_kv, 'bv': jnp.zeros((Cq,), jnp.float32), 'Wo': jax.random.normal(ks[5], (Cq, Cq), jnp.float32) * s_q, 'bo': jnp.zeros((Cq,), jnp.float32)}
    _L1_xattn_all = _L1_xattn_setup()
    _L1_xattn_in = {k: v for k, v in _L1_xattn_all.items() if k in ('Wq', 'bq', 'Wk', 'bk', 'Wv', 'bv', 'Wo', 'bo')}
    del _L1_xattn_all

    def _L1_attn_setup():
        import jax, jax.numpy as jnp
        import numpy as np
        B, L, D_MODEL = (2, 128, 128)
        D_STATE, D_CONV, EXPAND = (16, 4, 2)
        D_INNER = D_MODEL * EXPAND
        LN_EPS = 1e-05

        def _forward(x, in_proj_w, conv_w, conv_b, x_proj_w, A_log, D_param, dt_w, dt_b, out_w, ln_g, ln_b):
            Lq = x.shape[1]
            xz = jnp.einsum('bld,ed->ble', x, in_proj_w)
            xb, z = (xz[..., :D_INNER], xz[..., D_INNER:])
            xpad = jnp.pad(xb, ((0, 0), (D_CONV - 1, 0), (0, 0)))
            xc = conv_b
            for k in range(D_CONV):
                xc = xc + xpad[:, k:k + Lq, :] * conv_w[:, k]
            xb = jax.nn.silu(xc)
            proj = jnp.einsum('bld,ed->ble', xb, x_proj_w)
            dt_in = proj[..., :1]
            Bp = proj[..., 1:1 + D_STATE]
            Cp = proj[..., 1 + D_STATE:]
            dt = jax.nn.softplus(dt_in * dt_w[:, 0] + dt_b)
            A = -jnp.exp(A_log)
            dA = jnp.exp(dt[..., None] * A)
            x_scaled = (xb * dt)[..., None] * Bp[..., None, :]

            def comb(a, b):
                return (a[0] * b[0], b[0] * a[1] + b[1])
            _, h = jax.lax.associative_scan(comb, (dA, x_scaled), axis=1)
            y = jnp.einsum('bldn,bln->bld', h, Cp) + xb * D_param
            mu = jnp.mean(y, axis=-1, keepdims=True)
            var = jnp.var(y, axis=-1, keepdims=True)
            y = (y - mu) / jnp.sqrt(var + LN_EPS) * ln_g + ln_b
            y = y * jax.nn.silu(z)
            return jnp.einsum('bld,ed->ble', y, out_w)
        key = jax.random.key(seed)
        ks = jax.random.split(key, 6)
        g = lambda k, shape, scale: jax.random.normal(k, shape, jnp.float32) * scale
        x = jax.random.normal(ks[0], (B, L, D_MODEL), jnp.float32)
        in_proj_w = g(ks[1], (2 * D_INNER, D_MODEL), D_MODEL ** (-0.5))
        conv_w = g(ks[2], (D_INNER, D_CONV), D_CONV ** (-0.5))
        conv_b = jnp.zeros((D_INNER,), jnp.float32)
        x_proj_w = g(ks[3], (2 * D_STATE + 1, D_INNER), D_INNER ** (-0.5))
        A_log = jnp.tile(jnp.log(jnp.arange(1, D_STATE + 1, dtype=jnp.float32)), (D_INNER, 1))
        D_param = jnp.ones((D_INNER,), jnp.float32)
        dt_w = g(ks[4], (D_INNER, 1), 1.0)
        dt_b = jnp.full((D_INNER,), -4.0, jnp.float32)
        out_w = g(ks[5], (D_MODEL, D_INNER), D_INNER ** (-0.5))
        ln_g = jnp.ones((D_INNER,), jnp.float32)
        ln_b = jnp.zeros((D_INNER,), jnp.float32)
        return dict(x=x, in_proj_w=in_proj_w, conv_w=conv_w, conv_b=conv_b, x_proj_w=x_proj_w, A_log=A_log, D_param=D_param, dt_w=dt_w, dt_b=dt_b, out_w=out_w, ln_g=ln_g, ln_b=ln_b)
    _L1_attn_all = _L1_attn_setup()
    _L1_attn_in = {k: v for k, v in _L1_attn_all.items() if k in ('in_proj_w', 'conv_w', 'conv_b', 'x_proj_w', 'A_log', 'D_param', 'dt_w', 'dt_b', 'out_w', 'ln_g', 'ln_b')}
    del _L1_attn_all

    def _L1_ffn_setup():
        import jax, jax.numpy as jnp
        import numpy as np
        from jax import lax
        HIDDEN = 128
        INTER = 64
        E = 64
        K = 6
        G = 8
        TG = 4
        NSH = 2
        ISH = INTER * NSH

        def _moe_forward(hidden_states, gate_w, gate_bias, eg_w, eu_w, ed_w, sg_w, su_w, sd_w):
            B, S, H = hidden_states.shape
            x = hidden_states.reshape(-1, H)
            T = x.shape[0]
            shared = jax.nn.silu(x @ sg_w.T) * (x @ su_w.T) @ sd_w.T
            logits = x @ gate_w.T
            scores = jax.nn.sigmoid(logits) + gate_bias
            group_scores = scores.reshape(T, G, E // G).max(axis=-1)
            _, sel_groups = lax.top_k(group_scores, TG)
            group_mask = jnp.zeros((T, G), scores.dtype).at[jnp.arange(T)[:, None], sel_groups].set(1.0)
            mask = jnp.repeat(group_mask, E // G, axis=1)
            masked_scores = scores * mask
            topk_w, topk_i = lax.top_k(masked_scores, K)
            topk_w = topk_w / (topk_w.sum(axis=-1, keepdims=True) + 1e-08)
            comb = jnp.zeros((T, E), x.dtype).at[jnp.arange(T)[:, None], topk_i].add(topk_w)
            h = jax.nn.silu(jnp.einsum('th,eih->eti', x, eg_w)) * jnp.einsum('th,eih->eti', x, eu_w)
            routed = jnp.einsum('eti,ehi,te->th', h, ed_w, comb)
            return (shared + routed).reshape(B, S, H)
        key = jax.random.key(seed)
        ks = jax.random.split(key, 9)
        s = 0.02
        return {'hidden_states': jax.random.normal(ks[0], (1, 128, HIDDEN), jnp.float32), 'gate_w': jax.random.normal(ks[1], (E, HIDDEN), jnp.float32) * s, 'gate_bias': jnp.zeros((E,), jnp.float32), 'eg_w': jax.random.normal(ks[2], (E, INTER, HIDDEN), jnp.float32) * s, 'eu_w': jax.random.normal(ks[3], (E, INTER, HIDDEN), jnp.float32) * s, 'ed_w': jax.random.normal(ks[4], (E, HIDDEN, INTER), jnp.float32) * s, 'sg_w': jax.random.normal(ks[5], (ISH, HIDDEN), jnp.float32) * s, 'su_w': jax.random.normal(ks[6], (ISH, HIDDEN), jnp.float32) * s, 'sd_w': jax.random.normal(ks[7], (HIDDEN, ISH), jnp.float32) * s}
    _L1_ffn_all = _L1_ffn_setup()
    _L1_ffn_in = {k: v for k, v in _L1_ffn_all.items() if k in ('gate_w', 'gate_bias', 'eg_w', 'eu_w', 'ed_w', 'sg_w', 'su_w', 'sd_w')}
    del _L1_ffn_all

    def _L2_xattn_setup():
        import jax, jax.numpy as jnp
        import numpy as np
        DIM_IN, DIM_LAT, DIM_HEAD = (96, 128, 64)
        INNER = max(DIM_LAT, DIM_IN)
        HEADS = INNER // DIM_HEAD
        SCALE = DIM_HEAD ** (-0.5)
        RMS_EPS = 1e-08
        LN_EPS = 1e-05

        def layernorm(x, g, b):
            mu = jnp.mean(x, axis=-1, keepdims=True)
            var = jnp.mean((x - mu) ** 2, axis=-1, keepdims=True)
            return (x - mu) * jax.lax.rsqrt(var + LN_EPS) * g + b

        def rmsnorm(x, gamma):
            norm = jnp.sqrt(jnp.sum(x * x, axis=-1, keepdims=True)) * x.shape[-1] ** (-0.5)
            return x / jnp.maximum(norm, RMS_EPS) * gamma
        key = jax.random.key(seed)
        ks = jax.random.split(key, 12)
        b, n, m = (4, 512, 64)
        x = jax.random.normal(ks[0], (b, n, DIM_IN), jnp.float32)
        latents = jax.random.normal(ks[1], (b, m, DIM_LAT), jnp.float32)
        mask = jax.random.randint(ks[2], (b, n), 0, 2).astype(bool)
        s = lambda k, sh, fan: jax.random.normal(k, sh, jnp.float32) * fan ** (-0.5)
        return {'x': x, 'latents': latents, 'mask': mask, 'ln_x_g': jnp.ones((DIM_IN,), jnp.float32), 'ln_x_b': jnp.zeros((DIM_IN,), jnp.float32), 'ln_l_g': jnp.ones((DIM_LAT,), jnp.float32), 'ln_l_b': jnp.zeros((DIM_LAT,), jnp.float32), 'qn_g': jnp.ones((DIM_HEAD,), jnp.float32), 'kn_g': jnp.ones((DIM_HEAD,), jnp.float32), 'Wq': s(ks[3], (INNER, DIM_LAT), DIM_LAT), 'Wkv': s(ks[4], (2 * INNER, DIM_IN), DIM_IN), 'Wlkv': s(ks[5], (2 * INNER, DIM_LAT), DIM_LAT), 'Wo': s(ks[6], (DIM_LAT, INNER), INNER), 'bo': jnp.zeros((DIM_LAT,), jnp.float32)}
    _L2_xattn_all = _L2_xattn_setup()
    _L2_xattn_in = {k: v for k, v in _L2_xattn_all.items() if k in ('ln_x_g', 'ln_x_b', 'ln_l_g', 'ln_l_b', 'qn_g', 'kn_g', 'Wq', 'Wkv', 'Wlkv', 'Wo', 'bo')}
    del _L2_xattn_all

    def _L2_attn_setup():
        import jax, jax.numpy as jnp
        import numpy as np
        NUM_HEADS = 16
        D_MODEL = 128
        HEAD_DIM = D_MODEL // NUM_HEADS
        EPS = 1e-06

        def _feature_map(x):
            return jax.nn.elu(x) + 1.0
        key = jax.random.key(seed)
        ks = jax.random.split(key, 9)
        B, S, D = (4, 1024, D_MODEL)
        scale = 1.0 / np.sqrt(D)
        inputs_q = jax.random.normal(ks[0], (B, S, D), dtype=jnp.float32)
        Wq = jax.random.normal(ks[1], (D, D), dtype=jnp.float32) * scale
        Wk = jax.random.normal(ks[2], (D, D), dtype=jnp.float32) * scale
        Wv = jax.random.normal(ks[3], (D, D), dtype=jnp.float32) * scale
        Wo = jax.random.normal(ks[4], (D, D), dtype=jnp.float32) * scale
        bq = jnp.zeros((D,), jnp.float32)
        bk = jnp.zeros((D,), jnp.float32)
        bv = jnp.zeros((D,), jnp.float32)
        bo = jnp.zeros((D,), jnp.float32)
        return {'inputs_q': inputs_q, 'Wq': Wq, 'bq': bq, 'Wk': Wk, 'bk': bk, 'Wv': Wv, 'bv': bv, 'Wo': Wo, 'bo': bo}
    _L2_attn_all = _L2_attn_setup()
    _L2_attn_in = {k: v for k, v in _L2_attn_all.items() if k in ('Wq', 'bq', 'Wk', 'bk', 'Wv', 'bv', 'Wo', 'bo')}
    del _L2_attn_all

    def _L2_ffn_setup():
        import jax, jax.numpy as jnp
        import numpy as np
        TOP_K = 2
        key = jax.random.key(seed)
        k1, k2, k3 = jax.random.split(key, 3)
        B, S, H, E, D = (4, 128, 128, 32, 128)
        x = jax.random.normal(k1, (B, S, H), dtype=jnp.float32)
        router_w = jax.random.normal(k2, (E, H), dtype=jnp.float32) * (1.0 / np.sqrt(H))
        bound = float(np.sqrt(6.0 / ((1.0 + 0.01 ** 2) * H)))
        expert_weights = jax.random.uniform(k3, (E, H, D), dtype=jnp.float32, minval=-bound, maxval=bound)
        return {'x': x, 'router_w': router_w, 'expert_weights': expert_weights}
    _L2_ffn_all = _L2_ffn_setup()
    _L2_ffn_in = {k: v for k, v in _L2_ffn_all.items() if k in ('router_w', 'expert_weights')}
    del _L2_ffn_all

    def _L3_xattn_setup():
        import jax, jax.numpy as jnp
        import numpy as np
        DIM = 128
        CTX_DIM = 96
        HEADS = 16
        key = jax.random.key(seed)
        ks = jax.random.split(key, 7)
        B, N, M = (4, 512, 32)
        x = jax.random.normal(ks[0], (B, N, DIM), dtype=jnp.float32)
        context = jax.random.normal(ks[1], (B, M, CTX_DIM), dtype=jnp.float32)
        context_mask = jnp.ones((B, M), dtype=bool)
        s_d = 1.0 / np.sqrt(DIM)
        s_c = 1.0 / np.sqrt(CTX_DIM)
        Wq = jax.random.normal(ks[2], (DIM, DIM), dtype=jnp.float32) * s_d
        Wk = jax.random.normal(ks[3], (CTX_DIM, DIM), dtype=jnp.float32) * s_c
        Wv = jax.random.normal(ks[4], (CTX_DIM, DIM), dtype=jnp.float32) * s_c
        Wo = jax.random.normal(ks[5], (DIM, DIM), dtype=jnp.float32) * s_d
        return {'x': x, 'context': context, 'context_mask': context_mask, 'Wq': Wq, 'Wk': Wk, 'Wv': Wv, 'Wo': Wo}
    _L3_xattn_all = _L3_xattn_setup()
    _L3_xattn_in = {k: v for k, v in _L3_xattn_all.items() if k in ('Wq', 'Wk', 'Wv', 'Wo')}
    del _L3_xattn_all

    def _L3_attn_setup():
        import jax, jax.numpy as jnp
        import numpy as np
        NUM_HEADS = 16
        key = jax.random.key(seed)
        kx, kq, kk, kv = jax.random.split(key, 4)
        N, S, D = (2, 512, 128)
        scale = 1.0 / np.sqrt(D)
        x = jax.random.normal(kx, (N, S, D), dtype=jnp.float32)
        Wq = jax.random.normal(kq, (D, D), dtype=jnp.float32) * scale
        Wk = jax.random.normal(kk, (D, D), dtype=jnp.float32) * scale
        Wv = jax.random.normal(kv, (D, D), dtype=jnp.float32) * scale
        return {'x': x, 'Wq': Wq, 'Wk': Wk, 'Wv': Wv}
    _L3_attn_all = _L3_attn_setup()
    _L3_attn_in = {k: v for k, v in _L3_attn_all.items() if k in ('Wq', 'Wk', 'Wv')}
    del _L3_attn_all

    def _L3_ffn_setup():
        import jax, jax.numpy as jnp
        import numpy as np
        FEATURES = 128
        D_IN = 128

        def fp8_gemm_optimized(x, input_scale, kernel, kernel_scale):
            s_in = input_scale[0]
            s_k = kernel_scale[0]
            x_q = (x.astype(jnp.float32) / s_in).astype(jnp.float8_e4m3fn)
            k_q = (kernel.astype(jnp.float32) / s_k).astype(jnp.float8_e4m3fn)
            y = jnp.dot(x_q.astype(jnp.float32), k_q.astype(jnp.float32), preferred_element_type=jnp.float32)
            return y * (s_in * s_k)
        key = jax.random.key(seed)
        kx, kk, kb = jax.random.split(key, 3)
        x = jax.random.normal(kx, (4, 1024, D_IN), dtype=jnp.float32)
        limit = np.sqrt(6.0 / (D_IN + FEATURES)).astype(np.float32)
        kernel = jax.random.uniform(kk, (D_IN, FEATURES), dtype=jnp.float32, minval=-limit, maxval=limit).astype(jnp.bfloat16)
        input_scale = jnp.ones((1,), dtype=jnp.float32)
        kernel_scale = jnp.ones((1,), dtype=jnp.float32)
        bias = jnp.zeros((FEATURES,), dtype=jnp.bfloat16)
        return {'x': x, 'kernel': kernel, 'input_scale': input_scale, 'kernel_scale': kernel_scale, 'bias': bias}
    _L3_ffn_all = _L3_ffn_setup()
    _L3_ffn_in = {k: v for k, v in _L3_ffn_all.items() if k in ('kernel', 'input_scale', 'kernel_scale', 'bias')}
    del _L3_ffn_all
    return {'x': x, 'ctx_768': ctx_768, 'mask_BxS2_bk0': mask_BxS2_bk0, 'mask_BxS2_bf1': mask_BxS2_bf1, 'L0_xattn_Wq': _L0_xattn_in['Wq'], 'L0_xattn_Wk': _L0_xattn_in['Wk'], 'L0_xattn_Wv': _L0_xattn_in['Wv'], 'L0_xattn_Wo': _L0_xattn_in['Wo'], 'L0_xattn_bo': _L0_xattn_in['bo'], 'L0_attn_Wa_w': _L0_attn_in['Wa_w'], 'L0_attn_Wa_b': _L0_attn_in['Wa_b'], 'L0_attn_B_w': _L0_attn_in['B_w'], 'L0_attn_C_w': _L0_attn_in['C_w'], 'L0_attn_D_w': _L0_attn_in['D_w'], 'L0_ffn_gate_w': _L0_ffn_in['gate_w'], 'L0_ffn_gate_b': _L0_ffn_in['gate_b'], 'L0_ffn_w1': _L0_ffn_in['w1'], 'L0_ffn_b1': _L0_ffn_in['b1'], 'L0_ffn_w2': _L0_ffn_in['w2'], 'L0_ffn_b2': _L0_ffn_in['b2'], 'L1_xattn_Wq': _L1_xattn_in['Wq'], 'L1_xattn_bq': _L1_xattn_in['bq'], 'L1_xattn_Wk': _L1_xattn_in['Wk'], 'L1_xattn_bk': _L1_xattn_in['bk'], 'L1_xattn_Wv': _L1_xattn_in['Wv'], 'L1_xattn_bv': _L1_xattn_in['bv'], 'L1_xattn_Wo': _L1_xattn_in['Wo'], 'L1_xattn_bo': _L1_xattn_in['bo'], 'L1_attn_in_proj_w': _L1_attn_in['in_proj_w'], 'L1_attn_conv_w': _L1_attn_in['conv_w'], 'L1_attn_conv_b': _L1_attn_in['conv_b'], 'L1_attn_x_proj_w': _L1_attn_in['x_proj_w'], 'L1_attn_A_log': _L1_attn_in['A_log'], 'L1_attn_D_param': _L1_attn_in['D_param'], 'L1_attn_dt_w': _L1_attn_in['dt_w'], 'L1_attn_dt_b': _L1_attn_in['dt_b'], 'L1_attn_out_w': _L1_attn_in['out_w'], 'L1_attn_ln_g': _L1_attn_in['ln_g'], 'L1_attn_ln_b': _L1_attn_in['ln_b'], 'L1_ffn_gate_w': _L1_ffn_in['gate_w'], 'L1_ffn_gate_bias': _L1_ffn_in['gate_bias'], 'L1_ffn_eg_w': _L1_ffn_in['eg_w'], 'L1_ffn_eu_w': _L1_ffn_in['eu_w'], 'L1_ffn_ed_w': _L1_ffn_in['ed_w'], 'L1_ffn_sg_w': _L1_ffn_in['sg_w'], 'L1_ffn_su_w': _L1_ffn_in['su_w'], 'L1_ffn_sd_w': _L1_ffn_in['sd_w'], 'L2_xattn_ln_x_g': _L2_xattn_in['ln_x_g'], 'L2_xattn_ln_x_b': _L2_xattn_in['ln_x_b'], 'L2_xattn_ln_l_g': _L2_xattn_in['ln_l_g'], 'L2_xattn_ln_l_b': _L2_xattn_in['ln_l_b'], 'L2_xattn_qn_g': _L2_xattn_in['qn_g'], 'L2_xattn_kn_g': _L2_xattn_in['kn_g'], 'L2_xattn_Wq': _L2_xattn_in['Wq'], 'L2_xattn_Wkv': _L2_xattn_in['Wkv'], 'L2_xattn_Wlkv': _L2_xattn_in['Wlkv'], 'L2_xattn_Wo': _L2_xattn_in['Wo'], 'L2_xattn_bo': _L2_xattn_in['bo'], 'L2_attn_Wq': _L2_attn_in['Wq'], 'L2_attn_bq': _L2_attn_in['bq'], 'L2_attn_Wk': _L2_attn_in['Wk'], 'L2_attn_bk': _L2_attn_in['bk'], 'L2_attn_Wv': _L2_attn_in['Wv'], 'L2_attn_bv': _L2_attn_in['bv'], 'L2_attn_Wo': _L2_attn_in['Wo'], 'L2_attn_bo': _L2_attn_in['bo'], 'L2_ffn_router_w': _L2_ffn_in['router_w'], 'L2_ffn_expert_weights': _L2_ffn_in['expert_weights'], 'L3_xattn_Wq': _L3_xattn_in['Wq'], 'L3_xattn_Wk': _L3_xattn_in['Wk'], 'L3_xattn_Wv': _L3_xattn_in['Wv'], 'L3_xattn_Wo': _L3_xattn_in['Wo'], 'L3_attn_Wq': _L3_attn_in['Wq'], 'L3_attn_Wk': _L3_attn_in['Wk'], 'L3_attn_Wv': _L3_attn_in['Wv'], 'L3_ffn_kernel': _L3_ffn_in['kernel'], 'L3_ffn_input_scale': _L3_ffn_in['input_scale'], 'L3_ffn_kernel_scale': _L3_ffn_in['kernel_scale'], 'L3_ffn_bias': _L3_ffn_in['bias']}

def reference(x, ctx_768, mask_BxS2_bk0, mask_BxS2_bf1, L0_xattn_Wq, L0_xattn_Wk, L0_xattn_Wv, L0_xattn_Wo, L0_xattn_bo, L0_attn_Wa_w, L0_attn_Wa_b, L0_attn_B_w, L0_attn_C_w, L0_attn_D_w, L0_ffn_gate_w, L0_ffn_gate_b, L0_ffn_w1, L0_ffn_b1, L0_ffn_w2, L0_ffn_b2, L1_xattn_Wq, L1_xattn_bq, L1_xattn_Wk, L1_xattn_bk, L1_xattn_Wv, L1_xattn_bv, L1_xattn_Wo, L1_xattn_bo, L1_attn_in_proj_w, L1_attn_conv_w, L1_attn_conv_b, L1_attn_x_proj_w, L1_attn_A_log, L1_attn_D_param, L1_attn_dt_w, L1_attn_dt_b, L1_attn_out_w, L1_attn_ln_g, L1_attn_ln_b, L1_ffn_gate_w, L1_ffn_gate_bias, L1_ffn_eg_w, L1_ffn_eu_w, L1_ffn_ed_w, L1_ffn_sg_w, L1_ffn_su_w, L1_ffn_sd_w, L2_xattn_ln_x_g, L2_xattn_ln_x_b, L2_xattn_ln_l_g, L2_xattn_ln_l_b, L2_xattn_qn_g, L2_xattn_kn_g, L2_xattn_Wq, L2_xattn_Wkv, L2_xattn_Wlkv, L2_xattn_Wo, L2_xattn_bo, L2_attn_Wq, L2_attn_bq, L2_attn_Wk, L2_attn_bk, L2_attn_Wv, L2_attn_bv, L2_attn_Wo, L2_attn_bo, L2_ffn_router_w, L2_ffn_expert_weights, L3_xattn_Wq, L3_xattn_Wk, L3_xattn_Wv, L3_xattn_Wo, L3_attn_Wq, L3_attn_Wk, L3_attn_Wv, L3_ffn_kernel, L3_ffn_input_scale, L3_ffn_kernel_scale, L3_ffn_bias):
    import jax
    import jax.numpy as jnp

    def _L0_xattn_ref(x, context, Wq, Wk, Wv, Wo, bo):
        import jax, jax.numpy as jnp
        import numpy as np
        HEADS = 16
        DIM_HEAD = 64
        b, n, _ = x.shape
        h, d = (HEADS, DIM_HEAD)
        scale = d ** (-0.5)
        q = (x @ Wq).reshape(b, n, h, d).transpose(0, 2, 1, 3)
        k = (context @ Wk).reshape(b, -1, h, d).transpose(0, 2, 1, 3)
        v = (context @ Wv).reshape(b, -1, h, d).transpose(0, 2, 1, 3)
        sim = jnp.einsum('bhid,bhjd->bhij', q, k) * scale
        attn = jax.nn.softmax(sim, axis=-1)
        out = jnp.einsum('bhij,bhjd->bhid', attn, v)
        out = out.transpose(0, 2, 1, 3).reshape(b, n, h * d)
        return out @ Wo + bo

    def _L0_attn_ref(x, Wa_w, Wa_b, B_w, C_w, D_w):
        import jax, jax.numpy as jnp
        import numpy as np
        D_MODEL = 128
        STATE_DIM = 32
        a = jax.nn.sigmoid(jnp.einsum('bsd,nd->bsn', x, Wa_w) + Wa_b)
        b = jnp.einsum('bsd,nd->bsn', x, B_w)

        def combine(e1, e2):
            a1, b1 = e1
            a2, b2 = e2
            return (a2 * a1, a2 * b1 + b2)
        _, h = jax.lax.associative_scan(combine, (a, b), axis=1)
        y = jnp.einsum('bsn,dn->bsd', h, C_w) + jnp.einsum('bse,de->bsd', x, D_w)
        return y

    def _L0_ffn_ref(x, gate_w, gate_b, w1, b1, w2, b2):
        import jax, jax.numpy as jnp
        import numpy as np
        HIDDEN = 128
        FFN = 4 * HIDDEN
        NUM_EXPERTS = 8
        TOP_K = 2
        B, S = (4, 256)
        b, s, h = x.shape
        xt = x.reshape(b * s, h)
        probs = jax.nn.softmax(xt @ gate_w + gate_b, axis=-1)
        _, idx = jax.lax.top_k(probs, TOP_K)
        one_hot = jax.nn.one_hot(idx, NUM_EXPERTS, dtype=xt.dtype)
        mask = (one_hot.sum(axis=1) > 0).astype(xt.dtype)
        h1 = jax.nn.relu(jnp.einsum('th,ehf->etf', xt, w1) + b1[:, None, :])
        out_e = jnp.einsum('etf,efh->eth', h1, w2) + b2[:, None, :]
        out = jnp.einsum('eth,te->th', out_e, mask)
        return out.reshape(b, s, h)

    def _L1_xattn_ref(query, key_value, Wq, bq, Wk, bk, Wv, bv, Wo, bo):
        import jax, jax.numpy as jnp
        import numpy as np
        NUM_HEADS = 16
        CLAMP = 10000.0
        B, Nq, Cq = query.shape
        Nkv = key_value.shape[1]
        H = NUM_HEADS
        D = Cq // H
        scale = D ** (-0.5)
        q = (query @ Wq + bq).reshape(B, Nq, H, D).transpose(0, 2, 1, 3)
        k = (key_value @ Wk + bk).reshape(B, Nkv, H, D).transpose(0, 2, 1, 3)
        v = (key_value @ Wv + bv).reshape(B, Nkv, H, D).transpose(0, 2, 1, 3)
        attn = jnp.einsum('bhqd,bhkd->bhqk', q, k) * scale
        attn = jnp.clip(attn, -CLAMP, CLAMP)
        attn = jax.nn.softmax(attn, axis=-1)
        attn = jnp.where(jnp.any(jnp.isnan(attn)), jnp.asarray(1.0 / Nkv, attn.dtype), attn)
        x = jnp.einsum('bhqk,bhkd->bqhd', attn, v).reshape(B, Nq, Cq)
        return x @ Wo + bo

    def _L1_attn_ref(x, in_proj_w, conv_w, conv_b, x_proj_w, A_log, D_param, dt_w, dt_b, out_w, ln_g, ln_b):
        import jax, jax.numpy as jnp
        import numpy as np
        B, L, D_MODEL = (2, 128, 128)
        D_STATE, D_CONV, EXPAND = (16, 4, 2)
        D_INNER = D_MODEL * EXPAND
        LN_EPS = 1e-05

        def _forward(x, in_proj_w, conv_w, conv_b, x_proj_w, A_log, D_param, dt_w, dt_b, out_w, ln_g, ln_b):
            Lq = x.shape[1]
            xz = jnp.einsum('bld,ed->ble', x, in_proj_w)
            xb, z = (xz[..., :D_INNER], xz[..., D_INNER:])
            xpad = jnp.pad(xb, ((0, 0), (D_CONV - 1, 0), (0, 0)))
            xc = conv_b
            for k in range(D_CONV):
                xc = xc + xpad[:, k:k + Lq, :] * conv_w[:, k]
            xb = jax.nn.silu(xc)
            proj = jnp.einsum('bld,ed->ble', xb, x_proj_w)
            dt_in = proj[..., :1]
            Bp = proj[..., 1:1 + D_STATE]
            Cp = proj[..., 1 + D_STATE:]
            dt = jax.nn.softplus(dt_in * dt_w[:, 0] + dt_b)
            A = -jnp.exp(A_log)
            dA = jnp.exp(dt[..., None] * A)
            x_scaled = (xb * dt)[..., None] * Bp[..., None, :]

            def comb(a, b):
                return (a[0] * b[0], b[0] * a[1] + b[1])
            _, h = jax.lax.associative_scan(comb, (dA, x_scaled), axis=1)
            y = jnp.einsum('bldn,bln->bld', h, Cp) + xb * D_param
            mu = jnp.mean(y, axis=-1, keepdims=True)
            var = jnp.var(y, axis=-1, keepdims=True)
            y = (y - mu) / jnp.sqrt(var + LN_EPS) * ln_g + ln_b
            y = y * jax.nn.silu(z)
            return jnp.einsum('bld,ed->ble', y, out_w)
        return _forward(x, in_proj_w, conv_w, conv_b, x_proj_w, A_log, D_param, dt_w, dt_b, out_w, ln_g, ln_b)

    def _L1_ffn_ref(hidden_states, gate_w, gate_bias, eg_w, eu_w, ed_w, sg_w, su_w, sd_w):
        import jax, jax.numpy as jnp
        import numpy as np
        from jax import lax
        HIDDEN = 128
        INTER = 64
        E = 64
        K = 6
        G = 8
        TG = 4
        NSH = 2
        ISH = INTER * NSH

        def _moe_forward(hidden_states, gate_w, gate_bias, eg_w, eu_w, ed_w, sg_w, su_w, sd_w):
            B, S, H = hidden_states.shape
            x = hidden_states.reshape(-1, H)
            T = x.shape[0]
            shared = jax.nn.silu(x @ sg_w.T) * (x @ su_w.T) @ sd_w.T
            logits = x @ gate_w.T
            scores = jax.nn.sigmoid(logits) + gate_bias
            group_scores = scores.reshape(T, G, E // G).max(axis=-1)
            _, sel_groups = lax.top_k(group_scores, TG)
            group_mask = jnp.zeros((T, G), scores.dtype).at[jnp.arange(T)[:, None], sel_groups].set(1.0)
            mask = jnp.repeat(group_mask, E // G, axis=1)
            masked_scores = scores * mask
            topk_w, topk_i = lax.top_k(masked_scores, K)
            topk_w = topk_w / (topk_w.sum(axis=-1, keepdims=True) + 1e-08)
            comb = jnp.zeros((T, E), x.dtype).at[jnp.arange(T)[:, None], topk_i].add(topk_w)
            h = jax.nn.silu(jnp.einsum('th,eih->eti', x, eg_w)) * jnp.einsum('th,eih->eti', x, eu_w)
            routed = jnp.einsum('eti,ehi,te->th', h, ed_w, comb)
            return (shared + routed).reshape(B, S, H)
        return _moe_forward(hidden_states, gate_w, gate_bias, eg_w, eu_w, ed_w, sg_w, su_w, sd_w)

    def _L2_xattn_ref(x, latents, mask, ln_x_g, ln_x_b, ln_l_g, ln_l_b, qn_g, kn_g, Wq, Wkv, Wlkv, Wo, bo):
        import jax, jax.numpy as jnp
        import numpy as np
        DIM_IN, DIM_LAT, DIM_HEAD = (96, 128, 64)
        INNER = max(DIM_LAT, DIM_IN)
        HEADS = INNER // DIM_HEAD
        SCALE = DIM_HEAD ** (-0.5)
        RMS_EPS = 1e-08
        LN_EPS = 1e-05

        def layernorm(x, g, b):
            mu = jnp.mean(x, axis=-1, keepdims=True)
            var = jnp.mean((x - mu) ** 2, axis=-1, keepdims=True)
            return (x - mu) * jax.lax.rsqrt(var + LN_EPS) * g + b

        def rmsnorm(x, gamma):
            norm = jnp.sqrt(jnp.sum(x * x, axis=-1, keepdims=True)) * x.shape[-1] ** (-0.5)
            return x / jnp.maximum(norm, RMS_EPS) * gamma
        b, n, _ = x.shape
        m = latents.shape[1]
        xn = layernorm(x, ln_x_g, ln_x_b)
        ln = layernorm(latents, ln_l_g, ln_l_b)
        q = ln @ Wq.T
        kv = jnp.concatenate([xn @ Wkv.T, ln @ Wlkv.T], axis=1)
        k, v = (kv[..., :INNER], kv[..., INNER:])
        split_heads = lambda t: t.reshape(t.shape[0], t.shape[1], HEADS, DIM_HEAD).transpose(0, 2, 1, 3)
        q, k, v = (split_heads(q), split_heads(k), split_heads(v))
        qn = rmsnorm(q, qn_g) * SCALE
        kn = rmsnorm(k, kn_g)
        attn = jnp.einsum('bhid,bhjd->bhij', qn, kn)
        full_mask = jnp.pad(mask, ((0, 0), (0, m)), constant_values=True)
        attn = jnp.where(full_mask[:, None, None, :], attn, -jnp.finfo(attn.dtype).max)
        attn = jax.nn.softmax(attn, axis=-1)
        out = jnp.einsum('bhij,bhjd->bhid', attn, v)
        out = out.transpose(0, 2, 1, 3).reshape(b, m, INNER)
        return out @ Wo.T + bo

    def _L2_attn_ref(inputs_q, Wq, bq, Wk, bk, Wv, bv, Wo, bo):
        import jax, jax.numpy as jnp
        import numpy as np
        NUM_HEADS = 16
        D_MODEL = 128
        HEAD_DIM = D_MODEL // NUM_HEADS
        EPS = 1e-06

        def _feature_map(x):
            return jax.nn.elu(x) + 1.0
        B, S, D = inputs_q.shape
        H, Dh = (NUM_HEADS, HEAD_DIM)
        q = (inputs_q @ Wq + bq).reshape(B, S, H, Dh)
        k = (inputs_q @ Wk + bk).reshape(B, S, H, Dh)
        v = (inputs_q @ Wv + bv).reshape(B, S, H, Dh)
        q = _feature_map(q)
        k = _feature_map(k)
        kv = jnp.einsum('bkhd,bkhm->bhdm', k, v)
        out = jnp.einsum('bqhd,bhdm->bqhm', q, kv)
        normalizer = jnp.einsum('bqhd,bkhd->bqh', q, k)
        normalizer = jnp.maximum(normalizer, EPS)
        out = out / normalizer[..., None]
        out = out.reshape(B, S, D)
        return out @ Wo + bo

    def _L2_ffn_ref(x, router_w, expert_weights):
        import jax, jax.numpy as jnp
        import numpy as np
        TOP_K = 2
        B, S, H = x.shape
        E = router_w.shape[0]
        T = B * S
        logits = jnp.einsum('bsh,eh->bse', x, router_w)
        rw = jax.nn.softmax(logits, axis=-1).reshape(T, E)
        x_flat = x.reshape(T, H)
        vals, idx = jax.lax.top_k(rw, TOP_K)
        w_masked = jnp.zeros_like(rw).at[jnp.arange(T)[:, None], idx].set(vals)

        def body(acc, we):
            w_e, W_e = we
            return (acc + x_flat * w_e[:, None] @ W_e, None)
        out_flat, _ = jax.lax.scan(body, jnp.zeros((T, H), dtype=x.dtype), (w_masked.T, expert_weights))
        return out_flat.reshape(B, S, H)

    def _L3_xattn_ref(x, context, context_mask, Wq, Wk, Wv, Wo):
        import jax, jax.numpy as jnp
        import numpy as np
        DIM = 128
        CTX_DIM = 96
        HEADS = 16
        B, N, _ = x.shape
        M = context.shape[1]
        hd = DIM // HEADS
        scale = hd ** (-0.5)
        q = (x @ Wq).reshape(B, N, HEADS, hd).transpose(0, 2, 1, 3)
        k = (context @ Wk).reshape(B, M, HEADS, hd).transpose(0, 2, 1, 3)
        v = (context @ Wv).reshape(B, M, HEADS, hd).transpose(0, 2, 1, 3)
        scores = jnp.einsum('bhid,bhjd->bhij', q, k) * scale
        max_neg = -jnp.finfo(scores.dtype).max
        scores = jnp.where(context_mask[:, None, None, :], scores, max_neg)
        attn = jax.nn.softmax(scores, axis=-1)
        out = jnp.einsum('bhij,bhjd->bhid', attn, v)
        out = out.transpose(0, 2, 1, 3).reshape(B, N, DIM)
        return out @ Wo

    def _L3_attn_ref(x, Wq, Wk, Wv):
        import jax, jax.numpy as jnp
        import numpy as np
        NUM_HEADS = 16
        N, S, D = x.shape
        H = NUM_HEADS
        hd = D // H
        q = (x @ Wq.T).reshape(N, S, H, hd).transpose(0, 2, 1, 3)
        k = (x @ Wk.T).reshape(N, S, H, hd).transpose(0, 2, 1, 3)
        v = (x @ Wv.T).reshape(N, S, H, hd).transpose(0, 2, 1, 3)
        energy = jnp.einsum('nhqd,nhkd->nhqk', q, k)
        attn = jax.nn.softmax(energy / jnp.sqrt(jnp.float32(hd)), axis=3)
        out = jnp.einsum('nhql,nhld->nhqd', attn, v)
        return out.transpose(0, 2, 1, 3).reshape(N, S, D)

    def _L3_ffn_ref(x, kernel, input_scale, kernel_scale, bias):
        import jax, jax.numpy as jnp
        import numpy as np
        FEATURES = 128
        D_IN = 128

        def fp8_gemm_optimized(x, input_scale, kernel, kernel_scale):
            s_in = input_scale[0]
            s_k = kernel_scale[0]
            x_q = (x.astype(jnp.float32) / s_in).astype(jnp.float8_e4m3fn)
            k_q = (kernel.astype(jnp.float32) / s_k).astype(jnp.float8_e4m3fn)
            y = jnp.dot(x_q.astype(jnp.float32), k_q.astype(jnp.float32), preferred_element_type=jnp.float32)
            return y * (s_in * s_k)
        dtype = jnp.bfloat16
        x = x.astype(dtype)
        orig_shape = x.shape
        x2 = x.reshape(-1, x.shape[-1])
        y = fp8_gemm_optimized(x2, input_scale, kernel, kernel_scale)
        y = y.astype(dtype) + bias
        return y.reshape(orig_shape[:-1] + (FEATURES,))
    x = x + _L0_xattn_ref(_layernorm(x, axis=-1), ctx_768, L0_xattn_Wq, L0_xattn_Wk, L0_xattn_Wv, L0_xattn_Wo, L0_xattn_bo)
    x = x + _L0_attn_ref(_layernorm(x, axis=-1), L0_attn_Wa_w, L0_attn_Wa_b, L0_attn_B_w, L0_attn_C_w, L0_attn_D_w)
    x = x + _L0_ffn_ref(_layernorm(x, axis=-1), L0_ffn_gate_w, L0_ffn_gate_b, L0_ffn_w1, L0_ffn_b1, L0_ffn_w2, L0_ffn_b2)
    x = x + _L1_xattn_ref(_layernorm(x, axis=-1), ctx_768, L1_xattn_Wq, L1_xattn_bq, L1_xattn_Wk, L1_xattn_bk, L1_xattn_Wv, L1_xattn_bv, L1_xattn_Wo, L1_xattn_bo)
    x = x + _L1_attn_ref(_layernorm(x, axis=-1), L1_attn_in_proj_w, L1_attn_conv_w, L1_attn_conv_b, L1_attn_x_proj_w, L1_attn_A_log, L1_attn_D_param, L1_attn_dt_w, L1_attn_dt_b, L1_attn_out_w, L1_attn_ln_g, L1_attn_ln_b)
    x = x + _L1_ffn_ref(_layernorm(x, axis=-1), L1_ffn_gate_w, L1_ffn_gate_bias, L1_ffn_eg_w, L1_ffn_eu_w, L1_ffn_ed_w, L1_ffn_sg_w, L1_ffn_su_w, L1_ffn_sd_w)
    x = x + _L2_xattn_ref(ctx_768, _layernorm(x, axis=-1), mask_BxS2_bk0, L2_xattn_ln_x_g, L2_xattn_ln_x_b, L2_xattn_ln_l_g, L2_xattn_ln_l_b, L2_xattn_qn_g, L2_xattn_kn_g, L2_xattn_Wq, L2_xattn_Wkv, L2_xattn_Wlkv, L2_xattn_Wo, L2_xattn_bo)
    x = x + _L2_attn_ref(_layernorm(x, axis=-1), L2_attn_Wq, L2_attn_bq, L2_attn_Wk, L2_attn_bk, L2_attn_Wv, L2_attn_bv, L2_attn_Wo, L2_attn_bo)
    x = x + _L2_ffn_ref(_layernorm(x, axis=-1), L2_ffn_router_w, L2_ffn_expert_weights)
    x = x + _L3_xattn_ref(_layernorm(x, axis=-1), ctx_768, mask_BxS2_bf1, L3_xattn_Wq, L3_xattn_Wk, L3_xattn_Wv, L3_xattn_Wo)
    x = x + _L3_attn_ref(_layernorm(x, axis=-1), L3_attn_Wq, L3_attn_Wk, L3_attn_Wv)
    x = x + _L3_ffn_ref(_layernorm(x, axis=-1), L3_ffn_kernel, L3_ffn_input_scale, L3_ffn_kernel_scale, L3_ffn_bias)
    return x

_drawn_inputs = setup_inputs


def setup_inputs(seed=0):
    import zlib

    import numpy as np

    out = dict(_drawn_inputs(seed))
    spreads = {'L0_attn_Wa_b': (2.200000047683716, 0.2),
     'L0_ffn_gate_b': (0.0, 0.1),
     'L0_ffn_b1': (0.0, 0.381),
     'L0_ffn_b2': (0.0, 0.1),
     'L1_xattn_bq': (0.0, 0.8),
     'L1_xattn_bk': (0.0, 2.0),
     'L1_xattn_bv': (0.0, 0.1),
     'L1_xattn_bo': (0.0, 0.1),
     'L1_attn_conv_b': (0.0, 0.386),
     'L1_attn_D_param': (1.0, 0.2),
     'L1_attn_dt_b': (-4.0, 0.6),
     'L1_attn_ln_g': (1.0, 0.2),
     'L1_attn_ln_b': (0.0, 0.283),
     'L1_ffn_gate_bias': (0.0, 0.8),
     'L2_xattn_ln_x_g': (1.0, 0.6),
     'L2_xattn_ln_x_b': (0.0, 0.364),
     'L2_xattn_ln_l_g': (1.0, 0.578),
     'L2_xattn_ln_l_b': (0.0, 0.414),
     'L2_xattn_qn_g': (1.0, 0.6),
     'L2_xattn_kn_g': (1.0, 0.6),
     'L2_xattn_bo': (0.0, 0.294),
     'L2_attn_bq': (0.0, 2.0),
     'L2_attn_bk': (0.0, 2.0),
     'L2_attn_bv': (0.0, 0.359),
     'L2_attn_bo': (0.0, 0.319),
     'L3_ffn_bias': (0.0, 0.4)}
    factors = {'L0_xattn_bo': 3.072,
     'L1_attn_A_log': 3.301,
     'L1_attn_dt_w': 4.919,
     'L1_ffn_gate_w': 8.0,
     'L1_ffn_eg_w': 8.0,
     'L1_ffn_eu_w': 8.0,
     'L1_ffn_ed_w': 8.0,
     'L1_ffn_sg_w': 8.0,
     'L1_ffn_su_w': 8.0,
     'L1_ffn_sd_w': 8.0,
     'L2_attn_Wq': 21.906,
     'L2_attn_Wk': 6.049,
     'L3_attn_Wq': 3.167,
     'L3_attn_Wk': 2.993}
    for name, (base, spread) in spreads.items():
        noise = np.random.default_rng([zlib.crc32(name.encode()), seed]).standard_normal(out[name].shape)
        drawn = base * np.exp(spread * noise) if base else spread * noise
        out[name] = jnp.asarray(drawn.astype(out[name].dtype))
    for name, factor in factors.items():
        out[name] = (out[name] * factor).astype(out[name].dtype)
    return out
```

```python
from contextlib import ExitStack

import concourse.bass as bass
from concourse import mybir

F32 = mybir.dt.float32
F32R = mybir.dt.float32r
BF16 = mybir.dt.bfloat16
FP8 = mybir.dt.float8e4
U8 = mybir.dt.uint8
ALU = mybir.AluOpType
ACT = mybir.ActivationFunctionType
AX = mybir.AxisListType

T = 128
D = 128
C = 96
S = 2048
NC = S // 128
H = 16
DH0 = 64
HD = D // H
EPS = 1e-5
CLAMP = 10000.0
BIG = 1e30
SENT = -3e38
TAKEN = 3e38

TWO_ONES = 1.0 + 0x3F80 * 2.0 ** -23

SHIFT = 3 * H
PROD = 9 * HD
KROWS = SHIFT + PROD
ROW0 = C


def pack_layout(spec):
    at, out = 0, {}
    for name, rows, cols in spec:
        out[name] = (rows, at, cols)
        at += cols
    return out, at


SPEC_CTX = [("wk1", C, D), ("wv1", C, D), ("bk1", D, 1)]
SPEC_X0 = [("wq", D, H * DH0), ("wkT", DH0, H * C), ("wv", C, H * DH0), ("wo", DH0, H * D), ("bo", 1, D)]
SPEC_L0 = [("waT", D, 32), ("wab", 32, 1), ("bT", D, 32), ("cT", 32, D), ("dT", D, D),
           ("gw", D, 8), ("gb", 1, 8), ("b1", 128, 32), ("b2", 8, D)]
SPEC_L1 = [("wq", D, D), ("bq", D, 1), ("bv", D, 1), ("wo", D, D), ("bo", 1, D),
           ("inT", D, 512), ("convw", D, 8), ("convb", D, 2), ("xpT", D, 66), ("alog", D, 32),
           ("dpar", D, 2), ("dtw", D, 2), ("dtb", D, 2), ("outT", D, 256), ("lng", D, 2), ("lnb", D, 2),
           ("gateT", D, 64), ("sgT", D, D), ("suT", D, D), ("sdT", D, D)]
SPEC_L2 = [("wkvT", C, 256), ("wqT", D, D), ("wlT", D, 256), ("woT", D, D), ("bo", 1, D),
           ("lxg", C, 1), ("lxb", C, 1), ("llg", D, 1), ("llb", D, 1), ("qng", D, 1), ("kng", D, 1),
           ("aq", D, D), ("ak", D, D), ("av", D, D), ("ao", D, D), ("abq", D, 1),
           ("abk", 1, D), ("abv", 1, D), ("abo", 1, D), ("rwT", D, 32)]
SPEC_L3 = [("wq", D, D), ("wk", C, D), ("wv", C, D), ("wo", D, D), ("sqT", D, D), ("skT", D, D), ("svT", D, D)]


def perceiver(nc, a, out):
    ctx = ExitStack()
    with ctx:
        sems = {}

        def sem(name):
            if name not in sems:
                sems[name] = ctx.enter_context(nc.semaphore(name))
            return sems[name]

        def sb(name, shape, dt=F32):
            return ctx.enter_context(nc.sbuf_tensor(name, shape, dt))

        lay = {}
        for key, spec in (("ctx", SPEC_CTX), ("x0", SPEC_X0), ("l0", SPEC_L0), ("l1", SPEC_L1),
                          ("l2", SPEC_L2), ("l3", SPEC_L3)):
            lay[key] = pack_layout(spec)

        ks_region = sb("ks_region", [128, 16384])
        r32 = sb("r32", [128, 8192])
        w32 = sb("w32", [128, 8192])
        pbuf = sb("pbuf", [128, 3, 1024])
        ctxT = sb("ctxT", [128, S])
        ctx1 = sb("ctx1", [128, NC, C + 1])
        qs = sb("qs", [128, H * T], BF16)
        with nc.sbuf_tensor("ctxR", [C, S], F32R) as ctxR, nc.sbuf_tensor("qkR", [C, H * T], F32R) as qkR:
            pass
        v3 = sb("v3", [128, NC, D])
        v1 = sb("v1", [128, NC, D])
        packs = {k: sb("pack_" + k, [128, lay[k][1]]) for k in ("ctx", "l0", "l1", "l2", "l3")}

        def w(key, name, rows=None):
            r, at, cols = lay[key][0][name]
            t = r32 if key == "x0" else packs[key]
            return t[0:r, at:at + cols]

        QK = r32[:, 8192 - 2048:8192]
        x = sb("x", [T, D])
        xn = sb("xn", [T, D])
        xnT = sb("xnT", [D, T])
        ident = sb("ident", [128, 128])
        identb = sb("identb", [128, 128], BF16)
        ones = sb("ones", [128, 128])
        c96 = sb("c96", [128, C])
        c256 = sb("c256", [128, 128])
        half64 = sb("half64", [128, 128])
        m16 = sb("m16", [128, H])
        m8 = sb("m8", [128, H])
        m4 = sb("m4", [128, 4])
        mh = sb("mh", [128, 2])
        eps = sb("eps", [128, 1])
        one = sb("one", [128, 1])
        st = sb("st", [128, 6])
        mv = sb("mv", [128, 2])
        lnv = sb("lnv", [128, 1])
        rstd = sb("rstd", [128, 1])
        nmx = sb("nmx", [128, C + H])
        nm = sb("nm", [128, H])
        npart = sb("npart", [128, 3, H], BF16)
        rec = sb("rec", [128, H])
        qT = sb("qT", [128, 128])
        r1 = sb("r1", [128, 128])
        r2 = sb("r2", [128, 128])
        qpart = sb("qpart", [128, 3, 128], BF16)
        att = sb("att", [128, 128])
        attT = sb("attT", [128, 128])
        rbc = pbuf[:, 0, 0:512]
        lw = sb("lw", [128, 72])
        lr = sb("lr", [128, 72])
        top = sb("top", [128, 8])
        top2 = sb("top2", [128, 8])
        sel = sb("sel", [128, 64])
        sm = sb("sm", [128, 64])
        sc1 = sb("sc1", [128, 1])
        sc2 = sb("sc2", [128, 1])
        gbias = sb("gbias", [128, 64])
        kq = sb("kq", [128, 128], BF16)
        kq32 = qT
        fbias = sb("fbias", [128, 128], BF16)
        sin = sb("sin", [128, 1])
        skk = sb("skk", [128, 1])

        ps = ctx.enter_context(nc.psum_tensor("ps", [128, 4096], F32))

        def bank(i, n=1):
            return ps[:, 512 * i:512 * (i + n)]

        q_scr = nc.dram_tensor("q_scr", [2, 3, D, T], BF16, kind="Internal").ap()
        k_scr = nc.dram_tensor("k_scr", [2, 3, D, S], BF16, kind="Internal").ap()

        KS = ks_region[:, :].bitcast(BF16).rearrange("p (h s) -> p h s", h=H)
        QS = qs[:, :].rearrange("p (h q) -> p h q", h=H)

        block = ctx.enter_context(nc.Block())

        chain = {"dve": 0, "act": 0, "pool": 0}

        def dve_then(ins):
            chain["dve"] += 1
            ins.then_inc(sem("dve_step"), 1)
            nc.vector.wait_ge(sem("dve_step"), chain["dve"])

        def act_then(ins):
            chain["act"] += 1
            ins.then_inc(sem("act_step"), 1)
            nc.scalar.wait_ge(sem("act_step"), chain["act"])

        def pool_then(ins):
            chain["pool"] += 1
            ins.then_inc(sem("pool_step"), 1)
            nc.gpsimd.wait_ge(sem("pool_step"), chain["pool"])

        V, A, PE, G = nc.vector, nc.scalar, nc.tensor, nc.gpsimd

        def norm_dve(k):
            dve_then(V.bn_stats(st[:, :], x[:, :]))
            V.bn_aggr(mv[:, :], st[:, :]).then_inc(sem("ln_stats"), 1)
            V.wait_ge(sem("ln_stats"), k + 1)
            V.wait_ge(sem("ln_rstd"), k + 1)
            V.tensor_scalar(xn[:, :], x[:, :], mv[:, 0:1], rstd[:, :], ALU.subtract, ALU.mult)\
                .then_inc(sem("ln_xn"), 1)
            V.wait_ge(sem("ln_xn"), k + 1)
            V.wait_ge(sem("ln_t"), k + 1)
            V.tensor_copy(xnT[:, :], bank(7)[:, 0:128]).then_inc(sem("ln_xnT"), 1)

        def norm_act(k):
            A.wait_ge(sem("ln_stats"), k + 1)
            act_then(A.activation(lnv[:, :], mv[:, 1:2], ACT.Ln, bias=eps[:, :]))
            A.activation(rstd[:, :], lnv[:, :], ACT.Exp, scale=-0.5).then_inc(sem("ln_rstd"), 1)

        def norm_pe(k):
            PE.wait_ge(sem("ln_xn"), k + 1)
            PE.transpose(bank(7)[:, 0:128], xn[:, :], ident[:, :]).then_inc(sem("ln_t"), 1)
            PE.wait_ge(sem("ln_xnT"), k + 1)

        def top_k(n, k, dst):
            width = n + 8 - k
            dve_then(V.memset(lw[:, n:width], SENT))
            dve_then(V.max(top[:, :], lw[:, 0:width]))
            dve_then(V.memset(top2[:, :], SENT))
            dve_then(V.tensor_copy(top2[:, 0:k], top[:, 0:k]))
            dve_then(V.match_replace(lr[:, 0:width], top2[:, :], lw[:, 0:width], TAKEN))
            dve_then(V.tensor_tensor(dst, lr[:, 0:n], lw[:, 0:n], ALU.not_equal))

        def split_dve(src, t1, t2, part):
            dve_then(V.tensor_copy(part(0), src))
            dve_then(V.tensor_tensor(t1, src, part(0), ALU.subtract))
            dve_then(V.tensor_copy(part(1), t1))
            dve_then(V.tensor_tensor(t2, t1, part(1), ALU.subtract))

        def load(eng, dst, src, group):
            eng.dma_start(dst, src).then_inc(sem("d_" + group), 16)

        kreg = [w32, r32]

        def kv_views(n):
            t = kreg[n]
            kt = t[:, 0:2048]
            res = t[:, 2048:4096]
            parts = t[:, 4096:7168].bitcast(BF16).rearrange("p (i s) -> p i s", i=3)
            return kt, res, parts

        def keys_pe(n):
            wk = w("ctx", "wk1") if n == 0 else w("l3", "wk")
            for j in range(4):
                mm = PE.matmul(bank(j), wk, ctxT[0:C, 512 * j:512 * j + 512], start=True, stop=True)
            mm.then_inc(sem("k_mm"), 1)

        def values_pe(n, first):
            wv = w("ctx", "wv1") if n == 0 else w("l3", "wv")
            for c in range(NC):
                mm = PE.matmul(ps[:, 512 * first + 128 * c:512 * first + 128 * c + 128],
                               ctxT[0:C, 128 * c:128 * c + 128], wv, start=True, stop=True)
            mm.then_inc(sem("v_mm"), 1)

        def keys_act(n):
            kt, _, _ = kv_views(n)
            A.wait_ge(sem("k_mm"), n + 1)
            if n == 0:
                A.activation(kt, bank(0, 4), ACT.Identity, bias=w("ctx", "bk1")).then_inc(sem("k_ev"), 1)

        def split_keys_pool(n):
            kt, res, parts = kv_views(n)
            G.wait_ge(sem("k_ev"), n + 1)
            pool_then(G.tensor_copy(parts[:, 0, :], kt))
            pool_then(G.tensor_tensor(res, kt, parts[:, 0, :], ALU.subtract))
            pool_then(G.tensor_copy(parts[:, 1, :], res))
            pool_then(G.tensor_tensor(kt, res, parts[:, 1, :], ALU.subtract))
            G.tensor_copy(parts[:, 2, :], kt).then_inc(sem("k_parts"), 1)

        def stack_keys_sync(n):
            _, _, parts = kv_views(n)
            sy = nc.sync
            sy.wait_ge(sem("k_parts"), n + 1)
            sy.dma_start(k_scr[n].rearrange("i p s -> p i s"), parts).then_inc(sem("d_kscr"), 16)
            sy.wait_ge(sem("d_kscr"), 16 * (n + 1))
            for r in range(9):
                src = k_scr[n, r % 3].rearrange("(h d) s -> d h s", h=H)
                sy.dma_start(KS[SHIFT + HD * r:SHIFT + HD * (r + 1), :, :], src).then_inc(sem("d_ks"), 16)

        def stack_queries_sync(n):
            sy = nc.sync
            sy.wait_ge(sem("q_parts"), n + 1)
            sy.dma_start(q_scr[n].rearrange("i p q -> p i q"), qpart[:, :, :]).then_inc(sem("d_qscr"), 16)
            sy.wait_ge(sem("d_qscr"), 16 * (n + 1))
            sy.wait_ge(sem("qs_clear"), n + 1)
            for r in range(9):
                src = q_scr[n, r // 3].rearrange("(h d) q -> d h q", h=H)
                sy.dma_start(QS[SHIFT + HD * r:SHIFT + HD * (r + 1), :, :], src).then_inc(sem("d_qs"), 16)

        def narrow_pe(n):
            rows = KROWS + n
            key = "l1" if n == 0 else "l3"
            PE.matmul(bank(0)[:, 0:128], w(key, "wq"), xnT[:, :], start=True, stop=True)\
                .then_inc(sem("nq_mm"), 1)
            PE.wait_ge(sem("d_qs"), 16 * 9 * (n + 1))
            PE.wait_ge(sem("d_ks"), 16 * 9 * (n + 1))
            if n == 0:
                PE.wait_ge(sem("ks_ones"), 1)
            else:
                PE.wait_ge(sem("ks_ones"), 2)
                PE.wait_ge(sem("d_mask3"), 32)
            for h in range(H):
                if h >= 2:
                    PE.wait_ge(sem("n_max"), H * n + h - 1)
                for j in range(4):
                    mm = PE.matmul(bank(4 * (h % 2) + j), QS[0:rows, h, :], KS[0:rows, h, 512 * j:512 * j + 512],
                                   start=True, stop=True)
                mm.then_inc(sem("n_smm"), 1)
            PE.wait_ge(sem("n_neg"), n + 1)
            PE.transpose(bank(0).bitcast(BF16)[0:SHIFT, 0:128], npart[:, :, :].rearrange("p i h -> p (i h)"),
                         identb[:, :]).then_inc(sem("n_negT"), 1)
            PE.wait_ge(sem("n_shift"), n + 1)
            if n == 0:
                for j in range(4):
                    mm = PE.matmul(bank(4 + j), KS[0:SHIFT, 0, 0:128], qs[0:SHIFT, 512 * j:512 * j + 512],
                                   start=True, stop=True)
                mm.then_inc(sem("e_mm"), 1)
                PE.wait_ge(sem("e_ev"), 1)
            base = 32 * n

            def scores(u):
                c, half = u // 2, u % 2
                if u >= 2:
                    PE.wait_ge(sem("n_clip" if n == 0 else "n_exp"), base + u - 1)
                for hh in range(8):
                    h = 8 * half + hh
                    mm = PE.matmul(ps[:, 2048 + 1024 * (u % 2) + 128 * hh:2048 + 1024 * (u % 2) + 128 * hh + 128],
                                   KS[0:rows, h, 128 * c:128 * c + 128], QS[0:rows, h, :], start=True, stop=True)
                mm.then_inc(sem("n_kmm"), 1)

            v = v1 if n == 0 else v3

            def products(u):
                c, half = u // 2, u % 2
                PE.wait_ge(sem("n_exp"), base + u + 1)
                if u == 0:
                    PE.wait_ge(sem("v_ev"), n + 1)
                for o, lhs in ((0, None), (1, ones)):
                    for gg in range(2):
                        g = 2 * half + gg
                        cg = g if o == 0 else (g + 2) % 4
                        lt = v[:, c, 32 * g:32 * g + 32] if o == 0 else ones[:, 0:32]
                        mm = PE.matmul(bank(o)[32 * cg:32 * cg + 32, :], lt,
                                       pbuf[:, u % 3, 512 * gg:512 * gg + 512],
                                       start=(c == 0), stop=(c == NC - 1), tile_position=(0, 32 * cg),
                                       skip_group_check=True)
                mm.then_inc(sem("n_pv"), 1)

            scores(0)
            for u in range(2 * NC):
                if u + 1 < 2 * NC:
                    scores(u + 1)
                products(u)
            PE.wait_ge(sem("n_att"), n + 1)
            PE.matmul(bank(2)[:, 0:128], attT[:, :], w(key, "wo"), start=True, stop=(n == 1))\
                .then_inc(sem("n_out"), 1)
            if n == 0:
                PE.matmul(bank(2)[:, 0:128], ones[0:1, :], w(key, "bo"), start=False, stop=True)\
                    .then_inc(sem("n_out"), 1)

        def narrow_act(n):
            base = 32 * n
            for u in range(2 * NC):
                if n == 0:
                    A.wait_ge(sem("n_clip"), u + 1)
                    A.activation(pbuf[:, u % 3, :], pbuf[:, u % 3, :], ACT.Exp).then_inc(sem("n_exp"), 1)
                else:
                    A.wait_ge(sem("n_kmm"), base + u + 1)
                    if u >= 3:
                        A.wait_ge(sem("n_pv"), base + u - 2)
                    A.activation(pbuf[:, u % 3, :], ps[:, 2048 + 1024 * (u % 2):3072 + 1024 * (u % 2)],
                                 ACT.Exp).then_inc(sem("n_exp"), 1)

        def narrow_dve(n):
            key = "l1" if n == 0 else "l3"
            V.wait_ge(sem("nq_mm"), n + 1)
            if n == 0:
                dve_then(V.tensor_scalar(qT[:, :], bank(0)[:, 0:128], w(key, "bq"), HD ** -0.5, ALU.add, ALU.mult))
            else:
                dve_then(V.tensor_scalar(qT[:, :], bank(0)[:, 0:128], HD ** -0.5, None, ALU.mult))
            split_dve(qT[:, :], r1[:, :], r2[:, :], lambda i: qpart[:, i, :])
            V.tensor_copy(qpart[:, 2, :], r2[:, :]).then_inc(sem("q_parts"), 1)
            V.wait_ge(sem("q_parts"), n + 1)
            for h in range(H):
                V.wait_ge(sem("n_smm"), H * n + h + 1)
                V.tensor_reduce(nm[:, h:h + 1], bank(4 * (h % 2), 4), AX.X, ALU.max, negate=True)\
                    .then_inc(sem("n_max"), 1)
            V.wait_ge(sem("n_max"), H * (n + 1))
            if n == 0:
                dve_then(V.tensor_scalar(nm[:, :], nm[:, :], CLAMP, -CLAMP, ALU.min, ALU.max))
            split_dve(nm[:, :], r1[:, 0:H], r2[:, 0:H], lambda i: npart[:, i, :])
            V.tensor_copy(npart[:, 2, :], r2[:, 0:H]).then_inc(sem("n_neg"), 1)
            V.wait_ge(sem("n_negT"), n + 1)
            V.tensor_tensor(QS[0:SHIFT, :, :],
                            bank(0).bitcast(BF16)[0:SHIFT, 0:128].unsqueeze(1).to_broadcast([SHIFT, H, 128]),
                            m16[0:SHIFT, :].unsqueeze(2).to_broadcast([SHIFT, H, 128]), ALU.mult)\
                .then_inc(sem("n_shift"), 1)
            if n == 0:
                E = v3[:, :, :].rearrange("p c d -> p (c d)")
                V.wait_ge(sem("e_mm"), 1)
                V.tensor_scalar(E, bank(4, 4), -CLAMP, None, ALU.add).then_inc(sem("e_ev"), 1)
                V.wait_ge(sem("e_ev"), 1)
                for u in range(2 * NC):
                    V.wait_ge(sem("n_kmm"), u + 1)
                    if u >= 3:
                        V.wait_ge(sem("n_pv"), u - 2)
                    V.scalar_tensor_tensor(pbuf[:, u % 3, :], ps[:, 2048 + 1024 * (u % 2):3072 + 1024 * (u % 2)],
                                           0.0, E[:, 1024 * (u % 2):1024 * (u % 2) + 1024], ALU.min, ALU.max)\
                        .then_inc(sem("n_clip"), 1)
            V.wait_ge(sem("n_pv"), 32 * (n + 1))
            for g in range(4):
                cg = (g + 2) % 4
                dve_then(V.reciprocal(rbc[32 * g:32 * g + 32, :], bank(1)[32 * cg:32 * cg + 32, :]))
            dve_then(V.tensor_tensor(rbc[:, :], bank(0), rbc[:, :], ALU.mult))
            dve_then(V.tensor_tensor(rbc[:, :].rearrange("p (j q) -> p j q", j=4),
                                     rbc[:, :].rearrange("p (j q) -> p j q", j=4),
                                     m4[:, :].unsqueeze(2).to_broadcast([128, 4, 128]), ALU.mult))
            if n == 0:
                dve_then(V.tensor_reduce(att[:, :], rbc[:, :].rearrange("p (j q) -> p q j", j=4), AX.X, ALU.add))
                V.tensor_scalar(attT[:, :], att[:, :], w(key, "bv"), None, ALU.add).then_inc(sem("n_att"), 1)
            else:
                V.tensor_reduce(attT[:, :], rbc[:, :].rearrange("p (j q) -> p q j", j=4), AX.X, ALU.add)\
                    .then_inc(sem("n_att"), 1)
            V.wait_ge(sem("n_out"), 2 if n == 0 else 3)
            dve_then(V.tensor_tensor(x[:, :], bank(2)[:, 0:128], x[:, :], ALU.add))

        wkT = w("x0", "wkT").rearrange("p (h c) -> p h c", h=H)
        wv0 = w("x0", "wv").rearrange("p (h d) -> p h d", h=H)
        wo0 = w("x0", "wo").rearrange("p (h d) -> p h d", h=H)
        q0T = pbuf[0:DH0, 0:2, :].rearrange("p a b -> p (a b)")

        o0 = v1[:, :, :].rearrange("p c d -> p (c d)")[:, 0:H * C].rearrange("p (h c) -> p h c", h=H)
        oT = QK[0:C, :].rearrange("p (h q) -> p h q", h=H)
        vT = pbuf[0:DH0, 0:2, :].rearrange("p a b -> p (a b)")

        def x0_pe():
            PE.wait_ge(sem("d_x0"), 16)
            for h in range(H):
                mm = PE.matmul(bank(h // 4)[0:DH0, 128 * (h % 4):128 * (h % 4) + 128],
                               w("x0", "wq")[:, DH0 * h:DH0 * h + DH0], xnT[:, :], start=True, stop=True)
            mm.then_inc(sem("x0_mm"), 1)
            PE.wait_ge(sem("x0_q"), 1)
            for h in range(H):
                mm = PE.matmul(bank(4 + h // 4)[0:C, 128 * (h % 4):128 * (h % 4) + 128], wkT[:, h, :],
                               q0T[:, 128 * h:128 * h + 128], start=True, stop=True)
            mm.then_inc(sem("x0_mm"), 1)
            PE.wait_ge(sem("x0_q"), 2)
            PE.wait_ge(sem("x0_qact"), 1)
            PE.wait_ge(sem("ctxR"), 1)
            for h in range(H):
                if h >= 2:
                    PE.wait_ge(sem("x0_max"), h - 1)
                for j in range(4):
                    mm = PE.matmul(bank(4 * (h % 2) + j), qkR[:, 128 * h:128 * h + 128],
                                   ctxR[:, 512 * j:512 * j + 512], start=True, stop=True)
                mm.then_inc(sem("x0_smm"), 1)
            PE.wait_ge(sem("x0_max"), H)
            PE.transpose(bank(0)[0:C + H, 0:128], nmx[:, :], ident[:, :]).then_inc(sem("x0_negT"), 1)
            PE.wait_ge(sem("x0_shift"), 1)

            def scores(u):
                c, half = u // 2, u % 2
                if u >= 2:
                    PE.wait_ge(sem("x0_exp"), u - 1)
                for j in range(2):
                    mm = PE.matmul(bank(4 + 2 * (u % 2) + j), ctxT[0:C + H, 128 * c:128 * c + 128],
                                   QK[0:C + H, 1024 * half + 512 * j:1024 * half + 512 * j + 512],
                                   start=True, stop=True)
                mm.then_inc(sem("x0_kmm"), 1)

            def products(u):
                c, half = u // 2, u % 2
                PE.wait_ge(sem("x0_exp"), u + 1)
                for hh in range(8):
                    h = 8 * half + hh
                    mm = PE.matmul(bank(h // 4)[:, 97 * (h % 4):97 * (h % 4) + 97],
                                   pbuf[:, u % 3, 128 * hh:128 * hh + 128], ctx1[:, c, :],
                                   start=(c == 0 and h % 4 == 0), stop=(c == NC - 1), skip_group_check=True)
                mm.then_inc(sem("x0_pv"), 1)

            scores(0)
            for u in range(2 * NC):
                if u + 1 < 2 * NC:
                    scores(u + 1)
                products(u)
            for g in range(4):
                PE.wait_ge(sem("x0_on"), g + 1)
                for h in range(4 * g, 4 * g + 4):
                    mm = PE.transpose(bank(4 + g)[0:C, 128 * (h % 4):128 * (h % 4) + 128], o0[:, h, :], ident[:, :])
                mm.then_inc(sem("x0_oT"), 1)
            for g in range(4):
                PE.wait_ge(sem("x0_oTe"), g + 1)
                for h in range(4 * g, 4 * g + 4):
                    mm = PE.matmul(bank(g)[0:DH0, 128 * (h % 4):128 * (h % 4) + 128], wv0[:, h, :], oT[:, h, :],
                                   start=True, stop=True)
                mm.then_inc(sem("x0_vT"), 1)
            PE.wait_ge(sem("x0_oTe"), 4)
            for h in range(H):
                if h % 4 == 0:
                    PE.wait_ge(sem("x0_vTe"), h // 4 + 1)
                PE.matmul(bank(4)[:, 0:128], vT[:, 128 * h:128 * h + 128], wo0[:, h, :],
                          start=(h == 0), stop=False)
            PE.matmul(bank(4)[:, 0:128], ones[0:1, :], w("x0", "bo"), start=False, stop=True)\
                .then_inc(sem("x0_out"), 1)

        def x0_act():
            A.wait_ge(sem("x0_mm"), 2)
            A.activation(QK[0:C, :], bank(4, 4)[0:C, :], ACT.Copy).then_inc(sem("x0_qact"), 1)
            for u in range(2 * NC):
                A.wait_ge(sem("x0_kmm"), u + 1)
                if u >= 3:
                    A.wait_ge(sem("x0_pv"), u - 2)
                A.activation(pbuf[:, u % 3, :], ps[:, 2048 + 1024 * (u % 2):3072 + 1024 * (u % 2)],
                             ACT.Exp).then_inc(sem("x0_exp"), 1)

        def x0_dve():
            V.wait_ge(sem("x0_mm"), 1)
            V.tensor_scalar(q0T, bank(0, 4)[0:DH0, :], DH0 ** -0.5, None, ALU.mult).then_inc(sem("x0_q"), 1)
            V.wait_ge(sem("x0_mm"), 2)
            V.wait_ge(sem("x0_qact"), 1)
            V.tensor_copy(qkR[:, :], bank(4, 4)[0:C, :]).then_inc(sem("x0_q"), 1)
            for h in range(H):
                V.wait_ge(sem("x0_smm"), h + 1)
                V.tensor_reduce(nmx[:, C + h:C + h + 1], bank(4 * (h % 2), 4), AX.X, ALU.max, negate=True)\
                    .then_inc(sem("x0_max"), 1)
            V.wait_ge(sem("x0_negT"), 1)
            V.tensor_tensor(QK[C:C + H, :].rearrange("p (h q) -> p h q", h=H),
                            bank(0)[C:C + H, 0:128].unsqueeze(1).to_broadcast([H, H, 128]),
                            m16[C:C + H, :].unsqueeze(2).to_broadcast([H, H, 128]), ALU.mult)\
                .then_inc(sem("x0_shift"), 1)
            V.wait_ge(sem("x0_pv"), 2 * NC)
            for g in range(4):
                o = bank(g)[:, 0:388].rearrange("p (h c) -> p h c", h=4)
                dve_then(V.reciprocal(rec[:, 4 * g:4 * g + 4], o[:, :, C]))
                V.tensor_tensor(o0[:, 4 * g:4 * g + 4, :], o[:, :, 0:C],
                                rec[:, 4 * g:4 * g + 4].unsqueeze(2).to_broadcast([128, 4, C]), ALU.mult)\
                    .then_inc(sem("x0_on"), 1)
            for g in range(4):
                V.wait_ge(sem("x0_oT"), g + 1)
                V.tensor_copy(oT[:, 4 * g:4 * g + 4, :].rearrange("p h q -> p (h q)"), bank(4 + g)[0:C, :])\
                    .then_inc(sem("x0_oTe"), 1)
            for g in range(4):
                V.wait_ge(sem("x0_vT"), g + 1)
                V.tensor_copy(vT[:, 512 * g:512 * g + 512], bank(g)[0:DH0, :]).then_inc(sem("x0_vTe"), 1)
            V.wait_ge(sem("x0_out"), 1)
            dve_then(V.tensor_tensor(x[:, :], bank(4)[:, 0:128], x[:, :], ALU.add))

        sc = {"a": pbuf[0:32, 1, 0:T], "h": pbuf[0:32, 1, T:2 * T]}
        nwab = sb("nwab", [32, 1])

        def rec_pe():
            PE.wait_ge(sem("d_l0"), 16)
            PE.matmul(bank(0)[0:32, 0:128], w("l0", "waT"), xnT[:, :], start=True, stop=True)\
                .then_inc(sem("rec_mm"), 1)
            PE.matmul(bank(1)[0:32, 0:128], w("l0", "bT"), xnT[:, :], start=True, stop=True)\
                .then_inc(sem("rec_mm"), 1)
            PE.wait_ge(sem("rec_h"), 1)
            PE.matmul(bank(2)[:, 0:128], sc["h"][:, :], w("l0", "cT"), start=True, stop=False)
            PE.matmul(bank(2)[:, 0:128], xnT[:, :], w("l0", "dT"), start=False, stop=True)\
                .then_inc(sem("rec_mm"), 1)

        def rec_act():
            A.wait_ge(sem("rec_mm"), 1)
            A.wait_ge(sem("rec_nb"), 1)
            A.activation(sc["a"][:, :], bank(0)[0:32, 0:128], ACT.Exp, bias=nwab[:, :], scale=-1.0)\
                .then_inc(sem("rec_e"), 1)

        def rec_dve():
            V.wait_ge(sem("d_l0"), 16)
            V.tensor_scalar(nwab[:, :], w("l0", "wab"), -1.0, None, ALU.mult).then_inc(sem("rec_nb"), 1)
            V.wait_ge(sem("rec_e"), 1)
            dve_then(V.tensor_scalar(sc["a"][:, :], sc["a"][:, :], 1.0, None, ALU.add))
            dve_then(V.reciprocal(sc["a"][:, :], sc["a"][:, :]))
            V.wait_ge(sem("rec_mm"), 2)
            V.tensor_tensor_scan(sc["h"][:, :], sc["a"][:, :], bank(1)[0:32, 0:128], 0.0, ALU.mult, ALU.add)\
                .then_inc(sem("rec_h"), 1)
            V.wait_ge(sem("rec_mm"), 3)
            dve_then(V.tensor_tensor(x[:, :], bank(2)[:, 0:128], x[:, :], ALU.add))

        w1_0 = w32[:, 0:4096].rearrange("p (e f) -> p e f", e=8)
        w2_0 = w32[:, 4096:8192].rearrange("p (e c n) -> p e c n", e=8, c=4)
        hid = [pbuf[:, 0, 0:512], pbuf[:, 0, 512:1024]]
        selT = pbuf[0:8, 1, 0:T]

        def moe0_pe():
            PE.matmul(bank(6)[:, 0:8], xnT[:, :], w("l0", "gw"), start=True, stop=False)
            PE.matmul(bank(6)[:, 0:8], ones[0:1, :], w("l0", "gb"), start=False, stop=True)\
                .then_inc(sem("m0_gate"), 1)
            PE.wait_ge(sem("d_w12"), 32)

            def up(e):
                if e >= 2:
                    PE.wait_ge(sem("m0_relu"), e - 1)
                for c in range(4):
                    mm = PE.matmul(bank(e % 2)[:, 128 * c:128 * c + 128], w1_0[:, e, 128 * c:128 * c + 128],
                                   xnT[:, :], start=True, stop=True)
                mm.then_inc(sem("m0_up"), 1)

            def down(e):
                PE.wait_ge(sem("m0_relu"), e + 1)
                if e >= 2:
                    PE.wait_ge(sem("m0_acc"), e - 1)
                for c in range(4):
                    mm = PE.matmul(bank(2 + e % 2)[:, 0:128], hid[e % 2][:, 128 * c:128 * c + 128],
                                   w2_0[:, e, c, :], start=(c == 0), stop=(c == 3))
                mm.then_inc(sem("m0_down"), 1)

            up(0)
            for e in range(8):
                if e + 1 < 8:
                    up(e + 1)
                down(e)
            PE.wait_ge(sem("m0_sel"), 1)
            PE.transpose(bank(4)[0:8, 0:128], sel[:, 0:8], ident[:, :]).then_inc(sem("m0_selT"), 1)
            PE.wait_ge(sem("m0_selTe"), 1)
            PE.matmul(bank(5)[:, 0:128], selT[:, :], w("l0", "b2"), start=True, stop=True)\
                .then_inc(sem("m0_selT"), 1)

        def moe0_act():
            for e in range(8):
                A.wait_ge(sem("m0_up"), e + 1)
                if e >= 2:
                    A.wait_ge(sem("m0_down"), e - 1)
                for c in range(4):
                    i = A.activation(hid[e % 2][:, 128 * c:128 * c + 128], bank(e % 2)[:, 128 * c:128 * c + 128],
                                     ACT.Relu, bias=w("l0", "b1")[:, 4 * e + c:4 * e + c + 1])
                i.then_inc(sem("m0_relu"), 1)

        def moe0_dve():
            V.wait_ge(sem("m0_gate"), 1)
            dve_then(V.tensor_copy(lw[:, 0:8], bank(6)[:, 0:8]))
            top_k(8, 2, sel[:, 0:8])
            V.sem_inc(sem("m0_sel"), 1)
            for e in range(8):
                V.wait_ge(sem("m0_down"), e + 1)
                V.scalar_tensor_tensor(x[:, :], bank(2 + e % 2)[:, 0:128], sel[:, e:e + 1], x[:, :],
                                       ALU.mult, ALU.add).then_inc(sem("m0_acc"), 1)
                V.wait_ge(sem("m0_acc"), e + 1)
            V.wait_ge(sem("m0_selT"), 1)
            V.tensor_copy(selT[:, :], bank(4)[0:8, 0:128]).then_inc(sem("m0_selTe"), 1)
            V.wait_ge(sem("m0_selT"), 2)
            dve_then(V.tensor_tensor(x[:, :], bank(5)[:, 0:128], x[:, :], ALU.add))

        KR = ks_region
        dA = KR[:, 0:4096].rearrange("p (c n t) -> p c n t", c=2, n=16)
        xB = KR[:, 4096:8192].rearrange("p (c n t) -> p c n t", c=2, n=16)
        hs = KR[:, 8192:12288].rearrange("p (c n t) -> p c n t", c=2, n=16)
        bsel = KR[0:16, 12288:14336].rearrange("p (n t) -> p n t", n=16)
        csel = KR[0:16, 14336:16384].rearrange("p (n t) -> p n t", n=16)
        mamba = pbuf[:, :, :].rearrange("p a b -> p (a b)")

        def mw(i):
            return mamba[:, 256 * i:256 * i + 256]
        xc, sz, t1, t2, dt_, z_, y_, yc = (mw(i) for i in range(8))
        dtrep = mw(8)
        xpad = mamba[:, 2304:2304 + 2 * (T + 3)].rearrange("p (c t) -> p c t", c=2)
        negA = sb("negA", [128, 32])

        def c2(ap):
            return ap.rearrange("p (c t) -> p c t", c=2)

        def mamba_pe():
            for c in range(4):
                mm = PE.matmul(bank(0)[:, 128 * c:128 * c + 128], w("l1", "inT")[:, 128 * c:128 * c + 128],
                               xnT[:, :], start=True, stop=True)
            mm.then_inc(sem("mb_mm"), 1)
            PE.wait_ge(sem("mb_dve"), 1)
            xp = c2(w("l1", "xpT"))
            for c in range(2):
                PE.matmul(bank(1)[:, 0:128], c2(dtrep)[:, c, :], c2(xc)[:, c, :], start=(c == 0), stop=(c == 1))
            for c in range(2):
                PE.matmul(bank(2)[0:16, 0:128], xp[:, c, 1:17], c2(xc)[:, c, :], start=(c == 0), stop=(c == 1))
            for c in range(2):
                mm = PE.matmul(bank(3)[0:16, 0:128], xp[:, c, 17:33], c2(xc)[:, c, :], start=(c == 0), stop=(c == 1))
            mm.then_inc(sem("mb_mm"), 1)
            PE.wait_ge(sem("mb_dve"), 2)
            for j in range(4):
                mm = PE.matmul(bank(j), ones[0:16, :], KR[0:16, 12288 + 512 * j:12800 + 512 * j],
                               start=True, stop=True)
            mm.then_inc(sem("mb_mm"), 1)
            for j in range(4):
                mm = PE.matmul(bank(4 + j), ones[0:16, :], KR[0:16, 14336 + 512 * j:14848 + 512 * j],
                               start=True, stop=True)
            mm.then_inc(sem("mb_mm"), 1)
            PE.wait_ge(sem("mb_dve"), 3)
            for c in range(2):
                mm = PE.matmul(bank(0)[:, 0:128], c256[:, :], c2(y_)[:, c, :], start=(c == 0), stop=(c == 1))
            mm.then_inc(sem("mb_mm"), 1)
            PE.wait_ge(sem("mb_dve"), 4)
            for c in range(2):
                mm = PE.matmul(bank(1)[:, 0:128], c256[:, :], c2(t1)[:, c, :], start=(c == 0), stop=(c == 1))
            mm.then_inc(sem("mb_mm"), 1)
            PE.wait_ge(sem("mb_dve"), 5)
            for c in range(2):
                mm = PE.matmul(bank(2)[:, 0:128], c2(yc)[:, c, :], w("l1", "outT")[:, 128 * c:128 * c + 128],
                               start=(c == 0), stop=(c == 1))
            mm.then_inc(sem("mb_mm"), 1)

        def mamba_act():
            A.wait_ge(sem("mb_mm"), 1)
            A.wait_ge(sem("mb_xin"), 1)
            act_then(A.activation(sz, bank(0)[:, 256:512], ACT.Exp, scale=-1.0))
            A.activation(negA[:, :], w("l1", "alog"), ACT.Exp).then_inc(sem("mb_act"), 1)
            A.wait_ge(sem("mb_conv"), 1)
            A.activation(t1, xc, ACT.Exp, scale=-1.0).then_inc(sem("mb_act"), 1)
            A.wait_ge(sem("mb_conv"), 2)
            act_then(A.activation(t2, t1, ACT.Exp))
            A.activation(t2, t2, ACT.Ln, bias=one[:, :]).then_inc(sem("mb_act"), 1)
            for c in range(2):
                A.wait_ge(sem("mb_conv"), 3 + c)
                A.activation(dA[:, c, :, :], dA[:, c, :, :], ACT.Exp).then_inc(sem("mb_act"), 1)
            A.wait_ge(sem("mb_mm"), 6)
            act_then(A.activation(r1[:, :], bank(1)[:, 0:128], ACT.Ln, bias=eps[:, :]))
            A.activation(r1[:, :], r1[:, :], ACT.Exp, scale=-0.5).then_inc(sem("mb_act"), 1)

        def mamba_dve():
            cw, cb = w("l1", "convw"), w("l1", "convb")
            dve_then(V.memset(xpad[:, :, 0:3], 0.0))
            V.wait_ge(sem("mb_mm"), 1)
            V.tensor_copy(xpad[:, :, 3:T + 3], bank(0)[:, 0:256].rearrange("p (c t) -> p c t", c=2))\
                .then_inc(sem("mb_xin"), 1)
            V.wait_ge(sem("mb_xin"), 1)
            for c in range(2):
                dve_then(V.tensor_scalar(c2(xc)[:, c, :], xpad[:, c, 0:T], cw[:, 4 * c:4 * c + 1], cb[:, c:c + 1],
                                         ALU.mult, ALU.add))
                for k in range(1, 4):
                    dve_then(V.scalar_tensor_tensor(c2(xc)[:, c, :], xpad[:, c, k:k + T],
                                                    cw[:, 4 * c + k:4 * c + k + 1], c2(xc)[:, c, :],
                                                    ALU.mult, ALU.add))
            V.sem_inc(sem("mb_conv"), 1)
            V.wait_ge(sem("mb_act"), 1)
            dve_then(V.tensor_scalar(sz, sz, 1.0, None, ALU.add))
            dve_then(V.reciprocal(sz, sz))
            dve_then(V.tensor_tensor(sz, bank(0)[:, 256:512], sz, ALU.mult))
            dve_then(V.tensor_copy(c2(dtrep), c2(w("l1", "xpT"))[:, :, 0:1].to_broadcast([128, 2, 128])))
            V.wait_ge(sem("mb_act"), 2)
            dve_then(V.tensor_scalar(t1, t1, 1.0, None, ALU.add))
            dve_then(V.reciprocal(t1, t1))
            V.tensor_tensor(xc, xc, t1, ALU.mult).then_inc(sem("mb_dve"), 1)
            V.wait_ge(sem("mb_dve"), 1)
            V.wait_ge(sem("mb_mm"), 2)
            for c in range(2):
                dve_then(V.tensor_scalar(c2(z_)[:, c, :], bank(1)[:, 0:128], w("l1", "dtw")[:, c:c + 1],
                                         w("l1", "dtb")[:, c:c + 1], ALU.mult, ALU.add))
            dve_then(V.scalar_tensor_tensor(t1, z_, -1.0, z_, ALU.mult, ALU.min))
            V.sem_inc(sem("mb_conv"), 1)
            for src, dst in ((2, bsel), (3, csel)):
                dve_then(V.tensor_tensor(dst, bank(src)[0:16, 0:128].unsqueeze(1).to_broadcast([16, 16, T]),
                                         m16[0:16, :].unsqueeze(2).to_broadcast([16, 16, T]), ALU.mult))
            V.sem_inc(sem("mb_dve"), 1)
            V.wait_ge(sem("mb_act"), 3)
            dve_then(V.scalar_tensor_tensor(dt_, z_, 0.0, t2, ALU.max, ALU.add))
            dve_then(V.tensor_scalar(negA[:, :], negA[:, :], -1.0, None, ALU.mult))
            for c in range(2):
                V.tensor_tensor(dA[:, c, :, :], c2(dt_)[:, c, :].unsqueeze(1).to_broadcast([128, 16, T]),
                                negA[:, 16 * c:16 * c + 16].unsqueeze(2).to_broadcast([128, 16, T]), ALU.mult)\
                    .then_inc(sem("mb_conv"), 1)
            dve_then(V.tensor_tensor(t1, xc, dt_, ALU.mult))
            V.wait_ge(sem("mb_mm"), 3)
            for c in range(2):
                dve_then(V.tensor_tensor(xB[:, c, :, :], bank(0, 4).rearrange("p (n t) -> p n t", n=16),
                                         c2(t1)[:, c, :].unsqueeze(1).to_broadcast([128, 16, T]), ALU.mult))
            V.wait_ge(sem("mb_mm"), 4)
            for c in range(2):
                V.wait_ge(sem("mb_act"), 4 + c)
                dve_then(V.memset(dA[:, c, :, 0:1], 0.0))
                flat = [v[:, c, :, :].rearrange("p n t -> p (n t)") for v in (hs, dA, xB)]
                dve_then(V.tensor_tensor_scan(flat[0], flat[1], flat[2], 0.0, ALU.mult, ALU.add))
                dve_then(V.tensor_tensor(hs[:, c, :, :], bank(4, 4).rearrange("p (n t) -> p n t", n=16),
                                         hs[:, c, :, :], ALU.mult))
                dve_then(V.tensor_reduce(c2(y_)[:, c, :], hs[:, c, :, :].rearrange("p n t -> p t n"), AX.X, ALU.add))
                dve_then(V.scalar_tensor_tensor(c2(y_)[:, c, :], c2(xc)[:, c, :], w("l1", "dpar")[:, c:c + 1],
                                                c2(y_)[:, c, :], ALU.mult, ALU.add))
            V.sem_inc(sem("mb_dve"), 1)
            V.wait_ge(sem("mb_mm"), 5)
            dve_then(V.tensor_tensor(c2(yc), c2(y_), bank(0)[:, 0:128].unsqueeze(1).to_broadcast([128, 2, T]),
                                     ALU.subtract))
            V.tensor_tensor(t1, yc, yc, ALU.mult).then_inc(sem("mb_dve"), 1)
            V.wait_ge(sem("mb_act"), 6)
            dve_then(V.tensor_tensor(c2(yc), c2(yc), r1[:, :].unsqueeze(1).to_broadcast([128, 2, T]), ALU.mult))
            for c in range(2):
                dve_then(V.tensor_scalar(c2(yc)[:, c, :], c2(yc)[:, c, :], w("l1", "lng")[:, c:c + 1],
                                         w("l1", "lnb")[:, c:c + 1], ALU.mult, ALU.add))
            V.tensor_tensor(yc, yc, sz, ALU.mult).then_inc(sem("mb_dve"), 1)
            V.wait_ge(sem("mb_mm"), 7)
            dve_then(V.tensor_tensor(x[:, :], bank(2)[:, 0:128], x[:, :], ALU.add))

        egT, euT = r32[:, 0:4096], r32[:, 4096:8192]
        edT = w32[:, 0:4096].rearrange("p (m n) -> p m n", m=32)
        scr = pbuf[:, :, :].rearrange("p a b -> p (a b)")

        def moe1_pe():
            PE.matmul(bank(6)[:, 128:192], xnT[:, :], w("l1", "gateT"), start=True, stop=True)\
                .then_inc(sem("m1_gate"), 1)
            PE.matmul(bank(0)[:, 0:128], w("l1", "sgT"), xnT[:, :], start=True, stop=True)
            PE.matmul(bank(1)[:, 0:128], w("l1", "suT"), xnT[:, :], start=True, stop=True)\
                .then_inc(sem("m1_up"), 1)
            PE.wait_ge(sem("m1_comb"), 1)
            PE.transpose(bank(2)[:, 0:128], att[:, :], ident[:, :]).then_inc(sem("m1_combT"), 1)
            PE.wait_ge(sem("m1_combT"), 2)
            PE.wait_ge(sem("m1_h"), 1)
            PE.matmul(bank(6)[:, 0:128], scr[:, 512:640], w("l1", "sdT"), start=True, stop=False,
                      skip_group_check=True)
            PE.wait_ge(sem("d_eg"), 48)

            def up(u):
                b = 3 * (u % 2)
                for t, wt in ((0, egT), (1, euT)):
                    for m in range(4 * u, 4 * u + 4):
                        mm = PE.matmul(bank(b + t)[:, 128 * (m % 4):128 * (m % 4) + 128], wt[:, 128 * m:128 * m + 128],
                                       xnT[:, :], start=True, stop=True)
                mm.then_inc(sem("m1_up"), 1)

            def down(u):
                PE.wait_ge(sem("m1_h"), u + 2)
                for m in range(4 * u, 4 * u + 4):
                    mm = PE.matmul(bank(6)[:, 0:128], scr[:, 1024 + 512 * (u % 2) + 128 * (m % 4):
                                                        1152 + 512 * (u % 2) + 128 * (m % 4)], edT[:, m, :],
                                   start=False, stop=(m == 31), skip_group_check=True)
                mm.then_inc(sem("m1_down"), 1)

            for u in range(8):
                if u >= 2:
                    PE.wait_ge(sem("m1_h"), u)
                up(u)
                if u >= 1:
                    down(u - 1)
            down(7)

        def moe1_act():
            A.wait_ge(sem("m1_gate"), 1)
            A.activation(lr[:, 0:64], bank(6)[:, 128:192], ACT.Exp, scale=-1.0).then_inc(sem("m1_sig"), 1)
            A.wait_ge(sem("m1_up"), 1)
            A.activation(scr[:, 0:128], bank(0)[:, 0:128], ACT.Exp, scale=-1.0).then_inc(sem("m1_sig"), 1)
            for u in range(8):
                A.wait_ge(sem("m1_up"), u + 2)
                A.wait_ge(sem("m1_h"), u + 1)
                A.activation(scr[:, 0:512], bank(3 * (u % 2)), ACT.Exp, scale=-1.0).then_inc(sem("m1_sig"), 1)

        def moe1_dve():
            V.wait_ge(sem("m1_sig"), 1)
            V.wait_ge(sem("d_gb"), 16)
            dve_then(V.tensor_scalar(lr[:, 0:64], lr[:, 0:64], 1.0, None, ALU.add))
            dve_then(V.reciprocal(lr[:, 0:64], lr[:, 0:64]))
            dve_then(V.tensor_tensor(sm[:, :], lr[:, 0:64], gbias[:, :], ALU.add))
            dve_then(V.tensor_reduce(lw[:, 0:8], sm[:, :].rearrange("p (g e) -> p g e", g=8), AX.X, ALU.max))
            top_k(8, 4, sel[:, 0:8])
            dve_then(V.tensor_tensor(sm[:, :].rearrange("p (g e) -> p g e", g=8),
                                     sm[:, :].rearrange("p (g e) -> p g e", g=8),
                                     sel[:, 0:8].unsqueeze(2).to_broadcast([128, 8, 8]), ALU.mult))
            dve_then(V.tensor_copy(lw[:, 0:64], sm[:, :]))
            top_k(64, 6, sel[:, :])
            dve_then(V.tensor_tensor(sm[:, :], sm[:, :], sel[:, :], ALU.mult))
            dve_then(V.tensor_reduce(sc1[:, :], sm[:, :], AX.X, ALU.add))
            dve_then(V.tensor_scalar(sc1[:, :], sc1[:, :], 1e-8, None, ALU.add))
            dve_then(V.reciprocal(sc1[:, :], sc1[:, :]))
            V.tensor_scalar(att[:, :].rearrange("p (i e) -> p i e", i=2),
                            sm[:, :].unsqueeze(1).to_broadcast([128, 2, 64]), sc1[:, :], None, ALU.mult)\
                .then_inc(sem("m1_comb"), 1)
            V.wait_ge(sem("m1_combT"), 1)
            V.tensor_copy(attT[:, :], bank(2)[:, 0:128]).then_inc(sem("m1_combT"), 1)
            V.wait_ge(sem("m1_sig"), 2)
            dve_then(V.tensor_scalar(scr[:, 0:128], scr[:, 0:128], 1.0, None, ALU.add))
            dve_then(V.reciprocal(scr[:, 0:128], scr[:, 0:128]))
            dve_then(V.tensor_tensor(scr[:, 0:128], bank(0)[:, 0:128], scr[:, 0:128], ALU.mult))
            V.tensor_tensor(scr[:, 512:640], bank(1)[:, 0:128], scr[:, 0:128], ALU.mult).then_inc(sem("m1_h"), 1)
            V.wait_ge(sem("m1_h"), 1)
            for u in range(8):
                b = 3 * (u % 2)
                e = scr[:, 0:512]
                V.wait_ge(sem("m1_sig"), u + 3)
                dve_then(V.tensor_scalar(e, e, 1.0, None, ALU.add))
                dve_then(V.reciprocal(e, e))
                dve_then(V.tensor_tensor(e, bank(b), e, ALU.mult))
                dve_then(V.tensor_tensor(e, bank(b + 1), e, ALU.mult))
                if u >= 2:
                    V.wait_ge(sem("m1_down"), u - 1)
                V.tensor_tensor(scr[:, 1024 + 512 * (u % 2):1536 + 512 * (u % 2)]
                                .rearrange("p (m t) -> p m t", m=4),
                                e.rearrange("p (m t) -> p m t", m=4),
                                attT[:, :].unsqueeze(1).to_broadcast([128, 4, T]), ALU.mult)\
                    .then_inc(sem("m1_h"), 1)
                V.wait_ge(sem("m1_h"), u + 2)
            V.wait_ge(sem("m1_down"), 8)
            dve_then(V.tensor_tensor(x[:, :], bank(6)[:, 0:128], x[:, :], ALU.add))

        KL = S + T
        KQ = KL + T
        kq2 = KR[:, 0:KQ]
        aux = KR[:, 2304:2304 + KQ]
        vv = KR[:, 4608:4608 + 17 * D].rearrange("p (c d) -> p c d", c=17)
        pp = KR[:, 6784:6784 + KL]
        ppT = KR[:, 8960:8960 + 17 * D].rearrange("p (c q) -> p c q", c=17)
        xcn = KR[0:C, 11136:13184]
        mrow = KR[0:1, 13184:13184 + KL]
        mrow8 = KR[0:1, 15360:15360 + 512].bitcast(U8)
        l2s = pbuf[:, :, :].rearrange("p a b -> p (a b)")
        lnT, qm = l2s[:, 0:128], l2s[:, 128:384].rearrange("p (h q) -> p h q", h=2)

        def x2_pe():
            for j in range(4):
                mm = PE.matmul(bank(j)[0:C, :], c96[0:C, :], ctxT[0:C, 512 * j:512 * j + 512], start=True, stop=True)
            mm.then_inc(sem("x2_mm"), 1)
            PE.wait_ge(sem("x2_act"), 1)
            for j in range(4):
                mm = PE.matmul(bank(4 + j)[0:C, :], c96[0:C, :], aux[0:C, 512 * j:512 * j + 512],
                               start=True, stop=True)
            mm.then_inc(sem("x2_mm"), 1)
            PE.wait_ge(sem("x2_dve"), 2)
            for j in range(4):
                mm = PE.matmul(bank(j), w("l2", "wkvT")[:, 0:128], xcn[:, 512 * j:512 * j + 512],
                               start=True, stop=True)
            mm.then_inc(sem("x2_mm"), 1)
            for c in range(NC):
                mm = PE.matmul(ps[:, 2048 + 128 * c:2176 + 128 * c], xcn[:, 128 * c:128 * c + 128],
                               w("l2", "wkvT")[:, 128:256], start=True, stop=True)
            mm.then_inc(sem("x2_mm"), 1)
            PE.wait_ge(sem("x2_dve"), 4)
            PE.transpose(bank(0)[:, 0:128], att[:, :], ident[:, :]).then_inc(sem("x2_mm"), 1)
            PE.wait_ge(sem("x2_dve"), 5)
            PE.matmul(bank(1)[:, 0:128], w("l2", "wlT")[:, 0:128], lnT, start=True, stop=True)
            PE.matmul(bank(1)[:, 128:256], w("l2", "wqT"), lnT, start=True, stop=True)
            PE.matmul(bank(2)[:, 0:128], lnT, w("l2", "wlT")[:, 128:256], start=True, stop=True)\
                .then_inc(sem("x2_mm"), 1)
            PE.wait_ge(sem("x2_act"), 2)
            PE.wait_ge(sem("x2_dve"), 6)
            for j in range(5):
                n = min(512, KQ - 512 * j)
                mm = PE.matmul(bank(j)[:, 0:n], half64[:, :], aux[:, 512 * j:512 * j + n], start=True, stop=True)
            mm.then_inc(sem("x2_mm"), 1)
            PE.wait_ge(sem("x2_dve"), 8)
            for h in range(2):
                if h == 1:
                    PE.wait_ge(sem("x2_act"), 4)
                for j in range(5):
                    n = min(512, KL - 512 * j)
                    PE.matmul(bank(j)[:, 0:n], qm[:, h, :], kq2[:, 512 * j:512 * j + n], start=True, stop=False)
                    mm = PE.matmul(bank(j)[:, 0:n], ones[0:1, :], mrow[:, 512 * j:512 * j + n],
                                   start=False, stop=True)
                mm.then_inc(sem("x2_mm"), 1)
                PE.wait_ge(sem("x2_act"), 4 + h)
                for c in range(17):
                    if c % 4 == 0 and c:
                        mm.then_inc(sem("x2_t"), 1)
                    if c % 4 == 0 and c >= 8:
                        PE.wait_ge(sem("x2_te"), 5 * h + c // 4 - 1)
                    if c == 0 and h == 1:
                        PE.wait_ge(sem("x2_te"), 5)
                    mm = PE.transpose(bank(5 + c // 4 % 2)[:, 128 * (c % 4):128 * (c % 4) + 128],
                                      pp[:, 128 * c:128 * c + 128], ident[:, :])
                mm.then_inc(sem("x2_t"), 1)
                PE.wait_ge(sem("x2_te"), 5 * h + 5)
                for c in range(17):
                    mm = PE.matmul(bank(7)[:, 128 * h:128 * h + 128], ppT[:, c, :], vv[:, c, :],
                                   start=(c == 0), stop=(c == 16))
                mm.then_inc(sem("x2_mm"), 1)
            PE.wait_ge(sem("x2_dve"), 10)
            PE.transpose(bank(0)[:, 0:128], att[:, :], ident[:, :]).then_inc(sem("x2_mm"), 1)
            PE.wait_ge(sem("x2_dve"), 11)
            PE.matmul(bank(1)[:, 0:128], attT[:, :], w("l2", "woT"), start=True, stop=False)
            PE.matmul(bank(1)[:, 0:128], ones[0:1, :], w("l2", "bo"), start=False, stop=True)\
                .then_inc(sem("x2_mm"), 1)

        def x2_act():
            A.wait_ge(sem("x2_dve"), 1)
            A.activation(aux[0:C, 0:S], xcn, ACT.Square).then_inc(sem("x2_act"), 1)
            A.wait_ge(sem("x2_mm"), 2)
            act_then(A.activation(aux[0:C, 0:S], bank(4, 4)[0:C, :], ACT.Ln, bias=eps[0:C, :]))
            A.activation(aux[0:C, 0:S], aux[0:C, 0:S], ACT.Exp, scale=-0.5).then_inc(sem("x2_r"), 1)
            A.wait_ge(sem("x2_ls"), 1)
            act_then(A.activation(lnv[:, :], mv[:, 1:2], ACT.Ln, bias=eps[:, :]))
            A.activation(rstd[:, :], lnv[:, :], ACT.Exp, scale=-0.5).then_inc(sem("x2_r"), 1)
            A.wait_ge(sem("x2_dve"), 6)
            A.activation(aux, kq2, ACT.Square).then_inc(sem("x2_act"), 1)
            A.wait_ge(sem("x2_dve"), 7)
            act_then(A.activation(aux, aux, ACT.Ln))
            A.activation(aux, aux, ACT.Exp, scale=-0.5).then_inc(sem("x2_act"), 1)
            for h in range(2):
                A.wait_ge(sem("x2_m"), h + 1)
                if h == 1:
                    A.wait_ge(sem("x2_t"), 5)
                A.activation(pp, ps[:, 0:KL], ACT.Exp, bias=nm[:, h:h + 1], accum_out=rec[:, h:h + 1])\
                    .then_inc(sem("x2_act"), 1)

        def x2_dve():
            V.wait_ge(sem("x2_mm"), 1)
            V.tensor_tensor(xcn, ctxT[0:C, :], bank(0, 4)[0:C, :], ALU.subtract).then_inc(sem("x2_dve"), 1)
            V.wait_ge(sem("x2_dve"), 1)
            V.wait_ge(sem("x2_r"), 1)
            dve_then(V.tensor_tensor(xcn, xcn, aux[0:C, 0:S], ALU.mult))
            V.tensor_scalar(xcn, xcn, w("l2", "lxg"), w("l2", "lxb"), ALU.mult, ALU.add)\
                .then_inc(sem("x2_dve"), 1)
            dve_then(V.bn_stats(st[:, :], xn[:, :]))
            V.bn_aggr(mv[:, :], st[:, :]).then_inc(sem("x2_ls"), 1)
            V.wait_ge(sem("d_m8"), 16)
            dve_then(V.tensor_copy(mrow[:, 0:S], mrow8))
            dve_then(V.tensor_scalar(mrow[:, 0:S], mrow[:, 0:S], -1.0, BIG, ALU.add, ALU.mult))
            dve_then(V.memset(mrow[:, S:KL], 0.0))
            V.wait_ge(sem("x2_mm"), 3)
            V.tensor_copy(kq2[:, 0:S], bank(0, 4)).then_inc(sem("x2_dve"), 1)
            V.wait_ge(sem("x2_mm"), 4)
            dve_then(V.tensor_copy(KR[:, 4608:4608 + S], bank(4, 4)))
            V.wait_ge(sem("x2_r"), 2)
            V.wait_ge(sem("x2_ls"), 1)
            V.tensor_scalar(att[:, :], xn[:, :], mv[:, 0:1], rstd[:, :], ALU.subtract, ALU.mult)\
                .then_inc(sem("x2_dve"), 1)
            V.wait_ge(sem("x2_mm"), 5)
            V.tensor_scalar(lnT, bank(0)[:, 0:128], w("l2", "llg"), w("l2", "llb"), ALU.mult, ALU.add)\
                .then_inc(sem("x2_dve"), 1)
            V.wait_ge(sem("x2_mm"), 6)
            dve_then(V.tensor_copy(vv[:, 16, :], bank(2)[:, 0:128]))
            V.tensor_copy(kq2[:, S:KQ], bank(1)[:, 0:256]).then_inc(sem("x2_dve"), 1)
            V.wait_ge(sem("x2_dve"), 6)
            V.wait_ge(sem("x2_mm"), 7)
            V.tensor_scalar(aux, ps[:, 0:KQ], 1e-16, None, ALU.max).then_inc(sem("x2_dve"), 1)
            V.wait_ge(sem("x2_act"), 3)
            dve_then(V.tensor_tensor(kq2, kq2, aux, ALU.mult))
            dve_then(V.tensor_scalar(kq2[:, 0:KL], kq2[:, 0:KL], w("l2", "kng"), None, ALU.mult))
            dve_then(V.tensor_scalar(kq2[:, KL:KQ], kq2[:, KL:KQ], w("l2", "qng"), 64 ** -0.5, ALU.mult, ALU.mult))
            for h in range(2):
                dve_then(V.tensor_scalar(qm[:, h, :], kq2[:, KL:KQ], mh[:, h:h + 1], None, ALU.mult))
            V.sem_inc(sem("x2_dve"), 1)
            for h in range(2):
                V.wait_ge(sem("x2_mm"), 8 + 2 * h)
                V.tensor_reduce(nm[:, h:h + 1], ps[:, 0:KL], AX.X, ALU.max, negate=True).then_inc(sem("x2_m"), 1)
                for i in range(5):
                    V.wait_ge(sem("x2_t"), 5 * h + i + 1)
                    n = min(4, 17 - 4 * i)
                    V.tensor_copy(ppT[:, 4 * i:4 * i + n, :].rearrange("p c q -> p (c q)"),
                                  bank(5 + i % 2)[:, 0:128 * n]).then_inc(sem("x2_te"), 1)
                V.wait_ge(sem("x2_mm"), 9 + 2 * h)
                V.wait_ge(sem("x2_act"), 4 + h)
                dve_then(V.reciprocal(sc1[:, :], rec[:, h:h + 1]))
                V.tensor_scalar(att[:, 64 * h:64 * h + 64], bank(7)[:, 192 * h:192 * h + 64], sc1[:, :], None,
                                ALU.mult).then_inc(sem("x2_dve"), 1)
            V.wait_ge(sem("x2_mm"), 12)
            V.tensor_copy(attT[:, :], bank(0)[:, 0:128]).then_inc(sem("x2_dve"), 1)
            V.wait_ge(sem("x2_mm"), 13)
            dve_then(V.tensor_tensor(x[:, :], bank(1)[:, 0:128], x[:, :], ALU.add))

        fk, fq, ve, fe = (l2s[:, 512 + 256 * i:768 + 256 * i] for i in range(4))
        kvm = l2s[:, 1536:1536 + 144]

        def lin_pe():
            PE.matmul(bank(0)[:, 0:128], w("l2", "aq"), xnT[:, :], start=True, stop=True)
            PE.matmul(bank(1)[:, 0:128], xnT[:, :], w("l2", "ak"), start=True, stop=False)
            PE.matmul(bank(1)[:, 0:128], ones[0:1, :], w("l2", "abk"), start=False, stop=True)\
                .then_inc(sem("li_mm"), 1)
            PE.matmul(bank(2)[:, 0:128], xnT[:, :], w("l2", "av"), start=True, stop=False)
            PE.matmul(bank(2)[:, 0:128], ones[0:1, :], w("l2", "abv"), start=False, stop=True)\
                .then_inc(sem("li_mm"), 1)
            PE.wait_ge(sem("li_dve"), 3)
            PE.matmul(bank(3)[:, 0:129], fk[:, 0:128], ve[:, 0:129], start=True, stop=True)\
                .then_inc(sem("li_mm"), 1)
            PE.wait_ge(sem("li_dve"), 4)
            PE.matmul(bank(4)[:, 0:144], fq[:, 0:128], kvm, start=True, stop=True)\
                .then_inc(sem("li_mm"), 1)
            PE.wait_ge(sem("li_dve"), 5)
            PE.transpose(bank(5)[:, 0:128], att[:, :], ident[:, :]).then_inc(sem("li_mm"), 1)
            PE.wait_ge(sem("li_dve"), 6)
            PE.matmul(bank(6)[:, 0:128], attT[:, :], w("l2", "ao"), start=True, stop=False)
            PE.matmul(bank(6)[:, 0:128], ones[0:1, :], w("l2", "abo"), start=False, stop=True)\
                .then_inc(sem("li_mm"), 1)

        def lin_act():
            A.wait_ge(sem("li_dve"), 1)
            A.activation(fe[:, 0:128], fe[:, 0:128], ACT.Exp).then_inc(sem("li_act"), 1)
            A.wait_ge(sem("li_dve"), 2)
            A.activation(fe[:, 128:256], fe[:, 128:256], ACT.Exp).then_inc(sem("li_act"), 1)

        def lin_dve():
            V.wait_ge(sem("li_mm"), 1)
            dve_then(V.tensor_scalar(fq[:, 128:256], bank(0)[:, 0:128], w("l2", "abq"), None, ALU.add))
            V.tensor_scalar(fe[:, 0:128], fq[:, 128:256], 0.0, None, ALU.min).then_inc(sem("li_dve"), 1)
            V.tensor_scalar(fe[:, 128:256], bank(1)[:, 0:128], 0.0, None, ALU.min).then_inc(sem("li_dve"), 1)
            dve_then(V.memset(ve[:, 128:129], 1.0))
            V.wait_ge(sem("li_mm"), 2)
            dve_then(V.tensor_copy(ve[:, 0:128], bank(2)[:, 0:128]))
            V.wait_ge(sem("li_act"), 1)
            dve_then(V.scalar_tensor_tensor(fq[:, 0:128], fq[:, 128:256], 0.0, fe[:, 0:128], ALU.max, ALU.add))
            V.wait_ge(sem("li_act"), 2)
            V.scalar_tensor_tensor(fk[:, 0:128], bank(1)[:, 0:128], 0.0, fe[:, 128:256], ALU.max, ALU.add)\
                .then_inc(sem("li_dve"), 1)
            V.wait_ge(sem("li_mm"), 3)
            dve_then(V.tensor_tensor(kvm[:, 0:128].rearrange("p (h d) -> p h d", h=H),
                                     bank(3)[:, 0:128].rearrange("p (h d) -> p h d", h=H),
                                     m8[:, :].unsqueeze(2).to_broadcast([128, H, HD]), ALU.mult))
            dve_then(V.tensor_copy(sc1[:, :], bank(3)[:, 128:129]))
            V.tensor_scalar(kvm[:, 128:144], m8[:, :], sc1[:, :], None, ALU.mult).then_inc(sem("li_dve"), 1)
            V.wait_ge(sem("li_mm"), 4)
            dve_then(V.tensor_scalar(rec[:, :], bank(4)[:, 128:144], 1e-6, None, ALU.max))
            dve_then(V.reciprocal(rec[:, :], rec[:, :]))
            V.tensor_tensor(att[:, :].rearrange("p (h d) -> p h d", h=H),
                            bank(4)[:, 0:128].rearrange("p (h d) -> p h d", h=H),
                            rec[:, :].unsqueeze(2).to_broadcast([128, H, HD]), ALU.mult)\
                .then_inc(sem("li_dve"), 1)
            V.wait_ge(sem("li_mm"), 5)
            V.tensor_copy(attT[:, :], bank(5)[:, 0:128]).then_inc(sem("li_dve"), 1)
            V.wait_ge(sem("li_mm"), 6)
            dve_then(V.tensor_tensor(x[:, :], bank(6)[:, 0:128], x[:, :], ALU.add))

        ew = w32[:, 4096:8192]

        def moe2_pe():
            PE.matmul(bank(7)[:, 128:160], xnT[:, :], w("l2", "rwT"), start=True, stop=True)\
                .then_inc(sem("m2_gate"), 1)
            PE.wait_ge(sem("d_ew"), 16)
            for u in range(8):
                if u >= 4:
                    PE.wait_ge(sem("m2_acc"), 4 * (u - 3))
                PE.matmul(bank(u % 4), xnT[:, :], ew[:, 512 * u:512 * u + 512], start=True, stop=True)\
                    .then_inc(sem("m2_mm"), 1)

        def moe2_act():
            A.wait_ge(sem("m2_s"), 1)
            A.activation(sm[:, 0:32], bank(7)[:, 128:160], ACT.Exp, bias=nm[:, 0:1], accum_out=sc1[:, :])\
                .then_inc(sem("m2_e"), 1)

        def moe2_dve():
            V.wait_ge(sem("m2_gate"), 1)
            V.tensor_reduce(nm[:, 0:1], bank(7)[:, 128:160], AX.X, ALU.max, negate=True).then_inc(sem("m2_s"), 1)
            V.wait_ge(sem("m2_e"), 1)
            dve_then(V.reciprocal(sc1[:, :], sc1[:, :]))
            dve_then(V.tensor_scalar(lw[:, 0:32], sm[:, 0:32], sc1[:, :], None, ALU.mult))
            top_k(32, 2, sel[:, 0:32])
            dve_then(V.tensor_tensor(sel[:, 0:32], sel[:, 0:32], lw[:, 0:32], ALU.mult))
            for e in range(32):
                if e % 4 == 0:
                    V.wait_ge(sem("m2_mm"), e // 4 + 1)
                V.scalar_tensor_tensor(x[:, :], bank(e // 4 % 4)[:, 128 * (e % 4):128 * (e % 4) + 128],
                                       sel[:, e:e + 1], x[:, :], ALU.mult, ALU.add).then_inc(sem("m2_acc"), 1)
                V.wait_ge(sem("m2_acc"), e + 1)

        q3, k3, v3s = (l2s[:, 128 * i:128 * i + 128] for i in range(3))
        kbd = r32[:, 0:2048]
        s3 = r32[:, 2048:4096]
        p3T = r32[:, 4096:6144]

        def self_pe():
            PE.matmul(bank(0)[:, 0:128], w("l3", "sqT"), xnT[:, :], start=True, stop=True)
            PE.matmul(bank(1)[:, 0:128], w("l3", "skT"), xnT[:, :], start=True, stop=True)
            PE.matmul(bank(2)[:, 0:128], xnT[:, :], w("l3", "svT"), start=True, stop=True)\
                .then_inc(sem("sa_mm"), 1)
            PE.wait_ge(sem("sa_dve"), 1)
            for j in range(4):
                mm = PE.matmul(bank(4 + j), q3, kbd[:, 512 * j:512 * j + 512], start=True, stop=True)
            mm.then_inc(sem("sa_mm"), 1)
            PE.wait_ge(sem("sa_exp"), 1)
            for g in range(4):
                for h in range(4 * g, 4 * g + 4):
                    mm = PE.transpose(bank(g)[:, 128 * (h % 4):128 * (h % 4) + 128],
                                      s3[:, 128 * h:128 * h + 128], ident[:, :])
                mm.then_inc(sem("sa_t"), 1)
            for g in range(4):
                PE.wait_ge(sem("sa_te"), g + 1)
                for h in range(4 * g, 4 * g + 4):
                    mm = PE.matmul(bank(4)[:, HD * h:HD * h + HD], p3T[:, 128 * h:128 * h + 128],
                                   v3s[:, HD * h:HD * h + HD], start=True, stop=True)
            mm.then_inc(sem("sa_mm"), 1)

        def self_act():
            A.wait_ge(sem("sa_dve"), 2)
            A.activation(s3, s3, ACT.Exp).then_inc(sem("sa_exp"), 1)
            for g in (1, 3):
                A.wait_ge(sem("sa_t"), g + 1)
                A.wait_ge(sem("sa_te"), g)
                A.activation(p3T[:, 512 * g:512 * g + 512], bank(g), ACT.Copy).then_inc(sem("sa_te"), 1)

        def self_dve():
            V.wait_ge(sem("sa_mm"), 1)
            dve_then(V.tensor_scalar(q3, bank(0)[:, 0:128], HD ** -0.5, None, ALU.mult))
            dve_then(V.tensor_copy(v3s, bank(2)[:, 0:128]))
            V.tensor_tensor(kbd.rearrange("p (h k) -> p h k", h=H),
                            bank(1)[:, 0:128].unsqueeze(1).to_broadcast([128, H, 128]),
                            m8[:, :].unsqueeze(2).to_broadcast([128, H, 128]), ALU.mult).then_inc(sem("sa_dve"), 1)
            V.wait_ge(sem("sa_mm"), 2)
            dve_then(V.tensor_reduce(nm[:, :], bank(4, 4).rearrange("p (h k) -> p h k", h=H), AX.X, ALU.max))
            V.tensor_tensor(s3.rearrange("p (h k) -> p h k", h=H), bank(4, 4).rearrange("p (h k) -> p h k", h=H),
                            nm[:, :].unsqueeze(2).to_broadcast([128, H, 128]), ALU.subtract)\
                .then_inc(sem("sa_dve"), 1)
            V.wait_ge(sem("sa_exp"), 1)
            dve_then(V.tensor_reduce(rec[:, :], s3.rearrange("p (h k) -> p h k", h=H), AX.X, ALU.add))
            for g in (0, 2):
                V.wait_ge(sem("sa_t"), g + 1)
                V.wait_ge(sem("sa_te"), g) if g else None
                V.tensor_copy(p3T[:, 512 * g:512 * g + 512], bank(g)).then_inc(sem("sa_te"), 1)
            dve_then(V.reciprocal(rec[:, :], rec[:, :]))
            V.wait_ge(sem("sa_mm"), 3)
            dve_then(V.tensor_tensor(att[:, :].rearrange("p (h d) -> p h d", h=H),
                                     bank(4)[:, 0:128].rearrange("p (h d) -> p h d", h=H),
                                     rec[:, :].unsqueeze(2).to_broadcast([128, H, HD]), ALU.mult))
            dve_then(V.tensor_tensor(x[:, :], att[:, :], x[:, :], ALU.add))

        f8 = sb("f8", [128, 128], FP8)
        fb = sb("fb", [128, 128], BF16)
        fy = sb("fy", [128, 128], BF16)
        fout = sb("fout", [128, 128], BF16)
        u8m = attT[:, :].bitcast(mybir.dt.uint32)

        def quantise(src, dst):
            dve_then(V.tensor_scalar(r1[:, :], src, 240.0, -240.0, ALU.min, ALU.max))
            dve_then(V.tensor_copy(f8[:, :], r1[:, :], saturate=False))
            dve_then(V.tensor_copy(dst, f8[:, :]))
            dve_then(V.tensor_scalar(r1[:, :], src, 0.5, 240.0, ALU.mult, ALU.min))
            dve_then(V.tensor_scalar(r1[:, :], r1[:, :], -240.0, None, ALU.max))
            dve_then(V.tensor_copy(f8[:, :], r1[:, :], saturate=False))
            dve_then(V.tensor_scalar(r1[:, :], f8[:, :], 2.0, None, ALU.mult))
            dve_then(V.tensor_tensor(r2[:, :], r1[:, :], r1[:, :], ALU.mult))
            dve_then(V.tensor_scalar(r2[:, :], r2[:, :], 480.0 ** 2, 3e38, ALU.is_ge, ALU.mult))
            dve_then(V.tensor_scalar(r2[:, :], r2[:, :], 3e38, None, ALU.mult))
            dve_then(V.tensor_tensor(r1[:, :], r1[:, :], r2[:, :], ALU.add))
            dve_then(V.tensor_tensor(r1[:, :], r1[:, :], r2[:, :], ALU.subtract))
            dve_then(V.tensor_tensor(r2[:, :], src, src, ALU.mult))
            dve_then(V.tensor_scalar(u8m[:, :], r2[:, :], 240.0 ** 2, None, ALU.is_gt))
            dve_then(V.tensor_copy(fb[:, :], r1[:, :]))
            dve_then(V.copy_predicated(dst, u8m[:, :], fb[:, :]))

        def fp8_pe():
            PE.wait_ge(sem("f_q"), 1)
            PE.transpose(bank(0).bitcast(BF16)[:, 0:128], fy[:, :], identb[:, :]).then_inc(sem("f_mm"), 1)
            PE.wait_ge(sem("f_q"), 2)
            PE.matmul(bank(1)[:, 0:128], fout[:, :], kq[:, :], start=True, stop=True).then_inc(sem("f_mm"), 1)

        def fp8_dve():
            V.wait_ge(sem("d_f"), 64)
            dve_then(V.reciprocal(sc1[:, :], skk[:, :]))
            dve_then(V.tensor_scalar(kq32[:, :], kq[:, :], sc1[:, :], None, ALU.mult))
            quantise(kq32[:, :], kq[:, :])
            dve_then(V.reciprocal(sc2[:, :], sin[:, :]))
            dve_then(V.tensor_tensor(skk[:, :], skk[:, :], sin[:, :], ALU.mult))
            dve_then(V.tensor_copy(fb[:, :], xn[:, :]))
            dve_then(V.tensor_scalar(kq32[:, :], fb[:, :], sc2[:, :], None, ALU.mult))
            quantise(kq32[:, :], fy[:, :])
            V.sem_inc(sem("f_q"), 1)
            V.wait_ge(sem("f_mm"), 1)
            V.tensor_copy(fout[:, :], bank(0).bitcast(BF16)[:, 0:128]).then_inc(sem("f_q"), 1)
            V.wait_ge(sem("f_mm"), 2)
            dve_then(V.tensor_scalar(fb[:, :], bank(1)[:, 0:128], skk[:, :], None, ALU.mult))
            dve_then(V.tensor_tensor(fy[:, :], fb[:, :], fbias[:, :], ALU.add))
            V.tensor_tensor(x[:, :], x[:, :], fy[:, :], ALU.add).then_inc(sem("x_done"), 1)

        mask3 = w32[:, 0:2048]
        mask3u = w32[:, 2048:2560].bitcast(U8)
        mrow3 = w32[0:1, 2560:3584].bitcast(BF16)
        mrow3h = mrow3.unsqueeze(1).to_broadcast([1, H, S])

        @block.sync
        def _(sy):
            load(sy, x[:, :], a["x"], "x")
            load(sy, ctxT[0:C, :], a["ctxT"], "ctxT")
            load(sy, packs["ctx"][:, :], a["pack_ctx"], "ctx")
            load(sy, r32[:, 0:lay["x0"][1]], a["pack_x0"], "x0")
            load(sy, ctx1[:, :, 0:C], a["ctx"].rearrange("(c p) n -> p c n", p=128), "ctx1")
            load(sy, packs["l0"][:, :], a["pack_l0"], "l0")
            load(sy, packs["l1"][:, :], a["pack_l1"], "l1")
            load(sy, packs["l2"][:, :], a["pack_l2"], "l2")
            load(sy, packs["l3"][:, :], a["pack_l3"], "l3")
            load(sy, gbias[:, :], a["gbias"].to_broadcast([128, 64]), "gb")
            load(sy, kq[:, :], a["kernel"], "f")
            load(sy, fbias[:, :], a["fbias"].to_broadcast([128, 128]), "f")
            load(sy, sin[:, :], a["s_in"].to_broadcast([128, 1]), "f")
            load(sy, skk[:, :], a["s_k"].to_broadcast([128, 1]), "f")
            stack_keys_sync(0)
            load(sy, w32[:, 0:4096], a["w1"], "w12")
            load(sy, w32[:, 4096:8192], a["w2"], "w12")
            sy.wait_ge(sem("x0_done"), 1)
            load(sy, egT, a["eg"], "eg")
            load(sy, euT, a["eu"], "eg")
            sy.wait_ge(sem("m0_selT"), 2)
            load(sy, w32[:, 0:4096], a["ed"], "eg")
            load(sy, ew, a["ew"], "ew")
            stack_queries_sync(0)
            sy.wait_ge(sem("mamba_done"), 1)
            load(sy, mrow8, a["mask2"], "m8")
            sy.wait_ge(sem("moe1_done"), 1)
            load(sy, mask3u, a["mask3"].to_broadcast([128, S]), "m3")
            stack_keys_sync(1)
            sy.wait_ge(sem("mrow3"), 1)
            sy.dma_start(KS[KROWS:KROWS + 1, :, :], mrow3h).then_inc(sem("d_mask3"), 16)
            stack_queries_sync(1)
            sy.wait_ge(sem("ks_ones"), 2)
            sy.dma_start(qs[KROWS:KROWS + 1, :], KS[0:1, 0, 0:H * T]).then_inc(sem("d_mask3"), 16)
            sy.wait_ge(sem("x_done"), 1)
            sy.dma_start(out, x[:, :]).then_inc(sem("d_out"), 16)
            sy.wait_ge(sem("d_out"), 16)

        @block.gpsimd
        def _(g):
            pool_then(G.memset(ident[:, :], 0.0))
            pool_then(G.affine_select(out=ident[:, :], in_=ident[:, :], compare_op=ALU.not_equal, fill=1.0,
                                      base=0, pattern=[[-1, 128]], channel_multiplier=1))
            pool_then(G.memset(identb[:, :], 0.0))
            pool_then(G.affine_select(out=identb[:, :], in_=identb[:, :], compare_op=ALU.not_equal, fill=1.0,
                                      base=0, pattern=[[-1, 128]], channel_multiplier=1))
            pool_then(G.memset(ones[:, :], 1.0))
            pool_then(G.memset(one[:, :], 1.0))
            pool_then(G.memset(eps[:, :], EPS))
            pool_then(G.memset(c96[:, :], 1.0 / C))
            pool_then(G.memset(c256[:, :], 1.0 / 256))
            pool_then(G.memset(ctx1[:, :, C:C + 1], 1.0))
            pool_then(G.memset(ctxT[C:128, :], 1.0))
            pool_then(G.memset(nmx[:, :], 0.0))
            pool_then(G.memset(m16[:, :], 0.0))
            for b in (0, 16, 32, 96):
                pool_then(G.affine_select(out=m16[:, :], in_=m16[:, :], compare_op=ALU.not_equal, fill=1.0,
                                          base=-b, pattern=[[-1, H]], channel_multiplier=1))
            for t, wd, n, v, inner in ((m8, HD, H, 1.0, 1), (mh, 64, 2, 1.0, 1), (half64, 64, 2, 1.0 / 64, 64)):
                pool_then(G.memset(t[:, :], v))
                view = t[:, :].rearrange("p (h i) -> p h i", h=n)
                pool_then(G.affine_select(out=view, in_=view, compare_op=ALU.is_ge, fill=0.0, base=0,
                                          pattern=[[-wd, n], [0, inner]], channel_multiplier=1))
                pool_then(G.affine_select(out=view, in_=view, compare_op=ALU.is_ge, fill=0.0, base=wd - 1,
                                          pattern=[[wd, n], [0, inner]], channel_multiplier=-1))
            pool_then(G.memset(qs[:, :], 0.0))
            G.sem_inc(sem("qs_clear"), 1)
            G.sem_inc(sem("consts"), 1)
            pool_then(G.memset(ks_region[0:SHIFT, :], TWO_ONES))
            G.sem_inc(sem("ks_ones"), 1)
            split_keys_pool(0)
            G.wait_ge(sem("n_att"), 1)
            pool_then(G.memset(qs[:, :], 0.0))
            G.sem_inc(sem("qs_clear"), 1)
            split_keys_pool(1)
            G.wait_ge(sem("x2_done"), 1)
            pool_then(G.memset(ks_region[0:SHIFT, :], TWO_ONES))
            G.sem_inc(sem("ks_ones"), 1)

        @block.scalar
        def _(act):
            A.preload_act_table_set("natural_log_exp_and_others")
            A.wait_ge(sem("consts"), 1)
            A.wait_ge(sem("d_ctx"), 16)
            keys_act(0)
            norm_act(0)
            x0_act()
            norm_act(1)
            rec_act()
            norm_act(2)
            moe0_act()
            norm_act(3)
            narrow_act(0)
            norm_act(4)
            mamba_act()
            norm_act(5)
            moe1_act()
            norm_act(6)
            x2_act()
            norm_act(7)
            lin_act()
            norm_act(8)
            moe2_act()
            norm_act(9)
            narrow_act(1)
            norm_act(10)
            self_act()
            norm_act(11)

        @block.vector
        def _(dve):
            V.wait_ge(sem("consts"), 1)
            dve_then(V.tensor_reduce(m4[:, :], m8[:, :].rearrange("p (g j) -> p j g", g=4), AX.X, ALU.add))
            V.wait_ge(sem("d_x"), 16)
            norm_dve(0)
            V.wait_ge(sem("d_ctxT"), 16)
            V.tensor_copy(ctxR[:, :], ctxT[0:C, :]).then_inc(sem("ctxR"), 1)
            x0_dve()
            V.sem_inc(sem("x0_done"), 1)
            V.wait_ge(sem("v_mm"), 1)
            V.tensor_copy(v1[:, :, :].rearrange("p c d -> p (c d)"), bank(0, 4)).then_inc(sem("v_ev"), 1)
            norm_dve(1)
            rec_dve()
            norm_dve(2)
            moe0_dve()
            norm_dve(3)
            V.wait_ge(sem("d_l1"), 16)
            narrow_dve(0)
            norm_dve(4)
            mamba_dve()
            V.sem_inc(sem("mamba_done"), 1)
            norm_dve(5)
            moe1_dve()
            V.sem_inc(sem("moe1_done"), 1)
            norm_dve(6)
            V.wait_ge(sem("d_l2"), 16)
            x2_dve()
            V.sem_inc(sem("x2_done"), 1)
            V.wait_ge(sem("d_m3"), 16)
            dve_then(V.tensor_copy(mask3, mask3u))
            V.tensor_scalar(mrow3, mask3[0:1, :], -1.0, BIG, ALU.add, ALU.mult).then_inc(sem("mrow3"), 1)
            V.wait_ge(sem("k_mm"), 2)
            V.tensor_tensor(kv_views(1)[0], bank(0, 4), mask3, ALU.mult).then_inc(sem("k_ev"), 1)
            V.wait_ge(sem("v_mm"), 2)
            V.tensor_copy(v3[:, :, :].rearrange("p c d -> p (c d)"), bank(4, 4)).then_inc(sem("v_ev"), 1)
            norm_dve(7)
            lin_dve()
            norm_dve(8)
            moe2_dve()
            norm_dve(9)
            narrow_dve(1)
            norm_dve(10)
            self_dve()
            norm_dve(11)
            fp8_dve()

        @block.tensor
        def _(pe):
            PE.wait_ge(sem("consts"), 1)
            PE.wait_ge(sem("d_ctx"), 16)
            PE.wait_ge(sem("d_ctxT"), 16)
            keys_pe(0)
            norm_pe(0)
            PE.wait_ge(sem("k_ev"), 1)
            PE.wait_ge(sem("d_ctx1"), 16)
            x0_pe()
            PE.wait_ge(sem("x0_done"), 1)
            values_pe(0, 0)
            PE.wait_ge(sem("v_ev"), 1)
            norm_pe(1)
            rec_pe()
            norm_pe(2)
            moe0_pe()
            norm_pe(3)
            PE.wait_ge(sem("d_l1"), 16)
            narrow_pe(0)
            norm_pe(4)
            mamba_pe()
            norm_pe(5)
            moe1_pe()
            norm_pe(6)
            PE.wait_ge(sem("d_l2"), 16)
            x2_pe()
            PE.wait_ge(sem("x2_done"), 1)
            PE.wait_ge(sem("d_l3"), 16)
            keys_pe(1)
            values_pe(1, 4)
            PE.wait_ge(sem("v_ev"), 2)
            norm_pe(7)
            lin_pe()
            norm_pe(8)
            moe2_pe()
            norm_pe(9)
            narrow_pe(1)
            norm_pe(10)
            self_pe()
            norm_pe(11)
            fp8_pe()


def _packed(np, spec, parts):
    at = sum(cols for _, _, cols in spec)
    out = np.zeros((128, at), np.float32)
    at = 0
    for name, rows, cols in spec:
        out[0:rows, at:at + cols] = parts[name].reshape(rows, cols)
        at += cols
    return out


def kernel(**inputs):
    import numpy as np
    import concourse.bacc as _bacc
    from concourse import mybir as _mybir
    from concourse.bass_utils import run_bass_kernel_spmd as _run

    i = {k: np.asarray(v) for k, v in inputs.items()}

    def col(v, n=1):
        return v.reshape(n, -1).T

    cw = i["L1_attn_conv_w"].reshape(2, 128, 4).transpose(1, 0, 2)
    ar = {
        "x": i["x"].reshape(T, D),
        "ctx": i["ctx_768"].reshape(S, C),
        "ctxT": i["ctx_768"].reshape(S, C).T,
        "pack_ctx": _packed(np, SPEC_CTX, {
            "wk1": i["L1_xattn_Wk"], "wv1": i["L1_xattn_Wv"], "bk1": i["L1_xattn_bk"]}),
        "pack_x0": _packed(np, SPEC_X0, {
            "wq": i["L0_xattn_Wq"],
            "wkT": i["L0_xattn_Wk"].reshape(C, H, DH0).transpose(2, 1, 0),
            "wv": i["L0_xattn_Wv"],
            "wo": i["L0_xattn_Wo"].reshape(H, DH0, D).transpose(1, 0, 2),
            "bo": i["L0_xattn_bo"]}),
        "pack_l0": _packed(np, SPEC_L0, {
            "waT": i["L0_attn_Wa_w"].T, "wab": i["L0_attn_Wa_b"], "bT": i["L0_attn_B_w"].T,
            "cT": i["L0_attn_C_w"].T, "dT": i["L0_attn_D_w"].T, "gw": i["L0_ffn_gate_w"],
            "gb": i["L0_ffn_gate_b"], "b1": i["L0_ffn_b1"].reshape(8, 4, 128).transpose(2, 0, 1),
            "b2": i["L0_ffn_b2"]}),
        "pack_l1": _packed(np, SPEC_L1, {
            "wq": i["L1_xattn_Wq"], "bq": i["L1_xattn_bq"], "bv": i["L1_xattn_bv"], "wo": i["L1_xattn_Wo"],
            "bo": i["L1_xattn_bo"], "inT": i["L1_attn_in_proj_w"].T, "convw": cw,
            "convb": col(i["L1_attn_conv_b"], 2),
            "xpT": i["L1_attn_x_proj_w"].reshape(33, 2, 128).transpose(2, 1, 0),
            "alog": i["L1_attn_A_log"].reshape(2, 128, 16).transpose(1, 0, 2),
            "dpar": col(i["L1_attn_D_param"], 2), "dtw": col(i["L1_attn_dt_w"], 2),
            "dtb": col(i["L1_attn_dt_b"], 2),
            "outT": i["L1_attn_out_w"].reshape(D, 2, 128).transpose(2, 1, 0),
            "lng": col(i["L1_attn_ln_g"], 2), "lnb": col(i["L1_attn_ln_b"], 2),
            "gateT": i["L1_ffn_gate_w"].T, "sgT": i["L1_ffn_sg_w"].T, "suT": i["L1_ffn_su_w"].T,
            "sdT": i["L1_ffn_sd_w"].T}),
        "pack_l2": _packed(np, SPEC_L2, {
            "wkvT": i["L2_xattn_Wkv"].T, "wqT": i["L2_xattn_Wq"].T, "wlT": i["L2_xattn_Wlkv"].T,
            "woT": i["L2_xattn_Wo"].T, "bo": i["L2_xattn_bo"], "lxg": i["L2_xattn_ln_x_g"],
            "lxb": i["L2_xattn_ln_x_b"], "llg": i["L2_xattn_ln_l_g"], "llb": i["L2_xattn_ln_l_b"],
            "qng": np.concatenate([i["L2_xattn_qn_g"]] * 2), "kng": np.concatenate([i["L2_xattn_kn_g"]] * 2),
            "aq": i["L2_attn_Wq"], "ak": i["L2_attn_Wk"], "av": i["L2_attn_Wv"], "ao": i["L2_attn_Wo"],
            "abq": i["L2_attn_bq"], "abk": i["L2_attn_bk"], "abv": i["L2_attn_bv"], "abo": i["L2_attn_bo"],
            "rwT": i["L2_ffn_router_w"].T}),
        "pack_l3": _packed(np, SPEC_L3, {
            "wq": i["L3_xattn_Wq"], "wk": i["L3_xattn_Wk"], "wv": i["L3_xattn_Wv"], "wo": i["L3_xattn_Wo"],
            "sqT": i["L3_attn_Wq"].T, "skT": i["L3_attn_Wk"].T, "svT": i["L3_attn_Wv"].T}),
        "w1": i["L0_ffn_w1"].transpose(1, 0, 2).reshape(D, 4096),
        "w2": i["L0_ffn_w2"].reshape(8, 4, 128, D).transpose(2, 0, 1, 3).reshape(128, 4096),
        "eg": i["L1_ffn_eg_w"].transpose(2, 1, 0).reshape(D, 4096),
        "eu": i["L1_ffn_eu_w"].transpose(2, 1, 0).reshape(D, 4096),
        "ed": i["L1_ffn_ed_w"].transpose(2, 0, 1).reshape(32, 128, D).transpose(1, 0, 2).reshape(128, 4096),
        "ew": i["L2_ffn_expert_weights"].transpose(1, 0, 2).reshape(D, 4096),
        "gbias": i["L1_ffn_gate_bias"].reshape(1, 64),
        "kernel": i["L3_ffn_kernel"],
        "fbias": i["L3_ffn_bias"].reshape(1, D),
        "s_in": i["L3_ffn_input_scale"].reshape(1, 1),
        "s_k": i["L3_ffn_kernel_scale"].reshape(1, 1),
        "mask2": i["mask_BxS2_bk0"].reshape(1, S),
        "mask3": i["mask_BxS2_bf1"].reshape(1, S),
    }
    nc = _bacc.Bacc("TRN2", target_bir_lowering=False, num_devices=1)
    arrays, aps = {}, {}
    for name, v in ar.items():
        v = np.ascontiguousarray(v)
        arrays["in_" + name] = v
        aps[name] = nc.dram_tensor("in_" + name, v.shape, _mybir.dt.from_np(v.dtype), kind="ExternalInput").ap()
    res = nc.dram_tensor("out_0", (T, D), _mybir.dt.float32, kind="ExternalOutput").ap()
    perceiver(nc, aps, res)
    r = _run(nc, [arrays], core_ids=[0])
    return r.results[0]["out_0"].reshape(1, T, D)
```

```python
from contextlib import ExitStack

import concourse.bass as bass
from concourse import mybir

F32 = mybir.dt.float32
F32R = mybir.dt.float32r
BF16 = mybir.dt.bfloat16
FP8 = mybir.dt.float8e4
U8 = mybir.dt.uint8
ALU = mybir.AluOpType
ACT = mybir.ActivationFunctionType
AX = mybir.AxisListType

T = 128
D = 128
C = 96
S = 2048
NC = S // 128
H = 16
DH0 = 64
HD = D // H
EPS = 1e-5
CLAMP = 10000.0
BIG = 1e30
SENT = -3e38
TAKEN = 3e38

TWO_ONES = 1.0 + 0x3F80 * 2.0 ** -23

SHIFT = 3 * H
PROD = 9 * HD
KROWS = SHIFT + PROD
QH = 4


def pack_layout(spec):
    at, out = 0, {}
    for name, rows, cols in spec:
        out[name] = (rows, at, cols)
        at += cols
    return out, at


SPEC_CTX = [("wk1", C, D), ("wv1", C, D), ("bk1", D, 1)]
SPEC_X0 = [("wq", D, H * DH0), ("wkT", DH0, H * C), ("wv", C, H * DH0), ("wo", DH0, H * D), ("bo", 1, D)]
SPEC_L0 = [("waT", D, 32), ("wab", 32, 1), ("bT", D, 32), ("cT", 32, D), ("dT", D, D),
           ("gw", D, 8), ("gb", 1, 8), ("b1", 128, 32), ("b2", 8, D)]
SPEC_L1 = [("wq", D, D), ("bq", D, 1), ("bv", D, 1), ("wo", D, D), ("bo", 1, D),
           ("inT", D, 512), ("convw", D, 8), ("convb", D, 2), ("xpT", D, 66), ("alog", D, 32),
           ("dpar", D, 2), ("dtw", D, 2), ("dtb", D, 2), ("outT", D, 256), ("lng", D, 2), ("lnb", D, 2),
           ("gateT", D, 64), ("sgT", D, D), ("suT", D, D), ("sdT", D, D)]
SPEC_L2 = [("wkvT", C, 256), ("wqT", D, D), ("wlT", D, 256), ("woT", D, D), ("bo", 1, D),
           ("lxg", C, 1), ("lxb", C, 1), ("llg", D, 1), ("llb", D, 1), ("qng", D, 1), ("kng", D, 1),
           ("aq", D, D), ("ak", D, D), ("av", D, D), ("ao", D, D), ("abq", D, 1),
           ("abk", 1, D), ("abv", 1, D), ("abo", 1, D), ("rwT", D, 32)]
SPEC_L3 = [("wq", D, D), ("wk", C, D), ("wv", C, D), ("wo", D, D), ("sqT", D, D), ("skT", D, D), ("svT", D, D)]


def perceiver(nc, a, out):
    ctx = ExitStack()
    with ctx:
        sems = {}

        def sem(name):
            if name not in sems:
                sems[name] = ctx.enter_context(nc.semaphore(name))
            return sems[name]

        def sb(name, shape, dt=F32):
            return ctx.enter_context(nc.sbuf_tensor(name, shape, dt))

        lay = {}
        for key, spec in (("ctx", SPEC_CTX), ("x0", SPEC_X0), ("l0", SPEC_L0), ("l1", SPEC_L1),
                          ("l2", SPEC_L2), ("l3", SPEC_L3)):
            lay[key] = pack_layout(spec)

        ks_region = sb("ks_region", [128, 16384])
        r32 = sb("r32", [128, 8192])
        w32 = sb("w32", [128, 8192])
        pbuf = sb("pbuf", [128, 3, 1024])
        ctxT = sb("ctxT", [128, S])
        ctx1 = sb("ctx1", [128, NC, C + 1])
        qs = sb("qs", [128, H * T], BF16)
        with nc.sbuf_tensor("ctxR", [C, S], F32R) as ctxR, nc.sbuf_tensor("qkR", [C, H * T], F32R) as qkR:
            pass
        v3 = sb("v3", [128, NC, D])
        v1 = sb("v1", [128, NC, D])
        packs = {k: sb("pack_" + k, [128, lay[k][1]]) for k in ("ctx", "l0", "l1", "l2", "l3")}

        def w(key, name, rows=None):
            r, at, cols = lay[key][0][name]
            t = r32 if key == "x0" else packs[key]
            return t[0:r, at:at + cols]

        QK = r32[:, 8192 - 2048:8192]
        x = sb("x", [T, D])
        xn = sb("xn", [T, D])
        xnT = sb("xnT", [D, T])
        ident = sb("ident", [128, 128])
        identb = sb("identb", [128, 128], BF16)
        ones = sb("ones", [128, 128])
        c96 = sb("c96", [128, C])
        c256 = sb("c256", [128, 128])
        half64 = sb("half64", [128, 128])
        m16 = sb("m16", [128, H])
        m8 = sb("m8", [128, H])
        m4 = sb("m4", [128, 4])
        mh = sb("mh", [128, 2])
        eps = sb("eps", [128, 1])
        one = sb("one", [128, 1])
        st = sb("st", [128, 6])
        mv = sb("mv", [128, 2])
        lnv = sb("lnv", [128, 1])
        rstd = sb("rstd", [128, 1])
        nmx = sb("nmx", [128, C + H])
        nm = sb("nm", [128, H])
        pm = sb("pm", [128, 2 * H])
        nclamp = sb("nclamp", [128, 1])
        npart = sb("npart", [128, 3, H], BF16)
        rec = sb("rec", [128, H])
        qT = sb("qT", [128, 128])
        r1 = sb("r1", [128, 128])
        r2 = sb("r2", [128, 128])
        qpart = sb("qpart", [128, 3, 128], BF16)
        att = sb("att", [128, 128])
        attT = sb("attT", [128, 128])
        scr = pbuf[:, :, :].rearrange("p a b -> p (a b)")
        lw = sb("lw", [128, 72])
        lr = sb("lr", [128, 72])
        top = sb("top", [128, 8])
        top2 = sb("top2", [128, 8])
        sel = sb("sel", [128, 64])
        sm = sb("sm", [128, 64])
        sc1 = sb("sc1", [128, 1])
        sc2 = sb("sc2", [128, 1])
        gbias = sb("gbias", [128, 64])
        qsel = sb("qsel", [128, QH, PROD + 2 * 3 * HD + SHIFT], BF16)
        kq = sb("kq", [128, 128], BF16)
        kq32 = qT
        fbias = sb("fbias", [128, 128], BF16)
        sin = sb("sin", [128, 1])
        skk = sb("skk", [128, 1])
        inv_in = sb("inv_in", [128, 1])

        ps = ctx.enter_context(nc.psum_tensor("ps", [128, 4096], F32))

        def bank(i, n=1):
            return ps[:, 512 * i:512 * (i + n)]

        k_scr = nc.dram_tensor("k_scr", [2, 3, D, S], BF16, kind="Internal").ap()

        KS = ks_region[:, :].bitcast(BF16).rearrange("p (h s) -> p h s", h=H)
        QS = qs[:, :].rearrange("p (h q) -> p h q", h=H)

        block = ctx.enter_context(nc.Block())

        chain = {"dve": 0, "act": 0, "pool": 0}

        def dve_then(ins):
            chain["dve"] += 1
            ins.then_inc(sem("dve_step"), 1)
            nc.vector.wait_ge(sem("dve_step"), chain["dve"])

        def act_then(ins):
            chain["act"] += 1
            ins.then_inc(sem("act_step"), 1)
            nc.scalar.wait_ge(sem("act_step"), chain["act"])

        def pool_then(ins):
            chain["pool"] += 1
            ins.then_inc(sem("pool_step"), 1)
            nc.gpsimd.wait_ge(sem("pool_step"), chain["pool"])

        V, A, PE, G = nc.vector, nc.scalar, nc.tensor, nc.gpsimd

        def turned(k):
            return k + 1 - (k >= 6)

        def norm_dve(k):
            dve_then(V.bn_stats(st[:, :], x[:, :]))
            V.bn_aggr(mv[:, :], st[:, :]).then_inc(sem("ln_stats"), 1)
            V.wait_ge(sem("ln_stats"), k + 1)
            V.wait_ge(sem("ln_rstd"), k + 1)
            V.tensor_scalar(xn[:, :], x[:, :], mv[:, 0:1], rstd[:, :], ALU.subtract, ALU.mult)\
                .then_inc(sem("ln_xn"), 1)
            V.wait_ge(sem("ln_xn"), k + 1)
            if k == 6:
                return
            V.wait_ge(sem("ln_t"), turned(k))
            V.tensor_copy(xnT[:, :], bank(7)[:, 0:128]).then_inc(sem("ln_xnT"), 1)

        def norm_act(k):
            A.wait_ge(sem("ln_stats"), k + 1)
            act_then(A.activation(lnv[:, :], mv[:, 1:2], ACT.Ln, bias=eps[:, :]))
            A.activation(rstd[:, :], lnv[:, :], ACT.Exp, scale=-0.5).then_inc(sem("ln_rstd"), 1)

        def norm_pe(k):
            PE.wait_ge(sem("ln_xn"), k + 1)
            PE.transpose(bank(7)[:, 0:128], xn[:, :], ident[:, :]).then_inc(sem("ln_t"), 1)
            PE.wait_ge(sem("ln_xnT"), turned(k))

        def top_k(n, k, dst):
            width = n + 8 - k
            dve_then(V.memset(lw[:, n:width], SENT))
            dve_then(V.max(top[:, :], lw[:, 0:width]))
            dve_then(V.memset(top2[:, :], SENT))
            dve_then(V.tensor_copy(top2[:, 0:k], top[:, 0:k]))
            dve_then(V.match_replace(lr[:, 0:width], top2[:, :], lw[:, 0:width], TAKEN))
            dve_then(V.tensor_tensor(dst, lr[:, 0:n], lw[:, 0:n], ALU.not_equal))

        def split_dve(src, t1, t2, part):
            dve_then(V.tensor_copy(part(0), src))
            dve_then(V.tensor_tensor(t1, src, part(0), ALU.subtract))
            dve_then(V.tensor_copy(part(1), t1))
            dve_then(V.tensor_tensor(t2, t1, part(1), ALU.subtract))

        def load(eng, dst, src, group):
            eng.dma_start(dst, src).then_inc(sem("d_" + group), 16)

        kreg = [w32, r32]
        kb = [4, 0]

        def kv_views(n):
            t = kreg[n]
            kt = t[:, 0:2048]
            res = t[:, 2048:4096]
            parts = t[:, 4096:7168].bitcast(BF16).rearrange("p (i s) -> p i s", i=3)
            return kt, res, parts

        def keys_pe(n, chunks=range(4)):
            wk = w("ctx", "wk1") if n == 0 else w("l3", "wk")
            for j in chunks:
                mm = PE.matmul(bank(kb[n] + j), wk, ctxT[0:C, 512 * j:512 * j + 512], start=True, stop=True)
            if 3 in chunks:
                mm.then_inc(sem("k_mm"), 1)

        def values_pe(n, first, chunks=range(NC)):
            wv = w("ctx", "wv1") if n == 0 else w("l3", "wv")
            for i, c in enumerate(chunks):
                mm = PE.matmul(ps[:, 512 * first + 128 * i:512 * first + 128 * i + 128],
                               ctxT[0:C, 128 * c:128 * c + 128], wv, start=True, stop=True)
            mm.then_inc(sem("v_mm"), 1)

        V3_PARTS = (range(12, NC), range(0, 12))

        def values3_act(part, first):
            A.wait_ge(sem("v_mm"), 2 + part)
            c = V3_PARTS[part]
            A.activation(v3[:, c[0]:c[-1] + 1, :].rearrange("p c d -> p (c d)"),
                         ps[:, 512 * first:512 * first + 128 * len(c)], ACT.Copy).then_inc(sem("v_ev"), 1)

        def keys_act(n):
            kt, _, _ = kv_views(n)
            A.wait_ge(sem("k_mm"), n + 1)
            if n == 0:
                A.activation(kt, bank(4, 4), ACT.Identity, bias=w("ctx", "bk1")).then_inc(sem("k_ev"), 1)

        def split_keys_pool(n):
            kt, res, parts = kv_views(n)
            G.wait_ge(sem("k_ev"), n + 1)
            pool_then(G.tensor_copy(parts[:, 0, :], kt))
            pool_then(G.tensor_tensor(res, kt, parts[:, 0, :], ALU.subtract))
            pool_then(G.tensor_copy(parts[:, 1, :], res))
            pool_then(G.tensor_tensor(kt, res, parts[:, 1, :], ALU.subtract))
            G.tensor_copy(parts[:, 2, :], kt).then_inc(sem("k_parts"), 1)

        def stack_keys_sync(n):
            _, _, parts = kv_views(n)
            sy = nc.sync
            sy.wait_ge(sem("k_parts"), n + 1)
            sy.dma_start(k_scr[n].rearrange("i p s -> p i s"), parts).then_inc(sem("d_kscr"), 16)
            sy.wait_ge(sem("d_kscr"), 16 * (n + 1))
            for r in range(9):
                src = k_scr[n, r % 3].rearrange("(h d) s -> d h s", h=H)
                if n == 1 and r == 0:
                    sy.wait_ge(sem("x2_done"), 1)
                sy.dma_start(KS[SHIFT + HD * r:SHIFT + HD * (r + 1), :, :], src).then_inc(sem("d_ks"), 16)

        def stack_queries_pe(n, j):
            PE.wait_ge(sem("q_parts"), n + 1)
            rows = slice(32 * j, 32 * j + 32)
            for hh in range(QH):
                for i in range(3):
                    at = 2 * 3 * HD - 3 * HD * i
                    mm = PE.matmul(bank(j)[0:KROWS, 128 * hh:128 * hh + 128], qsel[rows, hh, at:at + KROWS],
                                   qpart[rows, i, :], start=(i == 0), stop=(i == 2), tile_position=(32 * j, 0))
            mm.then_inc(sem("q_stack"), 1)

        def stack_queries_act(n):
            for j in range(4):
                A.wait_ge(sem("q_stack"), 4 * n + j + 1)
                A.activation(qs[0:KROWS, 512 * j:512 * j + 512], bank(j)[0:KROWS, :], ACT.Copy)\
                    .then_inc(sem("qs"), 1)

        def selection_dve():
            dve_then(V.memset(qsel[:, :, :], 0.0))
            for r in range(3):
                at = SHIFT + 2 * 3 * HD + HD * r
                dve_then(V.tensor_reduce(qsel[:, :, at:at + HD],
                                         identb[:, :].rearrange("p (g j d) -> p j d g", g=4, j=QH), AX.X, ALU.max))

        NA, NB = 32, 64

        PBUFS = 4
        P = [scr[:, 512 * i:512 * i + 512] for i in range(PBUFS)]
        num, den = scr[:, 2048:2560], scr[:, 2560:3072]
        E = v3[:, :, :].rearrange("p c d -> p (c d)")

        def max_unit_pe(k, a):
            h, half = a // 2, a % 2
            if a >= 2:
                PE.wait_ge(sem("at_max"), NA * k + a - 1)
            if a % 8 == 0 and a:
                PE.wait_ge(sem("at_shift"), 4 * k + a // 8)
                if k == 1:
                    PE.wait_ge(sem("at_clipE"), a // 8)
            rows = KROWS + (k == 2)
            for j in range(2):
                key = 1024 * half + 512 * j
                out_ = bank(4 + 2 * (a % 2) + j)
                if k == 0:
                    mm = PE.matmul(out_, qkR[:, 128 * h:128 * h + 128], ctxR[:, key:key + 512], start=True, stop=True)
                else:
                    mm = PE.matmul(out_, QS[0:rows, h, :], KS[0:rows, h, key:key + 512], start=True, stop=True)
            mm.then_inc(sem("at_a"), 1)

        def shift_pe(k, g):
            PE.wait_ge(sem("at_neg"), 4 * k + g + 1)
            if k == 0:
                PE.transpose(bank(4)[0:C + H, 0:128], nmx[:, :], ident[:, :]).then_inc(sem("at_negT"), 1)
            else:
                PE.transpose(bank(4).bitcast(BF16)[0:SHIFT, 0:128], npart[:, :, :].rearrange("p i h -> p (i h)"),
                             identb[:, :]).then_inc(sem("at_negT"), 1)

        def clip_bound_pe(g):
            PE.wait_ge(sem("at_shift"), 4 + g + 1)
            PE.matmul(bank(5), KS[0:SHIFT, 0, 0:128], qs[0:SHIFT, 512 * g:512 * g + 512], start=True, stop=True)\
                .then_inc(sem("at_clipM"), 1)

        def scores_pe(k, b):
            g, c = b // NC, b % NC
            if c == 0:
                PE.wait_ge(sem("at_shift"), 4 * k + g + 1)
            if b >= 2:
                if k == 1:
                    PE.wait_ge(sem("at_clip"), b - 1)
                else:
                    PE.wait_ge(sem("at_exp"), NB * k + b - 1)
            if k == 0:
                mm = PE.matmul(bank(2 + b % 2), ctxT[0:C + H, 128 * c:128 * c + 128],
                               QK[0:C + H, 512 * g:512 * g + 512], start=True, stop=True)
            else:
                rows = KROWS + (k == 2)
                for hh in range(QH):
                    h = QH * g + hh
                    mm = PE.matmul(bank(2 + b % 2)[:, 128 * hh:128 * hh + 128],
                                   KS[0:rows, h, 128 * c:128 * c + 128], QS[0:rows, h, :], start=True, stop=True)
            mm.then_inc(sem("at_k"), 1)

        def products_pe(k, b):
            g, c = b // NC, b % NC
            PE.wait_ge(sem("at_exp"), NB * k + b + 1)
            if c == 0 and g >= 2:
                PE.wait_ge(sem("at_o"), 4 * k + g - 1)
            p, acc = P[b % PBUFS], bank(g % 2)
            if k == 0:
                for hh in range(QH):
                    mm = PE.matmul(acc[:, 97 * hh:97 * hh + 97], p[:, 128 * hh:128 * hh + 128], ctx1[:, c, :],
                                   start=(c == 0 and hh == 0), stop=(c == NC - 1), skip_group_check=True)
            else:
                v = v1 if k == 1 else v3
                for t in range(4):
                    mm = PE.matmul(acc[32 * t:32 * t + 32, 0:256],
                                   v[:, c, 32 * g:32 * g + 32] if t < 2 else ones[:, 0:32],
                                   p[:, 256 * (t % 2):256 * (t % 2) + 256], start=(c == 0), stop=(c == NC - 1),
                                   tile_position=(0, 32 * t), skip_group_check=True)
            mm.then_inc(sem("at_pv"), 1)

        def core_pe(k, extra):
            for a in range(8):
                if k and a % 2 == 0:
                    stack_queries_pe(k - 1, a // 2)
                if k and a == 0:
                    PE.wait_ge(sem("qs"), 4 * (k - 1) + 1)
                max_unit_pe(k, a)
            if k:
                PE.wait_ge(sem("qs"), 4 * k)
            shift_pe(k, 0)
            if k == 1:
                clip_bound_pe(0)
            scores_pe(k, 0)
            scores_pe(k, 1)
            for b in range(NB):
                g, c = b // NC, b % NC
                if b + 2 < NB:
                    scores_pe(k, b + 2)
                if c == 0 and g == 0 and k == 1:
                    PE.wait_ge(sem("v_ev"), 1)
                if c == 0 and g == 0 and k == 2:
                    PE.wait_ge(sem("v_ev"), 3)
                if g < 3 and c < 8:
                    max_unit_pe(k, 8 * (g + 1) + c)
                products_pe(k, b)
                if g < 3 and c == 9:
                    shift_pe(k, g + 1)
                if g < 3 and c == 11 and k == 1:
                    clip_bound_pe(g + 1)
                extra(g, c)

        def core_act(k):
            def clip_bound(g):
                A.wait_ge(sem("at_clipM"), g + 1)
                A.activation(E[:, 512 * g:512 * g + 512], bank(5), ACT.Identity, bias=nclamp[:, :])\
                    .then_inc(sem("at_clipE"), 1)

            if k == 1:
                clip_bound(0)
            for b in range(NB):
                g, c = b // NC, b % NC
                p = P[b % PBUFS]
                if k == 1:
                    A.wait_ge(sem("at_clip"), b + 1)
                    A.activation(p, p, ACT.Exp).then_inc(sem("at_exp"), 1)
                    if g < 3 and c == 12:
                        clip_bound(g + 1)
                else:
                    A.wait_ge(sem("at_k"), NB * k + b + 1)
                    if b >= PBUFS:
                        A.wait_ge(sem("at_pv"), NB * k + b - PBUFS + 1)
                    A.activation(p, bank(2 + b % 2), ACT.Exp).then_inc(sem("at_exp"), 1)

        def core_dve(k, extra):
            def reduce_max(a):
                V.wait_ge(sem("at_a"), NA * k + a + 1)
                V.tensor_reduce(pm[:, a:a + 1], bank(4 + 2 * (a % 2), 2), AX.X, ALU.max, negate=True)\
                    .then_inc(sem("at_max"), 1)

            def negated(g):
                V.wait_ge(sem("at_max"), NA * k + 8 * (g + 1))
                pairs = pm[:, 8 * g:8 * g + 8].rearrange("p (h i) -> p h i", i=2)
                q = slice(QH * g, QH * g + QH)
                if k == 0:
                    V.tensor_reduce(nmx[:, C + QH * g:C + QH * g + QH], pairs, AX.X, ALU.min)\
                        .then_inc(sem("at_neg"), 1)
                    return
                dve_then(V.tensor_reduce(nm[:, q], pairs, AX.X, ALU.min))
                if k == 1:
                    dve_then(V.tensor_scalar(nm[:, q], nm[:, q], CLAMP, -CLAMP, ALU.min, ALU.max))
                split_dve(nm[:, q], r1[:, 0:QH], r2[:, 0:QH], lambda i: npart[:, i, q])
                V.tensor_copy(npart[:, 2, q], r2[:, 0:QH]).then_inc(sem("at_neg"), 1)

            def shift(g):
                V.wait_ge(sem("at_negT"), 4 * k + g + 1)
                lo, n = (C, H) if k == 0 else (0, SHIFT)
                src = bank(4) if k == 0 else bank(4).bitcast(BF16)
                dst = QK[:, 512 * g:512 * g + 512].rearrange("p (h q) -> p h q", h=QH) if k == 0 \
                    else QS[:, QH * g:QH * g + QH, :]
                V.tensor_tensor(dst[lo:lo + n, :, :],
                                src[lo:lo + n, 0:128].unsqueeze(1).to_broadcast([n, QH, 128]),
                                m16[lo:lo + n, QH * g:QH * g + QH].unsqueeze(2).to_broadcast([n, QH, 128]),
                                ALU.mult).then_inc(sem("at_shift"), 1)

            def clip(b):
                V.wait_ge(sem("at_k"), NB * k + b + 1)
                if b >= PBUFS:
                    V.wait_ge(sem("at_pv"), NB * k + b - PBUFS + 1)
                if b % NC == 0:
                    V.wait_ge(sem("at_clipE"), b // NC + 1)
                V.scalar_tensor_tensor(P[b % PBUFS], bank(2 + b % 2), 0.0,
                                       E[:, 512 * (b // NC):512 * (b // NC) + 512], ALU.min, ALU.max)\
                    .then_inc(sem("at_clip"), 1)

            def results(g):
                V.wait_ge(sem("at_pv"), NB * k + NC * (g + 1))
                acc = bank(g % 2)
                if k == 0:
                    o = acc[:, 0:388].rearrange("p (h c) -> p h c", h=QH)
                    dve_then(V.reciprocal(rec[:, QH * g:QH * g + QH], o[:, :, C]))
                    V.tensor_tensor(o0[:, QH * g:QH * g + QH, :], o[:, :, 0:C],
                                    rec[:, QH * g:QH * g + QH].unsqueeze(2).to_broadcast([128, QH, C]), ALU.mult)\
                        .then_inc(sem("at_o"), 1)
                    return
                gr = slice(32 * g, 32 * g + 32)
                for t in range(4):
                    dst = num if t < 2 else den
                    i = V.tensor_tensor(dst[gr, 256 * (t % 2):256 * (t % 2) + 256].rearrange("p (j q) -> p j q", j=2),
                                        acc[32 * t:32 * t + 32, 0:256].rearrange("p (j q) -> p j q", j=2),
                                        m4[gr, 2 * (t % 2):2 * (t % 2) + 2].unsqueeze(2).to_broadcast([32, 2, 128]),
                                        ALU.mult)
                i.then_inc(sem("at_o"), 1)

            for a in range(8):
                reduce_max(a)
            negated(0)
            shift(0)
            if k == 1:
                clip(0)
            for b in range(NB):
                g, c = b // NC, b % NC
                if k == 1 and b + 1 < NB:
                    clip(b + 1)
                if g < 3 and c < 8:
                    reduce_max(8 * (g + 1) + c)
                if g < 3 and c == 8:
                    negated(g + 1)
                if g < 3 and c == 10:
                    shift(g + 1)
                if c == 4 and g:
                    results(g - 1)
                extra(g, c)
            results(3)

        def nothing(g, c):
            pass

        def narrow_pe(n):
            key = "l1" if n == 0 else "l3"
            PE.matmul(bank(4)[:, 0:128], w(key, "wq"), xnT[:, :], start=True, stop=True)\
                .then_inc(sem("nq_mm"), 1)
            PE.wait_ge(sem("d_ks"), 16 * 9 * (n + 1))
            PE.wait_ge(sem("ks_ones"), n + 1)
            if n == 1:
                PE.wait_ge(sem("d_mask3"), 32)
            core_pe(n + 1, nothing)
            PE.wait_ge(sem("n_att"), n + 1)
            mm = PE.matmul(bank(2)[:, 0:128], attT[:, :], w(key, "wo"), start=True, stop=(n == 1))
            if n == 0:
                mm = PE.matmul(bank(2)[:, 0:128], ones[0:1, :], w(key, "bo"), start=False, stop=True)
            mm.then_inc(sem("n_out"), 1)

        def narrow_act(n):
            stack_queries_act(n)
            core_act(n + 1)

        def narrow_dve(n):
            key = "l1" if n == 0 else "l3"
            V.wait_ge(sem("nq_mm"), n + 1)
            if n == 0:
                dve_then(V.tensor_scalar(qT[:, :], bank(4)[:, 0:128], w(key, "bq"), HD ** -0.5, ALU.add, ALU.mult))
            else:
                dve_then(V.tensor_scalar(qT[:, :], bank(4)[:, 0:128], HD ** -0.5, None, ALU.mult))
            split_dve(qT[:, :], r1[:, :], r2[:, :], lambda i: qpart[:, i, :])
            V.tensor_copy(qpart[:, 2, :], r2[:, :]).then_inc(sem("q_parts"), 1)
            core_dve(n + 1, nothing)
            V.wait_ge(sem("at_o"), 4 * (n + 2))
            dve_then(V.tensor_reduce(r1[:, :], den.rearrange("p (j q) -> p q j", j=4), AX.X, ALU.add))
            dve_then(V.reciprocal(r1[:, :], r1[:, :]))
            dve_then(V.tensor_reduce(att[:, :], num.rearrange("p (j q) -> p q j", j=4), AX.X, ALU.add))
            if n == 0:
                dve_then(V.tensor_tensor(att[:, :], att[:, :], r1[:, :], ALU.mult))
                V.tensor_scalar(attT[:, :], att[:, :], w(key, "bv"), None, ALU.add).then_inc(sem("n_att"), 1)
            else:
                V.tensor_tensor(attT[:, :], att[:, :], r1[:, :], ALU.mult).then_inc(sem("n_att"), 1)
            V.wait_ge(sem("n_out"), n + 1)
            dve_then(V.tensor_tensor(x[:, :], bank(2)[:, 0:128], x[:, :], ALU.add))

        wkT = w("x0", "wkT").rearrange("p (h c) -> p h c", h=H)
        wv0 = w("x0", "wv").rearrange("p (h d) -> p h d", h=H)
        wo0 = w("x0", "wo").rearrange("p (h d) -> p h d", h=H)
        q0T = scr[0:DH0, 0:2048]
        o0 = v1[:, :, :].rearrange("p c d -> p (c d)")[:, 0:H * C].rearrange("p (h c) -> p h c", h=H)
        oT = QK[0:C, :].rearrange("p (h q) -> p h q", h=H)
        vT = v3[0:DH0, :, :]
        x0_bank_T, x0_bank_W = (4, 5, 6, 7), (7, 4, 5, 4)

        def x0_turn_pe(g):
            if g == 0:
                PE.wait_ge(sem("at_max"), NA)
            PE.wait_ge(sem("at_o"), g + 1)
            if g == 3:
                PE.wait_ge(sem("x0_vTe"), 1)
            for h in range(QH * g, QH * g + QH):
                mm = PE.transpose(bank(x0_bank_T[g])[0:C, 128 * (h % 4):128 * (h % 4) + 128], o0[:, h, :], ident[:, :])
            mm.then_inc(sem("x0_oT"), 1)

        def x0_values_pe(g):
            PE.wait_ge(sem("x0_oTe"), g + 1)
            if g == 3:
                PE.wait_ge(sem("x0_vTe"), 2)
            for h in range(QH * g, QH * g + QH):
                mm = PE.matmul(bank(x0_bank_W[g])[0:DH0, 128 * (h % 4):128 * (h % 4) + 128], wv0[:, h, :],
                               oT[:, h, :], start=True, stop=True)
            mm.then_inc(sem("x0_vT"), 1)

        def x0_out_pe(g):
            PE.wait_ge(sem("x0_vTe"), g + 1)
            if g == 0:
                PE.wait_ge(sem("x0_oTe"), 3)
            for h in range(QH * g, QH * g + QH):
                PE.matmul(bank(6)[:, 0:128], vT[:, h, :], wo0[:, h, :], start=(h == 0), stop=False,
                          skip_group_check=True)

        def x0_extra_pe(g, c):
            if g == 3 and c in (1, 3, 5):
                x0_turn_pe((c - 1) // 2)
            if g == 3 and c in (7, 9, 11):
                x0_values_pe((c - 7) // 2)
            if g == 3 and c in (13, 14, 15):
                x0_out_pe(c - 13)

        def x0_pe():
            PE.wait_ge(sem("d_x0"), 16)
            for h in range(H):
                mm = PE.matmul(bank(h // 4)[0:DH0, 128 * (h % 4):128 * (h % 4) + 128],
                               w("x0", "wq")[:, DH0 * h:DH0 * h + DH0], xnT[:, :], start=True, stop=True)
                if h % 4 == 3:
                    mm.then_inc(sem("x0_q"), 1)
            PE.wait_ge(sem("k_ev"), 1)
            for h in range(H):
                if h % 4 == 0:
                    PE.wait_ge(sem("x0_qe"), h // 4 + 1)
                mm = PE.matmul(bank(4 + h // 4)[0:C, 128 * (h % 4):128 * (h % 4) + 128], wkT[:, h, :],
                               q0T[:, 128 * h:128 * h + 128], start=True, stop=True)
                if h % 4 == 3:
                    mm.then_inc(sem("x0_qk"), 1)
            PE.wait_ge(sem("x0_qkR"), 4)
            PE.wait_ge(sem("ctxR"), 1)
            PE.wait_ge(sem("d_ctx1"), 16)
            core_pe(0, x0_extra_pe)
            x0_turn_pe(3)
            x0_values_pe(3)
            x0_out_pe(3)
            PE.matmul(bank(6)[:, 0:128], ones[0:1, :], w("x0", "bo"), start=False, stop=True,
                      skip_group_check=True).then_inc(sem("x0_out"), 1)

        def x0_act():
            for g in range(4):
                A.wait_ge(sem("x0_qk"), g + 1)
                A.activation(QK[0:C, 512 * g:512 * g + 512], bank(4 + g)[0:C, :], ACT.Copy)\
                    .then_inc(sem("x0_qact"), 1)
            core_act(0)

        def x0_extra_dve(g, c):
            if g == 1 and c == 12:
                fp8_weights_dve()
            if g == 3 and c in (6, 8, 10):
                x0_turn_dve((c - 6) // 2)
            if g == 3 and c in (11, 13, 15):
                x0_values_dve((c - 11) // 2)

        def x0_turn_dve(g):
            V.wait_ge(sem("x0_oT"), g + 1)
            V.tensor_copy(oT[:, 4 * g:4 * g + 4, :].rearrange("p h q -> p (h q)"), bank(x0_bank_T[g])[0:C, :])\
                .then_inc(sem("x0_oTe"), 1)

        def x0_values_dve(g):
            V.wait_ge(sem("x0_vT"), g + 1)
            V.tensor_copy(vT[:, 4 * g:4 * g + 4, :].rearrange("p h q -> p (h q)"), bank(x0_bank_W[g])[0:DH0, :])\
                .then_inc(sem("x0_vTe"), 1)

        def x0_dve():
            for g in range(4):
                V.wait_ge(sem("x0_q"), g + 1)
                V.tensor_scalar(q0T[:, 512 * g:512 * g + 512], bank(g)[0:DH0, :], DH0 ** -0.5, None, ALU.mult)\
                    .then_inc(sem("x0_qe"), 1)
            for g in range(4):
                V.wait_ge(sem("x0_qact"), g + 1)
                V.tensor_copy(qkR[:, 512 * g:512 * g + 512], bank(4 + g)[0:C, :]).then_inc(sem("x0_qkR"), 1)
            core_dve(0, x0_extra_dve)
            x0_turn_dve(3)
            x0_values_dve(3)
            V.wait_ge(sem("x0_out"), 1)
            dve_then(V.tensor_tensor(x[:, :], bank(6)[:, 0:128], x[:, :], ALU.add))

        sc = {"a": pbuf[0:32, 1, 0:T], "h": pbuf[0:32, 1, T:2 * T]}
        nwab = sb("nwab", [32, 1])

        def rec_pe():
            PE.wait_ge(sem("d_l0"), 16)
            PE.matmul(bank(0)[0:32, 0:128], w("l0", "waT"), xnT[:, :], start=True, stop=True)\
                .then_inc(sem("rec_mm"), 1)
            PE.matmul(bank(1)[0:32, 0:128], w("l0", "bT"), xnT[:, :], start=True, stop=True)\
                .then_inc(sem("rec_mm"), 1)
            values_pe(0, 3)
            PE.wait_ge(sem("rec_h"), 1)
            PE.matmul(bank(2)[:, 0:128], sc["h"][:, :], w("l0", "cT"), start=True, stop=False)
            PE.matmul(bank(2)[:, 0:128], xnT[:, :], w("l0", "dT"), start=False, stop=True)\
                .then_inc(sem("rec_mm"), 1)

        def rec_act():
            A.wait_ge(sem("rec_mm"), 1)
            A.wait_ge(sem("rec_nb"), 1)
            A.activation(sc["a"][:, :], bank(0)[0:32, 0:128], ACT.Exp, bias=nwab[:, :], scale=-1.0)\
                .then_inc(sem("rec_e"), 1)
            A.wait_ge(sem("v_mm"), 1)
            A.activation(v1[:, :, :].rearrange("p c d -> p (c d)"), bank(3, 4), ACT.Copy).then_inc(sem("v_ev"), 1)

        def rec_dve():
            V.wait_ge(sem("d_l0"), 16)
            V.tensor_scalar(nwab[:, :], w("l0", "wab"), -1.0, None, ALU.mult).then_inc(sem("rec_nb"), 1)
            V.wait_ge(sem("rec_e"), 1)
            dve_then(V.tensor_scalar(sc["a"][:, :], sc["a"][:, :], 1.0, None, ALU.add))
            dve_then(V.reciprocal(sc["a"][:, :], sc["a"][:, :]))
            V.wait_ge(sem("rec_mm"), 2)
            V.tensor_tensor_scan(sc["h"][:, :], sc["a"][:, :], bank(1)[0:32, 0:128], 0.0, ALU.mult, ALU.add)\
                .then_inc(sem("rec_h"), 1)
            V.wait_ge(sem("rec_mm"), 3)
            dve_then(V.tensor_tensor(x[:, :], bank(2)[:, 0:128], x[:, :], ALU.add))

        w1_0 = w32[:, 0:4096].rearrange("p (e f) -> p e f", e=8)
        w2_0 = w32[:, 4096:8192].rearrange("p (e c n) -> p e c n", e=8, c=4)
        hid = [pbuf[:, 0, 0:512], pbuf[:, 0, 512:1024]]
        selT = pbuf[0:8, 1, 0:T]

        def moe0_pe():
            PE.wait_ge(sem("v_ev"), 1)
            PE.matmul(bank(6)[:, 0:8], xnT[:, :], w("l0", "gw"), start=True, stop=False)
            PE.matmul(bank(6)[:, 0:8], ones[0:1, :], w("l0", "gb"), start=False, stop=True)\
                .then_inc(sem("m0_gate"), 1)
            PE.wait_ge(sem("d_w12"), 32)

            def up(e):
                if e >= 2:
                    PE.wait_ge(sem("m0_relu"), e - 1)
                for c in range(4):
                    mm = PE.matmul(bank(e % 2)[:, 128 * c:128 * c + 128], w1_0[:, e, 128 * c:128 * c + 128],
                                   xnT[:, :], start=True, stop=True)
                mm.then_inc(sem("m0_up"), 1)

            def down(e):
                PE.wait_ge(sem("m0_relu"), e + 1)
                if e >= 2:
                    PE.wait_ge(sem("m0_acc"), e - 1)
                for c in range(4):
                    mm = PE.matmul(bank(2 + e % 2)[:, 0:128], hid[e % 2][:, 128 * c:128 * c + 128],
                                   w2_0[:, e, c, :], start=(c == 0), stop=(c == 3))
                mm.then_inc(sem("m0_down"), 1)

            up(0)
            for e in range(8):
                if e + 1 < 8:
                    up(e + 1)
                down(e)
            PE.wait_ge(sem("m0_sel"), 1)
            PE.transpose(bank(4)[0:8, 0:128], sel[:, 0:8], ident[:, :]).then_inc(sem("m0_selT"), 1)
            PE.wait_ge(sem("m0_selTe"), 1)
            PE.matmul(bank(5)[:, 0:128], selT[:, :], w("l0", "b2"), start=True, stop=True)\
                .then_inc(sem("m0_selT"), 1)

        def moe0_act():
            for e in range(8):
                A.wait_ge(sem("m0_up"), e + 1)
                if e >= 2:
                    A.wait_ge(sem("m0_down"), e - 1)
                for c in range(4):
                    i = A.activation(hid[e % 2][:, 128 * c:128 * c + 128], bank(e % 2)[:, 128 * c:128 * c + 128],
                                     ACT.Relu, bias=w("l0", "b1")[:, 4 * e + c:4 * e + c + 1])
                i.then_inc(sem("m0_relu"), 1)

        def moe0_dve():
            V.wait_ge(sem("m0_gate"), 1)
            dve_then(V.tensor_copy(lw[:, 0:8], bank(6)[:, 0:8]))
            top_k(8, 2, sel[:, 0:8])
            V.sem_inc(sem("m0_sel"), 1)
            for e in range(8):
                V.wait_ge(sem("m0_down"), e + 1)
                V.scalar_tensor_tensor(x[:, :], bank(2 + e % 2)[:, 0:128], sel[:, e:e + 1], x[:, :],
                                       ALU.mult, ALU.add).then_inc(sem("m0_acc"), 1)
                V.wait_ge(sem("m0_acc"), e + 1)
            V.wait_ge(sem("m0_selT"), 1)
            V.tensor_copy(selT[:, :], bank(4)[0:8, 0:128]).then_inc(sem("m0_selTe"), 1)
            V.wait_ge(sem("m0_selT"), 2)
            dve_then(V.tensor_tensor(x[:, :], bank(5)[:, 0:128], x[:, :], ALU.add))

        KR = ks_region
        dA = KR[:, 0:4096].rearrange("p (c n t) -> p c n t", c=2, n=16)
        xB = KR[:, 4096:8192].rearrange("p (c n t) -> p c n t", c=2, n=16)
        hs = KR[:, 8192:12288].rearrange("p (c n t) -> p c n t", c=2, n=16)
        bc = KR[0:48, 12288:12416]
        mamba = pbuf[:, :, :].rearrange("p a b -> p (a b)")

        def mw(i):
            return mamba[:, 256 * i:256 * i + 256]
        xc, sz, t1, t2, dt_, z_, y_, yc = (mw(i) for i in range(8))
        dtrep = mw(8)
        xpad = mamba[:, 2304:2304 + 2 * (T + 3)].rearrange("p (c t) -> p c t", c=2)
        negA = sb("negA", [128, 32])

        def c2(ap):
            return ap.rearrange("p (c t) -> p c t", c=2)

        def mamba_pe():
            for c in range(4):
                mm = PE.matmul(bank(0)[:, 128 * c:128 * c + 128], w("l1", "inT")[:, 128 * c:128 * c + 128],
                               xnT[:, :], start=True, stop=True)
            mm.then_inc(sem("mb_mm"), 1)
            PE.wait_ge(sem("mb_dve"), 1)
            xp = c2(w("l1", "xpT"))
            for c in range(2):
                mm = PE.matmul(bank(1)[:, 0:128], c2(dtrep)[:, c, :], c2(xc)[:, c, :], start=(c == 0), stop=(c == 1))
            mm.then_inc(sem("mb_mm"), 1)
            for c in range(2):
                PE.matmul(bank(2)[0:16, 0:128], xp[:, c, 1:17], c2(xc)[:, c, :], start=(c == 0), stop=(c == 1))
            for c in range(2):
                mm = PE.matmul(bank(3)[32:48, 0:128], xp[:, c, 17:33], c2(xc)[:, c, :], start=(c == 0),
                               stop=(c == 1), tile_position=(0, 32))
            mm.then_inc(sem("mb_mm"), 1)
            PE.wait_ge(sem("mb_dve"), 2)
            for n in range(16):
                for first, row in ((0, 0), (4, 32)):
                    mm = PE.matmul(bank(first + n // 4)[:, 128 * (n % 4):128 * (n % 4) + 128],
                                   ident[row:row + 16, row + n:row + n + 1].to_broadcast([16, 128]),
                                   bc[row:row + 16, :], start=True, stop=True, tile_position=(row, 0))
            mm.then_inc(sem("mb_mm"), 1)
            PE.wait_ge(sem("mb_dve"), 3)
            for c in range(2):
                mm = PE.matmul(bank(0)[:, 0:128], c256[:, :], c2(y_)[:, c, :], start=(c == 0), stop=(c == 1))
            mm.then_inc(sem("mb_mm"), 1)
            PE.wait_ge(sem("mb_dve"), 4)
            for c in range(2):
                mm = PE.matmul(bank(1)[:, 0:128], c256[:, :], c2(t1)[:, c, :], start=(c == 0), stop=(c == 1))
            mm.then_inc(sem("mb_mm"), 1)
            PE.wait_ge(sem("mb_dve"), 5)
            for c in range(2):
                mm = PE.matmul(bank(2)[:, 0:128], c2(yc)[:, c, :], w("l1", "outT")[:, 128 * c:128 * c + 128],
                               start=(c == 0), stop=(c == 1))
            mm.then_inc(sem("mb_mm"), 1)

        def sigmoid(dst, src, signal):
            act_then(A.activation(dst, src, ACT.Exp, scale=-1.0))
            act_then(A.activation(dst, dst, ACT.Ln, bias=one[:, :]))
            A.activation(dst, dst, ACT.Exp, scale=-1.0).then_inc(signal, 1)

        def mamba_act():
            A.wait_ge(sem("mb_mm"), 1)
            A.wait_ge(sem("mb_xin"), 1)
            A.activation(negA[:, :], w("l1", "alog"), ACT.Exp).then_inc(sem("mb_negA"), 1)
            sigmoid(sz, bank(0)[:, 256:512], sem("mb_act"))
            A.wait_ge(sem("mb_conv"), 1)
            sigmoid(t1, xc, sem("mb_act"))
            A.wait_ge(sem("mb_conv"), 2)
            act_then(A.activation(t2, t1, ACT.Exp))
            A.activation(t2, t2, ACT.Ln, bias=one[:, :]).then_inc(sem("mb_act"), 1)
            A.wait_ge(sem("mb_conv"), 3)
            for c in range(2):
                for n in range(16):
                    i = A.activation(dA[:, c, n, :], c2(dt_)[:, c, :], ACT.Exp,
                                     scale=negA[:, 16 * c + n:16 * c + n + 1])
                i.then_inc(sem("mb_act"), 1)
            A.wait_ge(sem("mb_mm"), 6)
            act_then(A.activation(r1[:, :], bank(1)[:, 0:128], ACT.Ln, bias=eps[:, :]))
            A.activation(r1[:, :], r1[:, :], ACT.Exp, scale=-0.5).then_inc(sem("mb_act"), 1)

        def mamba_dve():
            cw, cb = w("l1", "convw"), w("l1", "convb")
            dve_then(V.memset(xpad[:, :, 0:3], 0.0))
            V.wait_ge(sem("mb_mm"), 1)
            V.tensor_copy(xpad[:, :, 3:T + 3], bank(0)[:, 0:256].rearrange("p (c t) -> p c t", c=2))\
                .then_inc(sem("mb_xin"), 1)
            V.wait_ge(sem("mb_xin"), 1)
            for c in range(2):
                dve_then(V.tensor_scalar(c2(xc)[:, c, :], xpad[:, c, 0:T], cw[:, 4 * c:4 * c + 1], cb[:, c:c + 1],
                                         ALU.mult, ALU.add))
                for k in range(1, 4):
                    dve_then(V.scalar_tensor_tensor(c2(xc)[:, c, :], xpad[:, c, k:k + T],
                                                    cw[:, 4 * c + k:4 * c + k + 1], c2(xc)[:, c, :],
                                                    ALU.mult, ALU.add))
            V.sem_inc(sem("mb_conv"), 1)
            V.wait_ge(sem("mb_act"), 1)
            dve_then(V.tensor_tensor(sz, bank(0)[:, 256:512], sz, ALU.mult))
            dve_then(V.tensor_copy(c2(dtrep), c2(w("l1", "xpT"))[:, :, 0:1].to_broadcast([128, 2, 128])))
            V.wait_ge(sem("mb_negA"), 1)
            dve_then(V.tensor_scalar(negA[:, :], negA[:, :], -1.0, None, ALU.mult))
            V.wait_ge(sem("mb_act"), 2)
            V.tensor_tensor(xc, xc, t1, ALU.mult).then_inc(sem("mb_dve"), 1)
            V.wait_ge(sem("mb_dve"), 1)
            V.wait_ge(sem("mb_mm"), 2)
            for c in range(2):
                dve_then(V.tensor_scalar(c2(z_)[:, c, :], bank(1)[:, 0:128], w("l1", "dtw")[:, c:c + 1],
                                         w("l1", "dtb")[:, c:c + 1], ALU.mult, ALU.add))
            dve_then(V.scalar_tensor_tensor(t1, z_, -1.0, z_, ALU.mult, ALU.min))
            V.sem_inc(sem("mb_conv"), 1)
            V.wait_ge(sem("mb_mm"), 3)
            dve_then(V.tensor_copy(bc[0:16, :], bank(2)[0:16, 0:128]))
            V.tensor_copy(bc[32:48, :], bank(3)[32:48, 0:128]).then_inc(sem("mb_dve"), 1)
            V.wait_ge(sem("mb_act"), 3)
            dve_then(V.scalar_tensor_tensor(dt_, z_, 0.0, t2, ALU.max, ALU.add))
            V.sem_inc(sem("mb_conv"), 1)
            dve_then(V.tensor_tensor(t1, xc, dt_, ALU.mult))
            V.wait_ge(sem("mb_mm"), 4)
            for c in range(2):
                dve_then(V.tensor_tensor(xB[:, c, :, :], bank(0, 4).rearrange("p (n t) -> p n t", n=16),
                                         c2(t1)[:, c, :].unsqueeze(1).to_broadcast([128, 16, T]), ALU.mult))
            for c in range(2):
                V.wait_ge(sem("mb_act"), 4 + c)
                dve_then(V.memset(dA[:, c, :, 0:1], 0.0))
                flat = [v[:, c, :, :].rearrange("p n t -> p (n t)") for v in (hs, dA, xB)]
                dve_then(V.tensor_tensor_scan(flat[0], flat[1], flat[2], 0.0, ALU.mult, ALU.add))
                dve_then(V.tensor_tensor(hs[:, c, :, :], bank(4, 4).rearrange("p (n t) -> p n t", n=16),
                                         hs[:, c, :, :], ALU.mult))
                dve_then(V.tensor_reduce(c2(y_)[:, c, :], hs[:, c, :, :].rearrange("p n t -> p t n"), AX.X, ALU.add))
                dve_then(V.scalar_tensor_tensor(c2(y_)[:, c, :], c2(xc)[:, c, :], w("l1", "dpar")[:, c:c + 1],
                                                c2(y_)[:, c, :], ALU.mult, ALU.add))
            V.sem_inc(sem("mb_dve"), 1)
            V.wait_ge(sem("mb_mm"), 5)
            dve_then(V.tensor_tensor(c2(yc), c2(y_), bank(0)[:, 0:128].unsqueeze(1).to_broadcast([128, 2, T]),
                                     ALU.subtract))
            V.tensor_tensor(t1, yc, yc, ALU.mult).then_inc(sem("mb_dve"), 1)
            V.wait_ge(sem("mb_act"), 6)
            dve_then(V.tensor_tensor(c2(yc), c2(yc), r1[:, :].unsqueeze(1).to_broadcast([128, 2, T]), ALU.mult))
            for c in range(2):
                dve_then(V.tensor_scalar(c2(yc)[:, c, :], c2(yc)[:, c, :], w("l1", "lng")[:, c:c + 1],
                                         w("l1", "lnb")[:, c:c + 1], ALU.mult, ALU.add))
            V.tensor_tensor(yc, yc, sz, ALU.mult).then_inc(sem("mb_dve"), 1)
            V.wait_ge(sem("mb_mm"), 7)
            dve_then(V.tensor_tensor(x[:, :], bank(2)[:, 0:128], x[:, :], ALU.add))

        egT, euT = r32[:, 0:4096], r32[:, 4096:8192]
        edT = w32[:, 0:4096].rearrange("p (m n) -> p m n", m=32)

        shared_e, shared_h = scr[:, 2048:2176], scr[:, 2176:2304]

        def moe1_pe():
            PE.matmul(bank(6)[:, 128:192], xnT[:, :], w("l1", "gateT"), start=True, stop=True)\
                .then_inc(sem("m1_gate"), 1)
            PE.matmul(bank(4)[:, 0:128], w("l1", "sgT"), xnT[:, :], start=True, stop=True)
            PE.matmul(bank(5)[:, 0:128], w("l1", "suT"), xnT[:, :], start=True, stop=True)\
                .then_inc(sem("m1_up"), 1)
            PE.wait_ge(sem("d_eg"), 48)

            def up(u):
                b = 2 * (u % 2)
                for t, wt in ((0, egT), (1, euT)):
                    for m in range(4 * u, 4 * u + 4):
                        mm = PE.matmul(bank(b + t)[:, 128 * (m % 4):128 * (m % 4) + 128], wt[:, 128 * m:128 * m + 128],
                                       xnT[:, :], start=True, stop=True)
                mm.then_inc(sem("m1_up"), 1)

            def down(u):
                PE.wait_ge(sem("m1_h"), u + 2)
                for m in range(4 * u, 4 * u + 4):
                    mm = PE.matmul(bank(6)[:, 0:128], scr[:, 1024 + 512 * (u % 2) + 128 * (m % 4):
                                                        1152 + 512 * (u % 2) + 128 * (m % 4)], edT[:, m, :],
                                   start=False, stop=(m == 31), skip_group_check=True)
                mm.then_inc(sem("m1_down"), 1)

            up(0)
            up(1)
            PE.wait_ge(sem("m1_comb"), 1)
            PE.transpose(bank(7)[:, 0:128], att[:, :], ident[:, :]).then_inc(sem("m1_combT"), 1)
            PE.wait_ge(sem("m1_h"), 1)
            PE.matmul(bank(6)[:, 0:128], shared_h, w("l1", "sdT"), start=True, stop=False,
                      skip_group_check=True)
            for u in range(8):
                if u >= 2:
                    PE.wait_ge(sem("m1_h"), u)
                    up(u)
                context_stats_pe(u)
                if u >= 1:
                    down(u - 1)
                context_keys_pe(u)
            down(7)

        def moe1_act():
            A.wait_ge(sem("m1_gate"), 1)
            A.activation(lr[:, 0:64], bank(6)[:, 128:192], ACT.Exp, scale=-1.0).then_inc(sem("m1_sig"), 1)
            A.wait_ge(sem("m1_up"), 1)
            sigmoid(shared_e, bank(4)[:, 0:128], sem("m1_sig"))
            for u in range(8):
                A.wait_ge(sem("m1_up"), u + 2)
                if u >= 2:
                    A.wait_ge(sem("m1_h"), u)
                sigmoid(scr[:, 512 * (u % 2):512 * (u % 2) + 512], bank(2 * (u % 2)), sem("m1_sig"))
                context_act(u)

        def moe1_dve():
            V.wait_ge(sem("m1_sig"), 1)
            V.wait_ge(sem("d_gb"), 16)
            dve_then(V.tensor_scalar(lr[:, 0:64], lr[:, 0:64], 1.0, None, ALU.add))
            dve_then(V.reciprocal(lr[:, 0:64], lr[:, 0:64]))
            dve_then(V.tensor_tensor(sm[:, :], lr[:, 0:64], gbias[:, :], ALU.add))
            dve_then(V.tensor_reduce(lw[:, 0:8], sm[:, :].rearrange("p (g e) -> p g e", g=8), AX.X, ALU.max))
            top_k(8, 4, sel[:, 0:8])
            dve_then(V.tensor_tensor(sm[:, :].rearrange("p (g e) -> p g e", g=8),
                                     sm[:, :].rearrange("p (g e) -> p g e", g=8),
                                     sel[:, 0:8].unsqueeze(2).to_broadcast([128, 8, 8]), ALU.mult))
            dve_then(V.tensor_copy(lw[:, 0:64], sm[:, :]))
            top_k(64, 6, sel[:, :])
            dve_then(V.tensor_tensor(sm[:, :], sm[:, :], sel[:, :], ALU.mult))
            dve_then(V.tensor_reduce(sc1[:, :], sm[:, :], AX.X, ALU.add))
            dve_then(V.tensor_scalar(sc1[:, :], sc1[:, :], 1e-8, None, ALU.add))
            dve_then(V.reciprocal(sc1[:, :], sc1[:, :]))
            V.tensor_scalar(att[:, :].rearrange("p (i e) -> p i e", i=2),
                            sm[:, :].unsqueeze(1).to_broadcast([128, 2, 64]), sc1[:, :], None, ALU.mult)\
                .then_inc(sem("m1_comb"), 1)
            V.wait_ge(sem("m1_combT"), 1)
            dve_then(V.tensor_copy(attT[:, :], bank(7)[:, 0:128]))
            V.wait_ge(sem("m1_sig"), 2)
            dve_then(V.tensor_tensor(shared_e, bank(4)[:, 0:128], shared_e, ALU.mult))
            V.tensor_tensor(shared_h, bank(5)[:, 0:128], shared_e, ALU.mult).then_inc(sem("m1_h"), 1)
            for u in range(8):
                b = 2 * (u % 2)
                e = scr[:, 512 * (u % 2):512 * (u % 2) + 512]
                context_first_dve(u)
                V.wait_ge(sem("m1_sig"), u + 3)
                dve_then(V.tensor_tensor(e, bank(b), e, ALU.mult))
                dve_then(V.tensor_tensor(e, bank(b + 1), e, ALU.mult))
                if u >= 2:
                    V.wait_ge(sem("m1_down"), u - 1)
                V.tensor_tensor(scr[:, 1024 + 512 * (u % 2):1536 + 512 * (u % 2)]
                                .rearrange("p (m t) -> p m t", m=4),
                                e.rearrange("p (m t) -> p m t", m=4),
                                attT[:, :].unsqueeze(1).to_broadcast([128, 4, T]), ALU.mult)\
                    .then_inc(sem("m1_h"), 1)
                context_rest_dve(u)
            V.wait_ge(sem("m1_down"), 8)
            dve_then(V.tensor_tensor(x[:, :], bank(6)[:, 0:128], x[:, :], ALU.add))

        KL = S + T
        KQ = KL + T
        kq2 = KR[:, 0:KQ]
        aux = KR[:, 2304:2304 + KQ]
        vv = KR[:, 4608:4608 + 17 * D].rearrange("p (c d) -> p c d", c=17)
        pp = KR[:, 6784:6784 + KL]
        ppT = KR[:, 8960:8960 + 17 * D].rearrange("p (c q) -> p c q", c=17)
        xcn = KR[0:C, 11136:13184]
        mrow = KR[0:1, 13184:13184 + KL // 2].bitcast(BF16)
        onesb = ones[0:1, :].bitcast(BF16).rearrange("p (n i) -> p n i", i=2)[:, :, 1]
        mask3u = KR[:, 15872:15872 + 512].bitcast(U8)
        sums = rec
        mrow8 = KR[0:1, 15360:15360 + 512].bitcast(U8)
        l2s = pbuf[:, :, :].rearrange("p a b -> p (a b)")
        lnT, qm = l2s[:, 0:128], l2s[:, 128:384].rearrange("p (h q) -> p h q", h=2)

        CJ = 4

        def chunk(j, n=512):
            return slice(512 * j, 512 * j + n)

        def context_stats_pe(u):
            if u < CJ:
                if u >= 3:
                    PE.wait_ge(sem("xa_key_out"), u - 2)
                elif u:
                    PE.wait_ge(sem("xa_centred"), u)
                PE.matmul(bank(4)[0:C, :], c96[0:C, :], ctxT[0:C, chunk(u)], start=True, stop=True)\
                    .then_inc(sem("xa_mean"), 1)
            j = u - 1
            if 0 <= j < CJ:
                PE.wait_ge(sem("xa_square"), j + 1)
                if j >= 2:
                    PE.wait_ge(sem("xa_value_out"), j - 1)
                elif j:
                    PE.wait_ge(sem("xa_rstd"), j)
                PE.matmul(bank(5)[0:C, :], c96[0:C, :], aux[0:C, chunk(j)], start=True, stop=True)\
                    .then_inc(sem("xa_var"), 1)

        def context_keys_pe(u):
            j = u - 2
            if 0 <= j < CJ:
                PE.wait_ge(sem("xa_ctx"), j + 1)
                PE.wait_ge(sem("xa_centred"), min(u + 1, CJ))
                if j:
                    PE.wait_ge(sem("xa_key_out"), j)
                PE.matmul(bank(4), w("l2", "wkvT")[:, 0:128], xcn[:, chunk(j)], start=True, stop=True)\
                    .then_inc(sem("xa_key"), 1)
                PE.wait_ge(sem("xa_rstd"), min(u, CJ))
                if j:
                    PE.wait_ge(sem("xa_value_out"), j)
                for c in range(4 * j, 4 * j + 4):
                    mm = PE.matmul(bank(5)[:, 128 * (c % 4):128 * (c % 4) + 128], xcn[:, 128 * c:128 * c + 128],
                                   w("l2", "wkvT")[:, 128:256], start=True, stop=True)
                mm.then_inc(sem("xa_value"), 1)
            j = u - 3
            if 0 <= j < CJ:
                PE.wait_ge(sem("xa_key_square"), j + 1)
                if j:
                    PE.wait_ge(sem("xa_clamped"), j)
                PE.matmul(bank(7), half64[:, :], aux[:, chunk(j)], start=True, stop=True)\
                    .then_inc(sem("xa_length"), 1)

        def context_act(u):
            if u < CJ:
                A.wait_ge(sem("xa_centred"), u + 1)
                A.activation(aux[0:C, chunk(u)], xcn[:, chunk(u)], ACT.Square).then_inc(sem("xa_square"), 1)
            j = u - 1
            if 0 <= j < CJ:
                A.wait_ge(sem("xa_var"), j + 1)
                act_then(A.activation(aux[0:C, chunk(j)], bank(5)[0:C, :], ACT.Ln, bias=eps[0:C, :]))
                A.activation(aux[0:C, chunk(j)], aux[0:C, chunk(j)], ACT.Exp, scale=-0.5)\
                    .then_inc(sem("xa_rstd"), 1)
            j = u - 2
            if 0 <= j < CJ:
                A.wait_ge(sem("xa_key"), j + 1)
                A.activation(kq2[:, chunk(j)], bank(4), ACT.Copy).then_inc(sem("xa_key_out"), 1)
                A.wait_ge(sem("xa_key_out"), j + 1)
                A.activation(aux[:, chunk(j)], kq2[:, chunk(j)], ACT.Square).then_inc(sem("xa_key_square"), 1)
            j = u - 3
            if 0 <= j < CJ:
                A.wait_ge(sem("xa_clamped"), j + 1)
                act_then(A.activation(aux[:, chunk(j)], aux[:, chunk(j)], ACT.Ln))
                A.activation(aux[:, chunk(j)], aux[:, chunk(j)], ACT.Exp, scale=-0.5)\
                    .then_inc(sem("xa_key_rstd"), 1)

        def context_first_dve(u):
            j = u - 4
            if 0 <= j < CJ:
                V.wait_ge(sem("xa_key_rstd"), j + 1)
                V.scalar_tensor_tensor(kq2[:, chunk(j)], kq2[:, chunk(j)], w("l2", "kng"), aux[:, chunk(j)],
                                       ALU.mult, ALU.mult)
            if u < CJ:
                V.wait_ge(sem("xa_mean"), u + 1)
                V.tensor_tensor(xcn[:, chunk(u)], ctxT[0:C, chunk(u)], bank(4)[0:C, :], ALU.subtract)\
                    .then_inc(sem("xa_centred"), 1)

        def context_rest_dve(u):
            j = u - 1
            if 0 <= j < CJ:
                V.wait_ge(sem("xa_rstd"), j + 1)
                dve_then(V.scalar_tensor_tensor(xcn[:, chunk(j)], xcn[:, chunk(j)], w("l2", "lxg"),
                                                aux[0:C, chunk(j)], ALU.mult, ALU.mult))
                V.tensor_scalar(xcn[:, chunk(j)], xcn[:, chunk(j)], w("l2", "lxb"), None, ALU.add)\
                    .then_inc(sem("xa_ctx"), 1)
            j = u - 2
            if 0 <= j < CJ:
                V.wait_ge(sem("xa_value"), j + 1)
                V.tensor_copy(vv[:, 4 * j:4 * j + 4, :].rearrange("p c d -> p (c d)"), bank(5))\
                    .then_inc(sem("xa_value_out"), 1)
            j = u - 3
            if 0 <= j < CJ:
                V.wait_ge(sem("xa_length"), j + 1)
                V.tensor_scalar(aux[:, chunk(j)], bank(7), 1e-16, None, ALU.max).then_inc(sem("xa_clamped"), 1)

        SJ = 5

        def x2_scores_pe(h, j):
            n = min(512, KL - 512 * j)
            PE.matmul(bank(j)[:, 0:n], qm[:, h, :], kq2[:, chunk(j, n)], start=True, stop=False)
            return PE.matmul(bank(j)[:, 0:n], onesb, mrow[:, chunk(j, n)], start=False, stop=True)

        def x2_turn_pe(h, i):
            PE.wait_ge(sem("x2_exp"), SJ * h + i + 1)
            if i >= 2 or h == 1:
                PE.wait_ge(sem("x2_te"), SJ * h + i - 1)
            if h == 1 and i == 1:
                PE.wait_ge(sem("x2_te"), SJ)
            for c in range(4 * i, min(4 * i + 4, 17)):
                mm = PE.transpose(bank(5 + i % 2)[:, 128 * (c % 4):128 * (c % 4) + 128],
                                  pp[:, 128 * c:128 * c + 128], ident[:, :])
            mm.then_inc(sem("x2_t"), 1)

        def x2_products_pe(h):
            for c in range(17):
                if c % 4 == 0:
                    PE.wait_ge(sem("x2_te"), SJ * h + c // 4 + 1)
                mm = PE.matmul(bank(7)[:, 128 * h:128 * h + 128], ppT[:, c, :], vv[:, c, :],
                               start=(c == 0), stop=(c == 16))
            mm.then_inc(sem("x2_mm"), 1)

        def x2_pe():
            keys_pe(1, (0, 1))
            PE.wait_ge(sem("x2_dve"), 1)
            PE.transpose(bank(4)[:, 0:128], att[:, :], ident[:, :]).then_inc(sem("x2_mm"), 1)
            keys_pe(1, (2,))
            PE.wait_ge(sem("x2_dve"), 2)
            PE.matmul(bank(4)[:, 128:256], w("l2", "wlT")[:, 0:128], lnT, start=True, stop=True)
            PE.matmul(bank(4)[:, 256:384], w("l2", "wqT"), lnT, start=True, stop=True)
            PE.matmul(bank(4)[:, 384:512], lnT, w("l2", "wlT")[:, 128:256], start=True, stop=True)\
                .then_inc(sem("x2_mm"), 1)
            keys_pe(1, (3,))
            PE.wait_ge(sem("x2_square"), 1)
            PE.matmul(bank(5)[:, 0:256], half64[:, :], aux[:, S:KQ], start=True, stop=True)\
                .then_inc(sem("x2_mm"), 1)
            values_pe(1, 7, V3_PARTS[0])
            PE.wait_ge(sem("k_ev"), 2)
            PE.wait_ge(sem("x2_mask"), 1)
            PE.wait_ge(sem("x2_dve"), 3)
            for j in range(SJ):
                mm = x2_scores_pe(0, j)
            mm.then_inc(sem("x2_s"), 1)
            PE.wait_ge(sem("v_ev"), 2)
            values_pe(1, 5, V3_PARTS[1])
            PE.wait_ge(sem("v_ev"), 3)
            for j in range(SJ):
                PE.wait_ge(sem("x2_exp"), j + 1)
                mm = x2_scores_pe(1, j)
                if j == SJ - 1:
                    mm.then_inc(sem("x2_s"), 1)
                x2_turn_pe(0, j)
            x2_products_pe(0)
            for j in range(SJ):
                x2_turn_pe(1, j)
            x2_products_pe(1)
            PE.wait_ge(sem("x2_dve"), 5)
            PE.transpose(bank(0)[:, 0:128], att[:, :], ident[:, :]).then_inc(sem("x2_mm"), 1)
            PE.wait_ge(sem("x2_dve"), 6)
            PE.matmul(bank(1)[:, 0:128], attT[:, :], w("l2", "woT"), start=True, stop=False)
            PE.matmul(bank(1)[:, 0:128], ones[0:1, :], w("l2", "bo"), start=False, stop=True)\
                .then_inc(sem("x2_mm"), 1)

        def x2_act():
            A.wait_ge(sem("x2_ls"), 1)
            act_then(A.activation(lnv[:, :], mv[:, 1:2], ACT.Ln, bias=eps[:, :]))
            A.activation(rstd[:, :], lnv[:, :], ACT.Exp, scale=-0.5).then_inc(sem("x2_r"), 1)
            A.wait_ge(sem("x2_lat"), 1)
            A.activation(aux[:, S:KQ], kq2[:, S:KQ], ACT.Square).then_inc(sem("x2_square"), 1)
            A.wait_ge(sem("x2_lat"), 2)
            act_then(A.activation(aux[:, S:KQ], aux[:, S:KQ], ACT.Ln))
            A.activation(aux[:, S:KQ], aux[:, S:KQ], ACT.Exp, scale=-0.5).then_inc(sem("x2_r"), 1)
            values3_act(0, 7)
            values3_act(1, 5)
            for h in range(2):
                A.wait_ge(sem("x2_m"), h + 1)
                for j in range(SJ):
                    n = min(512, KL - 512 * j)
                    if h == 1:
                        A.wait_ge(sem("x2_t"), j + 1)
                    A.activation(pp[:, chunk(j, n)], bank(j)[:, 0:n], ACT.Exp, bias=nm[:, h:h + 1],
                                 accum_out=sums[:, SJ * h + j:SJ * h + j + 1]).then_inc(sem("x2_exp"), 1)

        def x2_dve():
            dve_then(V.bn_stats(st[:, :], xn[:, :]))
            V.bn_aggr(mv[:, :], st[:, :]).then_inc(sem("x2_ls"), 1)
            V.wait_ge(sem("x2_r"), 1)
            V.wait_ge(sem("x2_ls"), 1)
            V.tensor_scalar(att[:, :], xn[:, :], mv[:, 0:1], rstd[:, :], ALU.subtract, ALU.mult)\
                .then_inc(sem("x2_dve"), 1)
            V.wait_ge(sem("x2_mm"), 1)
            V.tensor_scalar(lnT, bank(4)[:, 0:128], w("l2", "llg"), w("l2", "llb"), ALU.mult, ALU.add)\
                .then_inc(sem("x2_dve"), 1)
            V.wait_ge(sem("x2_mm"), 2)
            V.tensor_copy(kq2[:, S:KQ], bank(4)[:, 128:384]).then_inc(sem("x2_lat"), 1)
            dve_then(V.tensor_copy(vv[:, 16, :], bank(4)[:, 384:512]))
            V.wait_ge(sem("d_m3"), 16)
            V.wait_ge(sem("k_mm"), 2)
            V.tensor_tensor(kv_views(1)[0], bank(0, 4), mask3u, ALU.mult).then_inc(sem("k_ev"), 1)
            V.wait_ge(sem("x2_mm"), 3)
            V.tensor_scalar(aux[:, S:KQ], bank(5)[:, 0:256], 1e-16, None, ALU.max).then_inc(sem("x2_lat"), 1)
            V.wait_ge(sem("x2_r"), 2)
            dve_then(V.scalar_tensor_tensor(kq2[:, S:KL], kq2[:, S:KL], w("l2", "kng"), aux[:, S:KL],
                                            ALU.mult, ALU.mult))
            dve_then(V.scalar_tensor_tensor(kq2[:, KL:KQ], kq2[:, KL:KQ], w("l2", "qng"), aux[:, KL:KQ],
                                            ALU.mult, ALU.mult))
            for h in range(2):
                dve_then(V.tensor_scalar(qm[:, h, :], kq2[:, KL:KQ], mh[:, h:h + 1], 64 ** -0.5,
                                         ALU.mult, ALU.mult))
            V.sem_inc(sem("x2_dve"), 1)
            V.tensor_scalar(mrow3, mask3u[0:1, :], -1.0, BIG, ALU.add, ALU.mult).then_inc(sem("mrow3"), 1)

            def largest(h):
                V.wait_ge(sem("x2_s"), h + 1)
                V.tensor_reduce(nm[:, h:h + 1], ps[:, 0:KL], AX.X, ALU.max, negate=True).then_inc(sem("x2_m"), 1)

            largest(0)
            for h in range(2):
                for i in range(SJ):
                    V.wait_ge(sem("x2_t"), SJ * h + i + 1)
                    if h == 1 and i == 0:
                        V.wait_ge(sem("x2_mm"), 4)
                    n = min(4, 17 - 4 * i)
                    V.tensor_copy(ppT[:, 4 * i:4 * i + n, :].rearrange("p c q -> p (c q)"),
                                  bank(5 + i % 2)[:, 0:128 * n]).then_inc(sem("x2_te"), 1)
                if h == 0:
                    largest(1)
                V.wait_ge(sem("x2_mm"), 4 + h)
                V.wait_ge(sem("x2_exp"), SJ * h + SJ)
                dve_then(V.tensor_reduce(sc1[:, :], sums[:, SJ * h:SJ * h + SJ], AX.X, ALU.add))
                dve_then(V.reciprocal(sc1[:, :], sc1[:, :]))
                V.tensor_scalar(att[:, 64 * h:64 * h + 64], bank(7)[:, 192 * h:192 * h + 64], sc1[:, :], None,
                                ALU.mult).then_inc(sem("x2_dve"), 1)
            V.wait_ge(sem("x2_mm"), 6)
            V.tensor_copy(attT[:, :], bank(0)[:, 0:128]).then_inc(sem("x2_dve"), 1)
            V.wait_ge(sem("x2_mm"), 7)
            dve_then(V.tensor_tensor(x[:, :], bank(1)[:, 0:128], x[:, :], ALU.add))

        fk, fq, ve, fe = (l2s[:, 512 + 256 * i:768 + 256 * i] for i in range(4))
        kvm = l2s[:, 1536:1536 + 144]

        def lin_pe():
            PE.matmul(bank(0)[:, 0:128], w("l2", "aq"), xnT[:, :], start=True, stop=True)
            PE.matmul(bank(1)[:, 0:128], xnT[:, :], w("l2", "ak"), start=True, stop=False)
            PE.matmul(bank(1)[:, 0:128], ones[0:1, :], w("l2", "abk"), start=False, stop=True)\
                .then_inc(sem("li_mm"), 1)
            PE.matmul(bank(2)[:, 0:128], xnT[:, :], w("l2", "av"), start=True, stop=False)
            PE.matmul(bank(2)[:, 0:128], ones[0:1, :], w("l2", "abv"), start=False, stop=True)\
                .then_inc(sem("li_mm"), 1)
            PE.wait_ge(sem("li_dve"), 3)
            PE.matmul(bank(3)[:, 0:129], fk[:, 0:128], ve[:, 0:129], start=True, stop=True)\
                .then_inc(sem("li_mm"), 1)
            PE.wait_ge(sem("li_dve"), 4)
            PE.matmul(bank(4)[:, 0:144], fq[:, 0:128], kvm, start=True, stop=True)\
                .then_inc(sem("li_mm"), 1)
            PE.wait_ge(sem("li_dve"), 5)
            PE.transpose(bank(5)[:, 0:128], att[:, :], ident[:, :]).then_inc(sem("li_mm"), 1)
            PE.wait_ge(sem("li_dve"), 6)
            PE.matmul(bank(6)[:, 0:128], attT[:, :], w("l2", "ao"), start=True, stop=False)
            PE.matmul(bank(6)[:, 0:128], ones[0:1, :], w("l2", "abo"), start=False, stop=True)\
                .then_inc(sem("li_mm"), 1)

        def lin_act():
            A.wait_ge(sem("li_dve"), 1)
            A.activation(fe[:, 0:128], fe[:, 0:128], ACT.Exp).then_inc(sem("li_act"), 1)
            A.wait_ge(sem("li_dve"), 2)
            A.activation(fe[:, 128:256], fe[:, 128:256], ACT.Exp).then_inc(sem("li_act"), 1)

        def lin_dve():
            V.wait_ge(sem("li_mm"), 1)
            dve_then(V.tensor_scalar(fq[:, 128:256], bank(0)[:, 0:128], w("l2", "abq"), None, ALU.add))
            V.tensor_scalar(fe[:, 0:128], fq[:, 128:256], 0.0, None, ALU.min).then_inc(sem("li_dve"), 1)
            V.tensor_scalar(fe[:, 128:256], bank(1)[:, 0:128], 0.0, None, ALU.min).then_inc(sem("li_dve"), 1)
            dve_then(V.memset(ve[:, 128:129], 1.0))
            V.wait_ge(sem("li_mm"), 2)
            dve_then(V.tensor_copy(ve[:, 0:128], bank(2)[:, 0:128]))
            V.wait_ge(sem("li_act"), 1)
            dve_then(V.scalar_tensor_tensor(fq[:, 0:128], fq[:, 128:256], 0.0, fe[:, 0:128], ALU.max, ALU.add))
            V.wait_ge(sem("li_act"), 2)
            V.scalar_tensor_tensor(fk[:, 0:128], bank(1)[:, 0:128], 0.0, fe[:, 128:256], ALU.max, ALU.add)\
                .then_inc(sem("li_dve"), 1)
            V.wait_ge(sem("li_mm"), 3)
            dve_then(V.tensor_tensor(kvm[:, 0:128].rearrange("p (h d) -> p h d", h=H),
                                     bank(3)[:, 0:128].rearrange("p (h d) -> p h d", h=H),
                                     m8[:, :].unsqueeze(2).to_broadcast([128, H, HD]), ALU.mult))
            dve_then(V.tensor_copy(sc1[:, :], bank(3)[:, 128:129]))
            V.tensor_scalar(kvm[:, 128:144], m8[:, :], sc1[:, :], None, ALU.mult).then_inc(sem("li_dve"), 1)
            V.wait_ge(sem("li_mm"), 4)
            dve_then(V.tensor_scalar(rec[:, :], bank(4)[:, 128:144], 1e-6, None, ALU.max))
            dve_then(V.reciprocal(rec[:, :], rec[:, :]))
            V.tensor_tensor(att[:, :].rearrange("p (h d) -> p h d", h=H),
                            bank(4)[:, 0:128].rearrange("p (h d) -> p h d", h=H),
                            rec[:, :].unsqueeze(2).to_broadcast([128, H, HD]), ALU.mult)\
                .then_inc(sem("li_dve"), 1)
            V.wait_ge(sem("li_mm"), 5)
            V.tensor_copy(attT[:, :], bank(5)[:, 0:128]).then_inc(sem("li_dve"), 1)
            V.wait_ge(sem("li_mm"), 6)
            dve_then(V.tensor_tensor(x[:, :], bank(6)[:, 0:128], x[:, :], ALU.add))

        ew = w32[:, 4096:8192]

        def moe2_pe():
            PE.matmul(bank(7)[:, 128:160], xnT[:, :], w("l2", "rwT"), start=True, stop=True)\
                .then_inc(sem("m2_gate"), 1)
            PE.wait_ge(sem("d_ew"), 16)
            for u in range(8):
                if u >= 4:
                    PE.wait_ge(sem("m2_acc"), 4 * (u - 3))
                PE.matmul(bank(u % 4), xnT[:, :], ew[:, 512 * u:512 * u + 512], start=True, stop=True)\
                    .then_inc(sem("m2_mm"), 1)

        def moe2_act():
            A.wait_ge(sem("m2_s"), 1)
            A.activation(sm[:, 0:32], bank(7)[:, 128:160], ACT.Exp, bias=nm[:, 0:1], accum_out=sc1[:, :])\
                .then_inc(sem("m2_e"), 1)

        def moe2_dve():
            V.wait_ge(sem("m2_gate"), 1)
            V.tensor_reduce(nm[:, 0:1], bank(7)[:, 128:160], AX.X, ALU.max, negate=True).then_inc(sem("m2_s"), 1)
            V.wait_ge(sem("m2_e"), 1)
            dve_then(V.reciprocal(sc1[:, :], sc1[:, :]))
            dve_then(V.tensor_scalar(lw[:, 0:32], sm[:, 0:32], sc1[:, :], None, ALU.mult))
            top_k(32, 2, sel[:, 0:32])
            dve_then(V.tensor_tensor(sel[:, 0:32], sel[:, 0:32], lw[:, 0:32], ALU.mult))
            for e in range(32):
                if e % 4 == 0:
                    V.wait_ge(sem("m2_mm"), e // 4 + 1)
                V.scalar_tensor_tensor(x[:, :], bank(e // 4 % 4)[:, 128 * (e % 4):128 * (e % 4) + 128],
                                       sel[:, e:e + 1], x[:, :], ALU.mult, ALU.add).then_inc(sem("m2_acc"), 1)
                V.wait_ge(sem("m2_acc"), e + 1)

        q3, k3, v3s = (l2s[:, 128 * i:128 * i + 128] for i in range(3))
        kbd = r32[:, 0:2048]
        s3 = r32[:, 2048:4096]
        p3T = r32[:, 4096:6144]

        def self_pe():
            PE.matmul(bank(0)[:, 0:128], w("l3", "sqT"), xnT[:, :], start=True, stop=True)
            PE.matmul(bank(1)[:, 0:128], w("l3", "skT"), xnT[:, :], start=True, stop=True)
            PE.matmul(bank(2)[:, 0:128], xnT[:, :], w("l3", "svT"), start=True, stop=True)\
                .then_inc(sem("sa_mm"), 1)
            PE.wait_ge(sem("sa_dve"), 1)
            for j in range(4):
                mm = PE.matmul(bank(4 + j), q3, kbd[:, 512 * j:512 * j + 512], start=True, stop=True)
            mm.then_inc(sem("sa_mm"), 1)
            PE.wait_ge(sem("sa_exp"), 1)
            for g in range(4):
                for h in range(4 * g, 4 * g + 4):
                    mm = PE.transpose(bank(g)[:, 128 * (h % 4):128 * (h % 4) + 128],
                                      s3[:, 128 * h:128 * h + 128], ident[:, :])
                mm.then_inc(sem("sa_t"), 1)
            for g in range(4):
                PE.wait_ge(sem("sa_te"), g + 1)
                for h in range(4 * g, 4 * g + 4):
                    mm = PE.matmul(bank(4)[:, HD * h:HD * h + HD], p3T[:, 128 * h:128 * h + 128],
                                   v3s[:, HD * h:HD * h + HD], start=True, stop=True)
            mm.then_inc(sem("sa_mm"), 1)

        def self_act():
            A.wait_ge(sem("sa_dve"), 2)
            A.activation(s3, s3, ACT.Exp).then_inc(sem("sa_exp"), 1)
            for g in (1, 3):
                A.wait_ge(sem("sa_t"), g + 1)
                A.wait_ge(sem("sa_te"), g)
                A.activation(p3T[:, 512 * g:512 * g + 512], bank(g), ACT.Copy).then_inc(sem("sa_te"), 1)

        def self_dve():
            V.wait_ge(sem("sa_mm"), 1)
            dve_then(V.tensor_scalar(q3, bank(0)[:, 0:128], HD ** -0.5, None, ALU.mult))
            dve_then(V.tensor_copy(v3s, bank(2)[:, 0:128]))
            V.tensor_tensor(kbd.rearrange("p (h k) -> p h k", h=H),
                            bank(1)[:, 0:128].unsqueeze(1).to_broadcast([128, H, 128]),
                            m8[:, :].unsqueeze(2).to_broadcast([128, H, 128]), ALU.mult).then_inc(sem("sa_dve"), 1)
            V.wait_ge(sem("sa_mm"), 2)
            dve_then(V.tensor_reduce(nm[:, :], bank(4, 4).rearrange("p (h k) -> p h k", h=H), AX.X, ALU.max))
            V.tensor_tensor(s3.rearrange("p (h k) -> p h k", h=H), bank(4, 4).rearrange("p (h k) -> p h k", h=H),
                            nm[:, :].unsqueeze(2).to_broadcast([128, H, 128]), ALU.subtract)\
                .then_inc(sem("sa_dve"), 1)
            V.wait_ge(sem("sa_exp"), 1)
            dve_then(V.tensor_reduce(rec[:, :], s3.rearrange("p (h k) -> p h k", h=H), AX.X, ALU.add))
            for g in (0, 2):
                V.wait_ge(sem("sa_t"), g + 1)
                V.wait_ge(sem("sa_te"), g) if g else None
                V.tensor_copy(p3T[:, 512 * g:512 * g + 512], bank(g)).then_inc(sem("sa_te"), 1)
            dve_then(V.reciprocal(rec[:, :], rec[:, :]))
            V.wait_ge(sem("sa_mm"), 3)
            dve_then(V.tensor_tensor(att[:, :].rearrange("p (h d) -> p h d", h=H),
                                     bank(4)[:, 0:128].rearrange("p (h d) -> p h d", h=H),
                                     rec[:, :].unsqueeze(2).to_broadcast([128, H, HD]), ALU.mult))
            dve_then(V.tensor_tensor(x[:, :], att[:, :], x[:, :], ALU.add))

        f8 = sb("f8", [128, 128], FP8)
        fb = sb("fb", [128, 128], BF16)
        fy = sb("fy", [128, 128], BF16)
        fout = sb("fout", [128, 128], BF16)
        u8m = attT[:, :].bitcast(mybir.dt.uint32)

        def quantise(src, dst):
            dve_then(V.tensor_scalar(r1[:, :], src, 240.0, -240.0, ALU.min, ALU.max))
            dve_then(V.tensor_copy(f8[:, :], r1[:, :], saturate=False))
            dve_then(V.tensor_copy(dst, f8[:, :]))
            dve_then(V.tensor_scalar(r1[:, :], src, 0.5, 240.0, ALU.mult, ALU.min))
            dve_then(V.tensor_scalar(r1[:, :], r1[:, :], -240.0, None, ALU.max))
            dve_then(V.tensor_copy(f8[:, :], r1[:, :], saturate=False))
            dve_then(V.tensor_scalar(r1[:, :], f8[:, :], 2.0, None, ALU.mult))
            dve_then(V.tensor_tensor(r2[:, :], r1[:, :], r1[:, :], ALU.mult))
            dve_then(V.tensor_scalar(r2[:, :], r2[:, :], 480.0 ** 2, 3e38, ALU.is_ge, ALU.mult))
            dve_then(V.tensor_scalar(r2[:, :], r2[:, :], 3e38, None, ALU.mult))
            dve_then(V.tensor_tensor(r1[:, :], r1[:, :], r2[:, :], ALU.add))
            dve_then(V.tensor_tensor(r1[:, :], r1[:, :], r2[:, :], ALU.subtract))
            dve_then(V.tensor_tensor(r2[:, :], src, src, ALU.mult))
            dve_then(V.tensor_scalar(u8m[:, :], r2[:, :], 240.0 ** 2, None, ALU.is_gt))
            dve_then(V.tensor_copy(fb[:, :], r1[:, :]))
            dve_then(V.copy_predicated(dst, u8m[:, :], fb[:, :]))

        def fp8_pe():
            PE.wait_ge(sem("f_q"), 1)
            PE.transpose(bank(0).bitcast(BF16)[:, 0:128], fy[:, :], identb[:, :]).then_inc(sem("f_mm"), 1)
            PE.wait_ge(sem("f_q"), 2)
            PE.matmul(bank(1)[:, 0:128], fout[:, :], kq[:, :], start=True, stop=True).then_inc(sem("f_mm"), 1)

        def fp8_weights_dve():
            V.wait_ge(sem("d_f"), 64)
            dve_then(V.reciprocal(sc1[:, :], skk[:, :]))
            dve_then(V.tensor_scalar(kq32[:, :], kq[:, :], sc1[:, :], None, ALU.mult))
            quantise(kq32[:, :], kq[:, :])
            dve_then(V.reciprocal(inv_in[:, :], sin[:, :]))
            dve_then(V.tensor_tensor(skk[:, :], skk[:, :], sin[:, :], ALU.mult))

        def fp8_dve():
            dve_then(V.tensor_copy(fb[:, :], xn[:, :]))
            dve_then(V.tensor_scalar(kq32[:, :], fb[:, :], inv_in[:, :], None, ALU.mult))
            quantise(kq32[:, :], fy[:, :])
            V.sem_inc(sem("f_q"), 1)
            V.wait_ge(sem("f_mm"), 1)
            V.tensor_copy(fout[:, :], bank(0).bitcast(BF16)[:, 0:128]).then_inc(sem("f_q"), 1)
            V.wait_ge(sem("f_mm"), 2)
            dve_then(V.tensor_scalar(fb[:, :], bank(1)[:, 0:128], skk[:, :], None, ALU.mult))
            dve_then(V.tensor_tensor(fy[:, :], fb[:, :], fbias[:, :], ALU.add))
            V.tensor_tensor(x[:, :], x[:, :], fy[:, :], ALU.add).then_inc(sem("x_done"), 1)

        mrow3 = w32[0:1, 2560:3584].bitcast(BF16)
        mrow3h = mrow3.unsqueeze(1).to_broadcast([1, H, S])

        @block.sync
        def _(sy):
            load(sy, x[:, :], a["x"], "x")
            load(sy, ctxT[0:C, :], a["ctxT"], "ctxT")
            load(sy, packs["ctx"][:, :], a["pack_ctx"], "ctx")
            load(sy, r32[:, 0:lay["x0"][1]], a["pack_x0"], "x0")
            load(sy, ctx1[:, :, 0:C], a["ctx"].rearrange("(c p) n -> p c n", p=128), "ctx1")
            load(sy, packs["l0"][:, :], a["pack_l0"], "l0")
            load(sy, packs["l1"][:, :], a["pack_l1"], "l1")
            load(sy, packs["l2"][:, :], a["pack_l2"], "l2")
            load(sy, packs["l3"][:, :], a["pack_l3"], "l3")
            load(sy, gbias[:, :], a["gbias"].to_broadcast([128, 64]), "gb")
            load(sy, kq[:, :], a["kernel"], "f")
            load(sy, fbias[:, :], a["fbias"].to_broadcast([128, 128]), "f")
            load(sy, sin[:, :], a["s_in"].to_broadcast([128, 1]), "f")
            load(sy, skk[:, :], a["s_k"].to_broadcast([128, 1]), "f")
            stack_keys_sync(0)
            load(sy, w32[:, 0:4096], a["w1"], "w12")
            load(sy, w32[:, 4096:8192], a["w2"], "w12")
            sy.wait_ge(sem("x0_done"), 1)
            load(sy, egT, a["eg"], "eg")
            load(sy, euT, a["eu"], "eg")
            sy.wait_ge(sem("m0_selT"), 2)
            load(sy, w32[:, 0:4096], a["ed"], "eg")
            load(sy, ew, a["ew"], "ew")
            sy.wait_ge(sem("mamba_done"), 1)
            load(sy, mrow8, a["mask2"], "m8")
            load(sy, mask3u, a["mask3"].to_broadcast([128, S]), "m3")
            stack_keys_sync(1)
            sy.wait_ge(sem("mrow3"), 1)
            sy.dma_start(KS[KROWS:KROWS + 1, :, :], mrow3h).then_inc(sem("d_mask3"), 16)
            sy.wait_ge(sem("ks_ones"), 2)
            sy.dma_start(qs[KROWS:KROWS + 1, :], KS[0:1, 0, 0:H * T]).then_inc(sem("d_mask3"), 16)
            sy.wait_ge(sem("x_done"), 1)
            sy.dma_start(out, x[:, :]).then_inc(sem("d_out"), 16)
            sy.wait_ge(sem("d_out"), 16)

        @block.gpsimd
        def _(g):
            pool_then(G.memset(ident[:, :], 0.0))
            pool_then(G.affine_select(out=ident[:, :], in_=ident[:, :], compare_op=ALU.not_equal, fill=1.0,
                                      base=0, pattern=[[-1, 128]], channel_multiplier=1))
            pool_then(G.memset(identb[:, :], 0.0))
            pool_then(G.affine_select(out=identb[:, :], in_=identb[:, :], compare_op=ALU.not_equal, fill=1.0,
                                      base=0, pattern=[[-1, 128]], channel_multiplier=1))
            pool_then(G.memset(ones[:, :], 1.0))
            pool_then(G.memset(one[:, :], 1.0))
            pool_then(G.memset(eps[:, :], EPS))
            pool_then(G.memset(c96[:, :], 1.0 / C))
            pool_then(G.memset(c256[:, :], 1.0 / 256))
            pool_then(G.memset(ctx1[:, :, C:C + 1], 1.0))
            pool_then(G.memset(ctxT[C:128, :], 1.0))
            pool_then(G.memset(nmx[:, :], 0.0))
            pool_then(G.memset(nclamp[:, :], -CLAMP))
            pool_then(G.memset(npart[:, :, :], 0.0))
            pool_then(G.memset(m16[:, :], 0.0))
            for b in (0, 16, 32, 96):
                pool_then(G.affine_select(out=m16[:, :], in_=m16[:, :], compare_op=ALU.not_equal, fill=1.0,
                                          base=-b, pattern=[[-1, H]], channel_multiplier=1))
            for t, wd, n, v, inner in ((m8, HD, H, 1.0, 1), (mh, 64, 2, 1.0, 1), (half64, 64, 2, 1.0 / 64, 64)):
                pool_then(G.memset(t[:, :], v))
                view = t[:, :].rearrange("p (h i) -> p h i", h=n)
                pool_then(G.affine_select(out=view, in_=view, compare_op=ALU.is_ge, fill=0.0, base=0,
                                          pattern=[[-wd, n], [0, inner]], channel_multiplier=1))
                pool_then(G.affine_select(out=view, in_=view, compare_op=ALU.is_ge, fill=0.0, base=wd - 1,
                                          pattern=[[wd, n], [0, inner]], channel_multiplier=-1))
            G.sem_inc(sem("consts"), 1)
            pool_then(G.memset(ks_region[0:SHIFT, :], TWO_ONES))
            G.sem_inc(sem("ks_ones"), 1)
            split_keys_pool(0)
            G.wait_ge(sem("d_m8"), 16)
            pool_then(G.memset(mrow[:, S:KL], 0.0))
            pool_then(G.tensor_scalar(mrow[:, 0:S], mrow8, -1.0, BIG, ALU.add, ALU.mult))
            G.sem_inc(sem("x2_mask"), 1)
            split_keys_pool(1)
            G.wait_ge(sem("x2_done"), 1)
            pool_then(G.memset(ks_region[0:SHIFT, :], TWO_ONES))
            G.sem_inc(sem("ks_ones"), 1)

        @block.scalar
        def _(act):
            A.preload_act_table_set("natural_log_exp_and_others")
            A.wait_ge(sem("consts"), 1)
            norm_act(0)
            A.wait_ge(sem("d_ctx"), 16)
            keys_act(0)
            x0_act()
            norm_act(1)
            rec_act()
            norm_act(2)
            moe0_act()
            norm_act(3)
            narrow_act(0)
            norm_act(4)
            mamba_act()
            norm_act(5)
            moe1_act()
            norm_act(6)
            x2_act()
            norm_act(7)
            lin_act()
            norm_act(8)
            moe2_act()
            norm_act(9)
            narrow_act(1)
            norm_act(10)
            self_act()
            norm_act(11)

        @block.vector
        def _(dve):
            V.wait_ge(sem("consts"), 1)
            dve_then(V.tensor_reduce(m4[:, :], m8[:, :].rearrange("p (g j) -> p j g", g=4), AX.X, ALU.add))
            V.wait_ge(sem("d_x"), 16)
            norm_dve(0)
            selection_dve()
            V.wait_ge(sem("d_ctxT"), 16)
            V.tensor_copy(ctxR[:, :], ctxT[0:C, :]).then_inc(sem("ctxR"), 1)
            x0_dve()
            V.sem_inc(sem("x0_done"), 1)
            norm_dve(1)
            rec_dve()
            norm_dve(2)
            moe0_dve()
            norm_dve(3)
            V.wait_ge(sem("d_l1"), 16)
            narrow_dve(0)
            norm_dve(4)
            mamba_dve()
            V.sem_inc(sem("mamba_done"), 1)
            norm_dve(5)
            V.wait_ge(sem("d_l2"), 16)
            moe1_dve()
            V.sem_inc(sem("moe1_done"), 1)
            norm_dve(6)
            x2_dve()
            V.sem_inc(sem("x2_done"), 1)
            norm_dve(7)
            lin_dve()
            norm_dve(8)
            moe2_dve()
            norm_dve(9)
            narrow_dve(1)
            norm_dve(10)
            self_dve()
            norm_dve(11)
            fp8_dve()

        @block.tensor
        def _(pe):
            PE.wait_ge(sem("consts"), 1)
            norm_pe(0)
            PE.wait_ge(sem("d_ctx"), 16)
            PE.wait_ge(sem("d_ctxT"), 16)
            keys_pe(0)
            x0_pe()
            norm_pe(1)
            rec_pe()
            norm_pe(2)
            moe0_pe()
            norm_pe(3)
            PE.wait_ge(sem("d_l1"), 16)
            narrow_pe(0)
            norm_pe(4)
            mamba_pe()
            norm_pe(5)
            PE.wait_ge(sem("d_l2"), 16)
            moe1_pe()
            PE.wait_ge(sem("d_l3"), 16)
            PE.wait_ge(sem("moe1_done"), 1)
            x2_pe()
            norm_pe(7)
            lin_pe()
            norm_pe(8)
            moe2_pe()
            norm_pe(9)
            narrow_pe(1)
            norm_pe(10)
            self_pe()
            norm_pe(11)
            fp8_pe()


def _packed(np, spec, parts):
    at = sum(cols for _, _, cols in spec)
    out = np.zeros((128, at), np.float32)
    at = 0
    for name, rows, cols in spec:
        out[0:rows, at:at + cols] = parts[name].reshape(rows, cols)
        at += cols
    return out


def kernel(**inputs):
    import numpy as np
    import concourse.bacc as _bacc
    from concourse import mybir as _mybir
    from concourse.bass_utils import run_bass_kernel_spmd as _run

    i = {k: np.asarray(v) for k, v in inputs.items()}

    def col(v, n=1):
        return v.reshape(n, -1).T

    cw = i["L1_attn_conv_w"].reshape(2, 128, 4).transpose(1, 0, 2)
    ar = {
        "x": i["x"].reshape(T, D),
        "ctx": i["ctx_768"].reshape(S, C),
        "ctxT": i["ctx_768"].reshape(S, C).T,
        "pack_ctx": _packed(np, SPEC_CTX, {
            "wk1": i["L1_xattn_Wk"], "wv1": i["L1_xattn_Wv"], "bk1": i["L1_xattn_bk"]}),
        "pack_x0": _packed(np, SPEC_X0, {
            "wq": i["L0_xattn_Wq"],
            "wkT": i["L0_xattn_Wk"].reshape(C, H, DH0).transpose(2, 1, 0),
            "wv": i["L0_xattn_Wv"],
            "wo": i["L0_xattn_Wo"].reshape(H, DH0, D).transpose(1, 0, 2),
            "bo": i["L0_xattn_bo"]}),
        "pack_l0": _packed(np, SPEC_L0, {
            "waT": i["L0_attn_Wa_w"].T, "wab": i["L0_attn_Wa_b"], "bT": i["L0_attn_B_w"].T,
            "cT": i["L0_attn_C_w"].T, "dT": i["L0_attn_D_w"].T, "gw": i["L0_ffn_gate_w"],
            "gb": i["L0_ffn_gate_b"], "b1": i["L0_ffn_b1"].reshape(8, 4, 128).transpose(2, 0, 1),
            "b2": i["L0_ffn_b2"]}),
        "pack_l1": _packed(np, SPEC_L1, {
            "wq": i["L1_xattn_Wq"], "bq": i["L1_xattn_bq"], "bv": i["L1_xattn_bv"], "wo": i["L1_xattn_Wo"],
            "bo": i["L1_xattn_bo"], "inT": i["L1_attn_in_proj_w"].T, "convw": cw,
            "convb": col(i["L1_attn_conv_b"], 2),
            "xpT": i["L1_attn_x_proj_w"].reshape(33, 2, 128).transpose(2, 1, 0),
            "alog": i["L1_attn_A_log"].reshape(2, 128, 16).transpose(1, 0, 2),
            "dpar": col(i["L1_attn_D_param"], 2), "dtw": col(i["L1_attn_dt_w"], 2),
            "dtb": col(i["L1_attn_dt_b"], 2),
            "outT": i["L1_attn_out_w"].reshape(D, 2, 128).transpose(2, 1, 0),
            "lng": col(i["L1_attn_ln_g"], 2), "lnb": col(i["L1_attn_ln_b"], 2),
            "gateT": i["L1_ffn_gate_w"].T, "sgT": i["L1_ffn_sg_w"].T, "suT": i["L1_ffn_su_w"].T,
            "sdT": i["L1_ffn_sd_w"].T}),
        "pack_l2": _packed(np, SPEC_L2, {
            "wkvT": i["L2_xattn_Wkv"].T, "wqT": i["L2_xattn_Wq"].T, "wlT": i["L2_xattn_Wlkv"].T,
            "woT": i["L2_xattn_Wo"].T, "bo": i["L2_xattn_bo"], "lxg": i["L2_xattn_ln_x_g"],
            "lxb": i["L2_xattn_ln_x_b"], "llg": i["L2_xattn_ln_l_g"], "llb": i["L2_xattn_ln_l_b"],
            "qng": np.concatenate([i["L2_xattn_qn_g"]] * 2), "kng": np.concatenate([i["L2_xattn_kn_g"]] * 2),
            "aq": i["L2_attn_Wq"], "ak": i["L2_attn_Wk"], "av": i["L2_attn_Wv"], "ao": i["L2_attn_Wo"],
            "abq": i["L2_attn_bq"], "abk": i["L2_attn_bk"], "abv": i["L2_attn_bv"], "abo": i["L2_attn_bo"],
            "rwT": i["L2_ffn_router_w"].T}),
        "pack_l3": _packed(np, SPEC_L3, {
            "wq": i["L3_xattn_Wq"], "wk": i["L3_xattn_Wk"], "wv": i["L3_xattn_Wv"], "wo": i["L3_xattn_Wo"],
            "sqT": i["L3_attn_Wq"].T, "skT": i["L3_attn_Wk"].T, "svT": i["L3_attn_Wv"].T}),
        "w1": i["L0_ffn_w1"].transpose(1, 0, 2).reshape(D, 4096),
        "w2": i["L0_ffn_w2"].reshape(8, 4, 128, D).transpose(2, 0, 1, 3).reshape(128, 4096),
        "eg": i["L1_ffn_eg_w"].transpose(2, 1, 0).reshape(D, 4096),
        "eu": i["L1_ffn_eu_w"].transpose(2, 1, 0).reshape(D, 4096),
        "ed": i["L1_ffn_ed_w"].transpose(2, 0, 1).reshape(32, 128, D).transpose(1, 0, 2).reshape(128, 4096),
        "ew": i["L2_ffn_expert_weights"].transpose(1, 0, 2).reshape(D, 4096),
        "gbias": i["L1_ffn_gate_bias"].reshape(1, 64),
        "kernel": i["L3_ffn_kernel"],
        "fbias": i["L3_ffn_bias"].reshape(1, D),
        "s_in": i["L3_ffn_input_scale"].reshape(1, 1),
        "s_k": i["L3_ffn_kernel_scale"].reshape(1, 1),
        "mask2": i["mask_BxS2_bk0"].reshape(1, S),
        "mask3": i["mask_BxS2_bf1"].reshape(1, S),
    }
    nc = _bacc.Bacc("TRN2", target_bir_lowering=False, num_devices=1)
    arrays, aps = {}, {}
    for name, v in ar.items():
        v = np.ascontiguousarray(v)
        arrays["in_" + name] = v
        aps[name] = nc.dram_tensor("in_" + name, v.shape, _mybir.dt.from_np(v.dtype), kind="ExternalInput").ap()
    res = nc.dram_tensor("out_0", (T, D), _mybir.dt.float32, kind="ExternalOutput").ap()
    perceiver(nc, aps, res)
    r = _run(nc, [arrays], core_ids=[0])
    return r.results[0]["out_0"].reshape(1, T, D)
```

```python
from contextlib import ExitStack

import concourse.bass as bass
from concourse import mybir

F32 = mybir.dt.float32
F32R = mybir.dt.float32r
BF16 = mybir.dt.bfloat16
FP8 = mybir.dt.float8e4
U8 = mybir.dt.uint8
ALU = mybir.AluOpType
ACT = mybir.ActivationFunctionType
AX = mybir.AxisListType

T = 128
D = 128
C = 96
S = 2048
NC = S // 128
H = 16
DH0 = 64
HD = D // H
EPS = 1e-5
CLAMP = 10000.0
BIG = 1e30
SENT = -3e38
TAKEN = 3e38

TWO_ONES = 1.0 + 0x3F80 * 2.0 ** -23

SHIFT = 3 * H
PROD = 9 * HD
KROWS = SHIFT + PROD
QH = 4


def pack_layout(spec):
    at, out = 0, {}
    for name, rows, cols in spec:
        out[name] = (rows, at, cols)
        at += cols
    return out, at


SPEC_CTX = [("wk1", C, D), ("wv1", C, D), ("bk1", D, 1)]
SPEC_X0 = [("wq", D, H * DH0), ("wkT", DH0, H * C), ("wv", C, H * DH0), ("wo", DH0, H * D), ("bo", 1, D)]
SPEC_L0 = [("waT", D, 32), ("wab", 32, 1), ("bT", D, 32), ("cT", 32, D), ("dT", D, D),
           ("gw", D, 8), ("gb", 1, 8), ("b1", 128, 32), ("b2", 8, D)]
SPEC_L1 = [("wq", D, D), ("bq", D, 1), ("bv", D, 1), ("wo", D, D), ("bo", 1, D),
           ("inT", D, 512), ("convw", D, 8), ("convb", D, 2), ("xpT", D, 66), ("alog", D, 32),
           ("dpar", D, 2), ("dtw", D, 2), ("dtb", D, 2), ("outT", D, 256), ("lng", D, 2), ("lnb", D, 2),
           ("gateT", D, 64), ("sgT", D, D), ("suT", D, D), ("sdT", D, D)]
SPEC_L2 = [("wkvT", C, 256), ("wqT", D, D), ("wlT", D, 256), ("woT", D, D), ("bo", 1, D),
           ("lxg", C, 1), ("lxb", C, 1), ("llg", D, 1), ("llb", D, 1), ("qng", D, 1), ("kng", D, 1),
           ("aq", D, D), ("ak", D, D), ("av", D, D), ("ao", D, D), ("abq", D, 1),
           ("abk", 1, D), ("abv", 1, D), ("abo", 1, D), ("rwT", D, 32)]
SPEC_L3 = [("wq", D, D), ("wk", C, D), ("wv", C, D), ("wo", D, D), ("sqT", D, D), ("skT", D, D), ("svT", D, D)]


def perceiver(nc, a, out):
    ctx = ExitStack()
    with ctx:
        sems = {}

        def sem(name):
            if name not in sems:
                sems[name] = ctx.enter_context(nc.semaphore(name))
            return sems[name]

        def sb(name, shape, dt=F32):
            return ctx.enter_context(nc.sbuf_tensor(name, shape, dt))

        lay = {}
        for key, spec in (("ctx", SPEC_CTX), ("x0", SPEC_X0), ("l0", SPEC_L0), ("l1", SPEC_L1),
                          ("l2", SPEC_L2), ("l3", SPEC_L3)):
            lay[key] = pack_layout(spec)

        with nc.sbuf_tensor("ctxL", [C, S], F32R) as ctxL, nc.sbuf_tensor("qkL", [C, H * T], F32R) as qkL:
            pass
        ks_region = sb("ks_region", [128, 16384])
        r32 = sb("r32", [128, 8192])
        w32 = sb("w32", [128, 8192])
        pbuf = sb("pbuf", [128, 3, 1024])
        ctxT = sb("ctxT", [128, S])
        ctx1 = sb("ctx1", [128, NC, C + 1])
        ctx_mv = sb("ctx_mv", [128, NC, 2])
        ctx_rstd = sb("ctx_rstd", [128, NC])
        qs = sb("qs", [128, H * T], BF16)
        with nc.sbuf_tensor("ctxR", [C + H, S], F32R) as ctxR, nc.sbuf_tensor("qkR", [C + H, H * T], F32R) as qkR:
            pass
        v3 = sb("v3", [128, NC, D])
        v1 = sb("v1", [128, NC, D])
        packs = {k: sb("pack_" + k, [128, lay[k][1]]) for k in ("ctx", "l0", "l1", "l2", "l3")}

        def w(key, name, rows=None):
            r, at, cols = lay[key][0][name]
            t = r32 if key == "x0" else packs[key]
            return t[0:r, at:at + cols]

        QK = r32[:, 8192 - 2048:8192]
        x = sb("x", [T, D])
        xn = sb("xn", [T, D])
        xnT = sb("xnT", [D, T])
        ident = sb("ident", [128, 128])
        identb = sb("identb", [128, 128], BF16)
        ones = sb("ones", [128, 128])
        c256 = sb("c256", [128, 128])
        half64 = sb("half64", [128, 128])
        m16 = sb("m16", [128, H])
        m8 = sb("m8", [128, H])
        m4 = sb("m4", [128, 4])
        mh = sb("mh", [128, 2])
        eps = sb("eps", [128, 1])
        one = sb("one", [128, 1])
        st = sb("st", [128, 6])
        mv = sb("mv", [128, 2])
        lnv = sb("lnv", [128, 1])
        rstd = sb("rstd", [128, 1])
        nmx = sb("nmx", [128, C + H])
        nm = sb("nm", [128, H])
        pm = sb("pm", [128, 2 * H])
        nclamp = sb("nclamp", [128, 1])
        npart = sb("npart", [128, 3, H], BF16)
        rec = sb("rec", [128, H])
        qT = sb("qT", [128, 128])
        r1 = sb("r1", [128, 128])
        r2 = sb("r2", [128, 128])
        qpart = sb("qpart", [128, 3, 128], BF16)
        att = sb("att", [128, 128])
        attT = sb("attT", [128, 128])
        scr = pbuf[:, :, :].rearrange("p a b -> p (a b)")
        lw = sb("lw", [128, 72])
        lr = sb("lr", [128, 72])
        top = sb("top", [128, 8])
        top2 = sb("top2", [128, 8])
        sel = sb("sel", [128, 64])
        sm = sb("sm", [128, 64])
        sc1 = sb("sc1", [128, 1])
        gbias = sb("gbias", [128, 64])
        sel32 = sb("sel32", [128, 16], BF16)
        qsel = sb("qsel", [128, QH, PROD + 2 * 3 * HD + SHIFT], BF16)
        kq = sb("kq", [128, 128], BF16)
        kq32 = qT
        fbias = sb("fbias", [128, 128], BF16)
        sin = sb("sin", [128, 1])
        skk = sb("skk", [128, 1])
        inv_in = sb("inv_in", [128, 1])

        ps = ctx.enter_context(nc.psum_tensor("ps", [128, 4096], F32))

        def bank(i, n=1):
            return ps[:, 512 * i:512 * (i + n)]

        k_scr = nc.dram_tensor("k_scr", [2, 3, D, S], BF16, kind="Internal").ap()

        KS = ks_region[:, :].bitcast(BF16).rearrange("p (h s) -> p h s", h=H)
        QS = qs[:, :].rearrange("p (h q) -> p h q", h=H)

        block = ctx.enter_context(nc.Block())

        chain = {"dve": 0, "act": 0, "pool": 0}

        def dve_then(ins):
            chain["dve"] += 1
            ins.then_inc(sem("dve_step"), 1)
            nc.vector.wait_ge(sem("dve_step"), chain["dve"])

        def act_then(ins):
            chain["act"] += 1
            ins.then_inc(sem("act_step"), 1)
            nc.scalar.wait_ge(sem("act_step"), chain["act"])

        def pool_then(ins):
            chain["pool"] += 1
            ins.then_inc(sem("pool_step"), 1)
            nc.gpsimd.wait_ge(sem("pool_step"), chain["pool"])

        V, A, PE, G = nc.vector, nc.scalar, nc.tensor, nc.gpsimd

        def turned(k):
            return k + 1 - (k >= 6)

        def norm_dve(k):
            dve_then(V.bn_stats(st[:, :], x[:, :]))
            V.bn_aggr(mv[:, :], st[:, :]).then_inc(sem("ln_stats"), 1)
            V.wait_ge(sem("ln_stats"), k + 1)
            V.wait_ge(sem("ln_rstd"), k + 1)
            V.tensor_scalar(xn[:, :], x[:, :], mv[:, 0:1], rstd[:, :], ALU.subtract, ALU.mult)\
                .then_inc(sem("ln_xn"), 1)
            V.wait_ge(sem("ln_xn"), k + 1)
            if k == 6:
                return
            V.wait_ge(sem("ln_t"), turned(k))
            V.tensor_copy(xnT[:, :], bank(7)[:, 0:128]).then_inc(sem("ln_xnT"), 1)

        def norm_act(k):
            A.wait_ge(sem("ln_stats"), k + 1)
            act_then(A.activation(lnv[:, :], mv[:, 1:2], ACT.Ln, bias=eps[:, :]))
            A.activation(rstd[:, :], lnv[:, :], ACT.Exp, scale=-0.5).then_inc(sem("ln_rstd"), 1)

        def norm_pe(k):
            PE.wait_ge(sem("ln_xn"), k + 1)
            PE.transpose(bank(7)[:, 0:128], xn[:, :], ident[:, :]).then_inc(sem("ln_t"), 1)
            PE.wait_ge(sem("ln_xnT"), turned(k))

        def top_k(n, k, dst):
            width = n + 8 - k
            dve_then(V.memset(lw[:, n:width], SENT))
            dve_then(V.max(top[:, :], lw[:, 0:width]))
            dve_then(V.memset(top2[:, :], SENT))
            dve_then(V.tensor_copy(top2[:, 0:k], top[:, 0:k]))
            dve_then(V.match_replace(lr[:, 0:width], top2[:, :], lw[:, 0:width], TAKEN))
            dve_then(V.tensor_tensor(dst, lr[:, 0:n], lw[:, 0:n], ALU.not_equal))

        def split_dve(src, t1, t2, part):
            dve_then(V.tensor_copy(part(0), src))
            dve_then(V.tensor_tensor(t1, src, part(0), ALU.subtract))
            dve_then(V.tensor_copy(part(1), t1))
            dve_then(V.tensor_tensor(t2, t1, part(1), ALU.subtract))

        def load(eng, dst, src, group):
            eng.dma_start(dst, src).then_inc(sem("d_" + group), 16)

        kreg = [w32, r32]

        def kv_views(n):
            t = kreg[n]
            kt = t[:, 0:2048]
            res = t[:, 2048:4096]
            parts = t[:, 4096:7168].bitcast(BF16).rearrange("p (i s) -> p i s", i=3)
            return kt, res, parts

        def keys_pe(n, chunks=range(4), first=0):
            wk = w("ctx", "wk1") if n == 0 else w("l3", "wk")
            for j in chunks:
                PE.matmul(bank(first + j), wk, ctxT[0:C, 512 * j:512 * j + 512], start=True, stop=True)\
                    .then_inc(sem("k_mm"), 1)

        def values3_pe(part):
            first, chunks = V3_PARTS[part]
            for i, c in enumerate(chunks):
                mm = PE.matmul(ps[:, 512 * first + 128 * i:512 * first + 128 * i + 128],
                               ctxT[0:C, 128 * c:128 * c + 128], w("l3", "wv"), start=True, stop=True)
            mm.then_inc(sem("v3_mm"), 1)

        def values3_act(part):
            A.wait_ge(sem("v3_mm"), part + 1)
            values_act(v3, *V3_PARTS[part], "v3_ev")

        def values_act(v, first, c, done):
            A.activation(v[:, c[0]:c[-1] + 1, :].rearrange("p c d -> p (c d)"),
                         ps[:, 512 * first:512 * first + 128 * len(c)], ACT.Copy).then_inc(sem(done), 1)

        def values1_pe(chunks):
            for c in chunks:
                mm = PE.matmul(ps[:, 1536 + 128 * c:1536 + 128 * c + 128], ctxT[0:C, 128 * c:128 * c + 128],
                               w("ctx", "wv1"), start=True, stop=True)
            mm.then_inc(sem("v1_mm"), 1)

        V3_PARTS = ((7, range(12, NC)), (6, range(4, 12)), (5, range(0, 4)))

        def keys_act():
            kt, _, _ = kv_views(0)
            for j in range(4):
                A.wait_ge(sem("k_mm"), j + 1)
                i = A.activation(kt[:, 512 * j:512 * j + 512], bank(j), ACT.Identity, bias=w("ctx", "bk1"))
            i.then_inc(sem("k_ev"), 1)

        def keys3_act():
            for j in range(4):
                A.wait_ge(sem("k_mm"), 4 + j + 1)
                i = A.activation(kt3[:, 512 * j:512 * j + 512], bank(4 + j), ACT.Copy)
            i.then_inc(sem("k_ev"), 1)

        def mask_keys3_pool():
            mask = v3[:, :, :].rearrange("p c d -> p (c d)")
            G.wait_ge(sem("d_m3"), 16)
            pool_then(G.tensor_copy(mask, mask3u))
            G.wait_ge(sem("k_ev"), 2)
            pool_then(G.tensor_tensor(kt3, kt3, mask, ALU.mult))
            G.sem_inc(sem("k3_masked"), 1)

        def split_keys_pool(n):
            kt, res, parts = kv_views(n)
            if n == 1:
                kt = kt3
            G.wait_ge(sem("k_ev"), n + 1)
            pool_then(G.tensor_copy(parts[:, 0, :], kt))
            pool_then(G.tensor_tensor(res, kt, parts[:, 0, :], ALU.subtract))
            pool_then(G.tensor_copy(parts[:, 1, :], res))
            pool_then(G.tensor_tensor(kt, res, parts[:, 1, :], ALU.subtract))
            G.tensor_copy(parts[:, 2, :], kt).then_inc(sem("k_parts"), 1)

        def store_keys_sync(n):
            _, _, parts = kv_views(n)
            sy = nc.sync
            sy.wait_ge(sem("k_parts"), n + 1)
            sy.dma_start(k_scr[n].rearrange("i p s -> p i s"), parts).then_inc(sem("d_kscr"), 16)
            sy.wait_ge(sem("d_kscr"), 16 * (n + 1))

        def stack_keys_sync(n):
            sy = nc.sync
            for r in range(9):
                src = k_scr[n, r % 3].rearrange("(h d) s -> d h s", h=H)
                if n == 1 and r == 0:
                    sy.wait_ge(sem("x2_done"), 1)
                sy.dma_start(KS[SHIFT + HD * r:SHIFT + HD * (r + 1), :, :], src).then_inc(sem("d_ks"), 16)

        def stack_queries_pe(n, j):
            PE.wait_ge(sem("q_parts"), n + 1)
            rows = slice(32 * j, 32 * j + 32)
            for hh in range(QH):
                for i in range(3):
                    at = 2 * 3 * HD - 3 * HD * i
                    mm = PE.matmul(bank(j)[0:KROWS, 128 * hh:128 * hh + 128], qsel[rows, hh, at:at + KROWS],
                                   qpart[rows, i, :], start=(i == 0), stop=(i == 2), tile_position=(32 * j, 0))
            mm.then_inc(sem("q_stack"), 1)

        def stack_queries_act(n):
            for j in range(4):
                A.wait_ge(sem("q_stack"), 4 * n + j + 1)
                A.activation(qs[0:KROWS, 512 * j:512 * j + 512], bank(j)[0:KROWS, :], ACT.Copy)\
                    .then_inc(sem("qs"), 1)

        def selection_dve():
            dve_then(V.tensor_reduce(sel32[:, :], identb[:, :].rearrange("p (g n) -> p n g", g=4)[:, 0:16, :],
                                     AX.X, ALU.max))
            dve_then(V.memset(qsel[:, :, :], 0.0))
            for r in range(3):
                at = SHIFT + 2 * 3 * HD + HD * r
                dve_then(V.tensor_reduce(qsel[:, :, at:at + HD],
                                         identb[:, :].rearrange("p (g j d) -> p j d g", g=4, j=QH), AX.X, ALU.max))

        NA, NB = 32, 64
        SLOTS = (0, 1, 3, 4, 6, 7, 9, 10)

        PBUFS = 4
        P = [scr[:, 512 * i:512 * i + 512] for i in range(PBUFS)]
        num, den = scr[:, 2048:2560], scr[:, 2560:3072]
        E = v3[:, :, :].rearrange("p c d -> p (c d)")

        def max_unit_pe(k, a):
            h, half = a // 2, a % 2
            if k == 0 and a < 2:
                PE.wait_ge(sem("x0_qkR"), 2 * a + 2)
            if a >= 2:
                PE.wait_ge(sem("at_max"), NA * k + a - 1)
            if a % 8 == 0 and a:
                PE.wait_ge(sem("at_shift"), 4 * k + a // 8)
                if k == 1:
                    PE.wait_ge(sem("at_clipE"), a // 8)
            rows = KROWS + (k == 2)
            for j in range(2):
                key = 1024 * half + 512 * j
                out_ = bank(4 + 2 * (a % 2) + j)
                if k == 0:
                    mm = PE.matmul(out_, qkR[0:C, 128 * h:128 * h + 128], ctxR[0:C, key:key + 512],
                                   start=True, stop=True)
                else:
                    mm = PE.matmul(out_, QS[0:rows, h, :], KS[0:rows, h, key:key + 512], start=True, stop=True)
            mm.then_inc(sem("at_a"), 1)

        def shift_pe(k, g):
            PE.wait_ge(sem("at_neg"), 4 * k + g + 1)
            if k == 0:
                PE.transpose(bank(4)[0:C + H, 0:128], nmx[:, :], ident[:, :]).then_inc(sem("at_negT"), 1)
            else:
                PE.transpose(bank(4).bitcast(BF16)[0:SHIFT, 0:128], npart[:, :, :].rearrange("p i h -> p (i h)"),
                             identb[:, :]).then_inc(sem("at_negT"), 1)

        def clip_bound_pe(g):
            PE.wait_ge(sem("at_shift"), 4 + g + 1)
            PE.matmul(bank(5), KS[0:SHIFT, 0, 0:128], qs[0:SHIFT, 512 * g:512 * g + 512], start=True, stop=True)\
                .then_inc(sem("at_clipM"), 1)

        def scores_pe(k, b):
            g, c = b // NC, b % NC
            if c == 0:
                PE.wait_ge(sem("at_shift"), 4 * k + g + 1)
                if k == 0:
                    PE.wait_ge(sem("x0_low"), g + 2)
            if b >= 2:
                PE.wait_ge(sem("at_exp"), NB * k + b - 1)
            if k == 0:
                keys, quad = slice(128 * c, 128 * c + 128), slice(512 * g, 512 * g + 512)
                PE.matmul(bank(2 + b % 2), ctxR[0:C + H, keys], qkR[0:C + H, quad], start=True, stop=False)
                PE.matmul(bank(2 + b % 2), ctxR[0:C, keys], qkL[:, quad], start=False, stop=False)
                mm = PE.matmul(bank(2 + b % 2), ctxL[:, keys], qkR[0:C, quad], start=False, stop=True)
            else:
                rows = KROWS + (k == 2)
                for hh in range(QH):
                    h = QH * g + hh
                    mm = PE.matmul(bank(2 + b % 2)[:, 128 * hh:128 * hh + 128],
                                   KS[0:rows, h, 128 * c:128 * c + 128], QS[0:rows, h, :], start=True, stop=True)
            mm.then_inc(sem("at_k"), 1)

        def products_pe(k, b):
            g, c = b // NC, b % NC
            if k == 1:
                PE.wait_ge(sem("at_clip"), b + 1)
            else:
                PE.wait_ge(sem("at_exp"), NB * k + b + 1)
            if c == 0 and g >= 2:
                PE.wait_ge(sem("at_o"), 4 * k + g - 1)
            p, acc = P[b % PBUFS], bank(g % 2)
            if k == 0:
                for hh in range(QH):
                    mm = PE.matmul(acc[:, 97 * hh:97 * hh + 97], p[:, 128 * hh:128 * hh + 128], ctx1[:, c, :],
                                   start=(c == 0 and hh == 0), stop=(c == NC - 1), skip_group_check=True)
            else:
                v = v1 if k == 1 else v3
                for t in range(4):
                    mm = PE.matmul(acc[32 * t:32 * t + 32, 0:256],
                                   v[:, c, 32 * g:32 * g + 32] if t < 2 else ones[:, 0:32],
                                   p[:, 256 * (t % 2):256 * (t % 2) + 256], start=(c == 0), stop=(c == NC - 1),
                                   tile_position=(0, 32 * t), skip_group_check=True)
            mm.then_inc(sem("at_pv"), 1)

        def core_pe(k, extra):
            if k:
                stack_queries_pe(k - 1, 0)
            for a in range(8):
                if k and a % 2 == 0 and a < 6:
                    stack_queries_pe(k - 1, a // 2 + 1)
                if k and a == 0:
                    PE.wait_ge(sem("qs"), 4 * (k - 1) + 1)
                max_unit_pe(k, a)
                if k == 0 and a % 2 == 1:
                    keys_pe(0, (a // 2,))
            if k == 0:
                PE.wait_ge(sem("k_ev"), 1)
            if k:
                PE.wait_ge(sem("qs"), 4 * k)
            shift_pe(k, 0)
            if k == 1:
                clip_bound_pe(0)
            scores_pe(k, 0)
            scores_pe(k, 1)
            for b in range(NB):
                g, c = b // NC, b % NC
                if b + 2 < NB:
                    scores_pe(k, b + 2)
                if c == 0 and g == 0 and k == 1:
                    PE.wait_ge(sem("v1_ev"), 2)
                if c == 0 and g == 0 and k == 2:
                    PE.wait_ge(sem("v3_ev"), 3)
                if g < 3 and c in SLOTS:
                    max_unit_pe(k, 8 * (g + 1) + SLOTS.index(c))
                products_pe(k, b)
                if g < 3 and c == 12:
                    shift_pe(k, g + 1)
                if g < 3 and c == 13 and k == 1:
                    clip_bound_pe(g + 1)
                extra(g, c)

        def core_act(k):
            def clip_bound(g):
                A.wait_ge(sem("at_clipM"), g + 1)
                A.activation(E[:, 512 * g:512 * g + 512], bank(5), ACT.Exp, bias=nclamp[:, :])\
                    .then_inc(sem("at_clipE"), 1)

            if k == 1:
                clip_bound(0)
            for b in range(NB):
                g, c = b // NC, b % NC
                p = P[b % PBUFS]
                A.wait_ge(sem("at_k"), NB * k + b + 1)
                if b >= PBUFS:
                    A.wait_ge(sem("at_pv"), NB * k + b - PBUFS + 1)
                A.activation(p, bank(2 + b % 2), ACT.Exp).then_inc(sem("at_exp"), 1)
                if k == 1 and g < 3 and c == 14:
                    clip_bound(g + 1)

        def core_dve(k, extra):
            def reduce_max(a):
                V.wait_ge(sem("at_a"), NA * k + a + 1)
                V.tensor_reduce(pm[:, a:a + 1], bank(4 + 2 * (a % 2), 2), AX.X, ALU.max, negate=True)\
                    .then_inc(sem("at_max"), 1)

            def negated(g):
                V.wait_ge(sem("at_max"), NA * k + 8 * (g + 1))
                pairs = pm[:, 8 * g:8 * g + 8].rearrange("p (h i) -> p h i", i=2)
                q = slice(QH * g, QH * g + QH)
                if k == 0:
                    V.tensor_reduce(nmx[:, C + QH * g:C + QH * g + QH], pairs, AX.X, ALU.min)\
                        .then_inc(sem("at_neg"), 1)
                    return
                dve_then(V.tensor_reduce(nm[:, q], pairs, AX.X, ALU.min))
                if k == 1:
                    dve_then(V.tensor_scalar(nm[:, q], nm[:, q], CLAMP, -CLAMP, ALU.min, ALU.max))
                split_dve(nm[:, q], r1[:, 0:QH], r2[:, 0:QH], lambda i: npart[:, i, q])
                V.tensor_copy(npart[:, 2, q], r2[:, 0:QH]).then_inc(sem("at_neg"), 1)

            def shift(g):
                V.wait_ge(sem("at_negT"), 4 * k + g + 1)
                lo, n = (C, H) if k == 0 else (0, SHIFT)
                src = bank(4) if k == 0 else bank(4).bitcast(BF16)
                dst = qkR[:, 512 * g:512 * g + 512].rearrange("p (h q) -> p h q", h=QH) if k == 0 \
                    else QS[:, QH * g:QH * g + QH, :]
                V.tensor_tensor(dst[lo:lo + n, :, :],
                                src[lo:lo + n, 0:128].unsqueeze(1).to_broadcast([n, QH, 128]),
                                m16[lo:lo + n, QH * g:QH * g + QH].unsqueeze(2).to_broadcast([n, QH, 128]),
                                ALU.mult).then_inc(sem("at_shift"), 1)

            def clip(b):
                V.wait_ge(sem("at_exp"), NB * k + b + 1)
                if b % NC == 0:
                    V.wait_ge(sem("at_clipE"), b // NC + 1)
                V.scalar_tensor_tensor(P[b % PBUFS], P[b % PBUFS], 1.0,
                                       E[:, 512 * (b // NC):512 * (b // NC) + 512], ALU.min, ALU.max)\
                    .then_inc(sem("at_clip"), 1)

            def results(g):
                V.wait_ge(sem("at_pv"), NB * k + NC * (g + 1))
                acc = bank(g % 2)
                if k == 0:
                    o = acc[:, 0:388].rearrange("p (h c) -> p h c", h=QH)
                    dve_then(V.reciprocal(rec[:, QH * g:QH * g + QH], o[:, :, C]))
                    V.tensor_tensor(o0[:, QH * g:QH * g + QH, :], o[:, :, 0:C],
                                    rec[:, QH * g:QH * g + QH].unsqueeze(2).to_broadcast([128, QH, C]), ALU.mult)\
                        .then_inc(sem("at_o"), 1)
                    return
                gr = slice(32 * g, 32 * g + 32)
                for t in range(4):
                    dst = num if t < 2 else den
                    i = V.tensor_tensor(dst[gr, 256 * (t % 2):256 * (t % 2) + 256].rearrange("p (j q) -> p j q", j=2),
                                        acc[32 * t:32 * t + 32, 0:256].rearrange("p (j q) -> p j q", j=2),
                                        m4[gr, 2 * (t % 2):2 * (t % 2) + 2].unsqueeze(2).to_broadcast([32, 2, 128]),
                                        ALU.mult)
                i.then_inc(sem("at_o"), 1)

            for a in range(8):
                reduce_max(a)
            negated(0)
            shift(0)
            if k == 1:
                clip(0)
            for b in range(NB):
                g, c = b // NC, b % NC
                if k == 1 and b + 1 < NB:
                    clip(b + 1)
                if g < 3 and c in SLOTS:
                    reduce_max(8 * (g + 1) + SLOTS.index(c))
                if g < 3 and c == 11:
                    negated(g + 1)
                if g < 3 and c == 12:
                    shift(g + 1)
                if c == 4 and g:
                    results(g - 1)
                extra(g, c)
            results(3)

        def nothing(g, c):
            pass

        def narrow_pe(n):
            key = "l1" if n == 0 else "l3"
            PE.matmul(bank(4)[:, 0:128], w(key, "wq"), xnT[:, :], start=True, stop=True)\
                .then_inc(sem("nq_mm"), 1)
            PE.wait_ge(sem("d_ks"), 16 * 9 * (n + 1))
            PE.wait_ge(sem("ks_ones"), n + 1)
            if n == 1:
                PE.wait_ge(sem("d_mask3"), 32)
            core_pe(n + 1, nothing)
            PE.wait_ge(sem("n_att"), n + 1)
            mm = PE.matmul(bank(2)[:, 0:128], attT[:, :], w(key, "wo"), start=True, stop=(n == 1))
            if n == 0:
                mm = PE.matmul(bank(2)[:, 0:128], ones[0:1, :], w(key, "bo"), start=False, stop=True)
            mm.then_inc(sem("n_out"), 1)

        def narrow_act(n):
            stack_queries_act(n)
            core_act(n + 1)

        def narrow_dve(n):
            key = "l1" if n == 0 else "l3"
            V.wait_ge(sem("nq_mm"), n + 1)
            if n == 0:
                dve_then(V.tensor_scalar(qT[:, :], bank(4)[:, 0:128], w(key, "bq"), HD ** -0.5, ALU.add, ALU.mult))
            else:
                dve_then(V.tensor_scalar(qT[:, :], bank(4)[:, 0:128], HD ** -0.5, None, ALU.mult))
            split_dve(qT[:, :], r1[:, :], r2[:, :], lambda i: qpart[:, i, :])
            V.tensor_copy(qpart[:, 2, :], r2[:, :]).then_inc(sem("q_parts"), 1)
            core_dve(n + 1, nothing)
            V.wait_ge(sem("at_o"), 4 * (n + 2))
            dve_then(V.tensor_reduce(r1[:, :], den.rearrange("p (j q) -> p q j", j=4), AX.X, ALU.add))
            dve_then(V.reciprocal(r1[:, :], r1[:, :]))
            dve_then(V.tensor_reduce(att[:, :], num.rearrange("p (j q) -> p q j", j=4), AX.X, ALU.add))
            if n == 0:
                dve_then(V.tensor_tensor(att[:, :], att[:, :], r1[:, :], ALU.mult))
                V.tensor_scalar(attT[:, :], att[:, :], w(key, "bv"), None, ALU.add).then_inc(sem("n_att"), 1)
            else:
                V.tensor_tensor(attT[:, :], att[:, :], r1[:, :], ALU.mult).then_inc(sem("n_att"), 1)
            V.wait_ge(sem("n_out"), n + 1)
            dve_then(V.tensor_tensor(x[:, :], bank(2)[:, 0:128], x[:, :], ALU.add))

        wkT = w("x0", "wkT").rearrange("p (h c) -> p h c", h=H)
        wv0 = w("x0", "wv").rearrange("p (h d) -> p h d", h=H)
        wo0 = w("x0", "wo").rearrange("p (h d) -> p h d", h=H)
        q0T = scr[0:DH0, 0:2048]
        o0 = v1[:, :, :].rearrange("p c d -> p (c d)")[:, 0:H * C].rearrange("p (h c) -> p h c", h=H)
        oT = QK[0:C, :].rearrange("p (h q) -> p h q", h=H)
        vT = ks_region[0:DH0, 4096:6144].rearrange("p (h q) -> p h q", h=H)
        x0_bank_T, x0_bank_W = (4, 5, 6, 7), (7, 4, 5, 4)

        def x0_turn_pe(g):
            if g == 0:
                PE.wait_ge(sem("at_max"), NA)
            PE.wait_ge(sem("at_o"), g + 1)
            if g == 3:
                PE.wait_ge(sem("x0_vTe"), 1)
            for h in range(QH * g, QH * g + QH):
                mm = PE.transpose(bank(x0_bank_T[g])[0:C, 128 * (h % 4):128 * (h % 4) + 128], o0[:, h, :], ident[:, :])
            mm.then_inc(sem("x0_oT"), 1)

        def x0_values_pe(g):
            PE.wait_ge(sem("x0_oTe"), g + 1)
            if g == 3:
                PE.wait_ge(sem("x0_vTe"), 2)
            for h in range(QH * g, QH * g + QH):
                mm = PE.matmul(bank(x0_bank_W[g])[0:DH0, 128 * (h % 4):128 * (h % 4) + 128], wv0[:, h, :],
                               oT[:, h, :], start=True, stop=True)
            mm.then_inc(sem("x0_vT"), 1)

        def x0_out_pe(g):
            PE.wait_ge(sem("x0_vTe"), g + 1)
            if g == 0:
                PE.wait_ge(sem("x0_oTe"), 3)
            for h in range(QH * g, QH * g + QH):
                PE.matmul(bank(6)[:, 0:128], vT[:, h, :], wo0[:, h, :], start=(h == 0), stop=False,
                          skip_group_check=True)

        def x0_extra_pe(g, c):
            if g == 3 and c in (1, 3, 5):
                x0_turn_pe((c - 1) // 2)
            if g == 3 and c in (7, 9, 11):
                x0_values_pe((c - 7) // 2)
            if g == 3 and c in (13, 14, 15):
                x0_out_pe(c - 13)

        def x0_pe():
            PE.wait_ge(sem("d_x0"), 16)
            for h in range(H):
                mm = PE.matmul(bank(h // 4)[0:DH0, 128 * (h % 4):128 * (h % 4) + 128],
                               w("x0", "wq")[:, DH0 * h:DH0 * h + DH0], xnT[:, :], start=True, stop=True)
                if h % 4 == 3:
                    mm.then_inc(sem("x0_q"), 1)
            PE.wait_ge(sem("d_x0r"), 16)
            for h in range(H):
                if h % 4 == 0:
                    PE.wait_ge(sem("x0_qe"), h // 4 + 1)
                mm = PE.matmul(bank(4 + h // 4)[0:C, 128 * (h % 4):128 * (h % 4) + 128], wkT[:, h, :],
                               q0T[:, 128 * h:128 * h + 128], start=True, stop=True)
                if h % 4 == 3:
                    mm.then_inc(sem("x0_qk"), 1)
            PE.wait_ge(sem("consts"), 2)
            PE.wait_ge(sem("ctxR"), 1)
            PE.wait_ge(sem("d_ctx1"), 16)
            core_pe(0, x0_extra_pe)
            x0_turn_pe(3)
            x0_values_pe(3)
            x0_out_pe(3)
            PE.matmul(bank(6)[:, 0:128], ones[0:1, :], w("x0", "bo"), start=False, stop=True,
                      skip_group_check=True).then_inc(sem("x0_out"), 1)
            values1_pe(range(0, 6))

        def x0_act():
            for g in range(4):
                A.wait_ge(sem("x0_qk"), g + 1)
                A.activation(QK[0:C, 512 * g:512 * g + 512], bank(4 + g)[0:C, :], ACT.Copy)\
                    .then_inc(sem("x0_qact"), 1)
            keys_act()
            core_act(0)

        def x0_extra_dve(g, c):
            if g == 3 and c == 0:
                fp8_weights_dve()
            if g == 3 and c in (6, 8, 10):
                x0_turn_dve((c - 6) // 2)
            if g == 3 and c in (11, 13, 15):
                x0_values_dve((c - 11) // 2)

        def x0_turn_dve(g):
            V.wait_ge(sem("x0_oT"), g + 1)
            V.tensor_copy(oT[:, 4 * g:4 * g + 4, :].rearrange("p h q -> p (h q)"), bank(x0_bank_T[g])[0:C, :])\
                .then_inc(sem("x0_oTe"), 1)

        def x0_values_dve(g):
            V.wait_ge(sem("x0_vT"), g + 1)
            V.tensor_copy(vT[:, 4 * g:4 * g + 4, :].rearrange("p h q -> p (h q)"), bank(x0_bank_W[g])[0:DH0, :])\
                .then_inc(sem("x0_vTe"), 1)

        def x0_dve():
            for g in range(4):
                V.wait_ge(sem("x0_q"), g + 1)
                V.tensor_scalar(q0T[:, 512 * g:512 * g + 512], bank(g)[0:DH0, :], DH0 ** -0.5, None, ALU.mult)\
                    .then_inc(sem("x0_qe"), 1)
            V.wait_ge(sem("consts"), 2)
            dve_then(V.tensor_reduce(m4[:, :], m8[:, :].rearrange("p (g j) -> p j g", g=4), AX.X, ALU.add))
            selection_dve()
            for g in range(4):
                quad = slice(512 * g, 512 * g + 512)
                V.wait_ge(sem("x0_qact"), g + 1)
                V.tensor_copy(qkR[0:C, quad], QK[0:C, quad]).then_inc(sem("x0_qkR"), 1)
            core_dve(0, x0_extra_dve)
            x0_turn_dve(3)
            x0_values_dve(3)
            V.wait_ge(sem("x0_out"), 1)
            dve_then(V.tensor_tensor(x[:, :], bank(6)[:, 0:128], x[:, :], ALU.add))

        sc = {"a": pbuf[0:32, 1, 0:T], "h": pbuf[0:32, 1, T:2 * T]}
        nwab = sb("nwab", [32, 1])

        def rec_pe():
            PE.wait_ge(sem("d_l0"), 16)
            PE.matmul(bank(0)[0:32, 0:128], w("l0", "waT"), xnT[:, :], start=True, stop=True)\
                .then_inc(sem("rec_mm"), 1)
            PE.matmul(bank(1)[0:32, 0:128], w("l0", "bT"), xnT[:, :], start=True, stop=True)\
                .then_inc(sem("rec_mm"), 1)
            values1_pe(range(6, 12))
            PE.wait_ge(sem("rec_h"), 1)
            PE.matmul(bank(2)[:, 0:128], sc["h"][:, :], w("l0", "cT"), start=True, stop=False)
            PE.matmul(bank(2)[:, 0:128], xnT[:, :], w("l0", "dT"), start=False, stop=True)\
                .then_inc(sem("rec_mm"), 1)
            values1_pe(range(12, NC))

        def rec_act():
            A.wait_ge(sem("rec_mm"), 1)
            A.wait_ge(sem("rec_nb"), 1)
            A.activation(sc["a"][:, :], bank(0)[0:32, 0:128], ACT.Exp, bias=nwab[:, :], scale=-1.0)\
                .then_inc(sem("rec_e"), 1)
            A.wait_ge(sem("v1_mm"), 2)
            values_act(v1, 3, range(0, 12), "v1_ev")

        def rec_dve():
            V.wait_ge(sem("d_l0"), 16)
            V.tensor_scalar(nwab[:, :], w("l0", "wab"), -1.0, None, ALU.mult).then_inc(sem("rec_nb"), 1)
            V.wait_ge(sem("rec_e"), 1)
            dve_then(V.tensor_scalar(sc["a"][:, :], sc["a"][:, :], 1.0, None, ALU.add))
            dve_then(V.reciprocal(sc["a"][:, :], sc["a"][:, :]))
            V.wait_ge(sem("rec_mm"), 2)
            V.tensor_tensor_scan(sc["h"][:, :], sc["a"][:, :], bank(1)[0:32, 0:128], 0.0, ALU.mult, ALU.add)\
                .then_inc(sem("rec_h"), 1)
            V.wait_ge(sem("rec_mm"), 3)
            dve_then(V.tensor_tensor(x[:, :], bank(2)[:, 0:128], x[:, :], ALU.add))

        w1_0 = w32[:, 0:4096].rearrange("p (e f) -> p e f", e=8)
        w2_0 = w32[:, 4096:8192].rearrange("p (e c n) -> p e c n", e=8, c=4)
        hid = [pbuf[:, 0, 0:512], pbuf[:, 0, 512:1024]]
        selT = pbuf[0:8, 1, 0:T]

        def moe0_pe():
            PE.wait_ge(sem("v1_ev"), 2)
            PE.matmul(bank(6)[:, 0:8], xnT[:, :], w("l0", "gw"), start=True, stop=False)
            PE.matmul(bank(6)[:, 0:8], ones[0:1, :], w("l0", "gb"), start=False, stop=True)\
                .then_inc(sem("m0_gate"), 1)
            PE.wait_ge(sem("d_w12"), 32)

            def up(e):
                if e >= 2:
                    PE.wait_ge(sem("m0_relu"), e - 1)
                for c in range(4):
                    mm = PE.matmul(bank(e % 2)[:, 128 * c:128 * c + 128], w1_0[:, e, 128 * c:128 * c + 128],
                                   xnT[:, :], start=True, stop=True)
                mm.then_inc(sem("m0_up"), 1)

            def down(e):
                PE.wait_ge(sem("m0_relu"), e + 1)
                if e >= 2:
                    PE.wait_ge(sem("m0_acc"), e - 1)
                for c in range(4):
                    mm = PE.matmul(bank(2 + e % 2)[:, 0:128], hid[e % 2][:, 128 * c:128 * c + 128],
                                   w2_0[:, e, c, :], start=(c == 0), stop=(c == 3))
                mm.then_inc(sem("m0_down"), 1)

            up(0)
            for e in range(8):
                if e + 1 < 8:
                    up(e + 1)
                down(e)
            PE.wait_ge(sem("m0_sel"), 1)
            PE.transpose(bank(4)[0:8, 0:128], sel[:, 0:8], ident[:, :]).then_inc(sem("m0_selT"), 1)
            PE.wait_ge(sem("m0_selTe"), 1)
            PE.matmul(bank(5)[:, 0:128], selT[:, :], w("l0", "b2"), start=True, stop=True)\
                .then_inc(sem("m0_selT"), 1)

        def moe0_act():
            for e in range(8):
                A.wait_ge(sem("m0_up"), e + 1)
                if e >= 2:
                    A.wait_ge(sem("m0_down"), e - 1)
                for c in range(4):
                    i = A.activation(hid[e % 2][:, 128 * c:128 * c + 128], bank(e % 2)[:, 128 * c:128 * c + 128],
                                     ACT.Relu, bias=w("l0", "b1")[:, 4 * e + c:4 * e + c + 1])
                i.then_inc(sem("m0_relu"), 1)

        def context_rstd_act():
            A.wait_ge(sem("ctx_stats"), 1)
            act_then(A.activation(ctx_rstd[:, :], ctx_mv[:, :, 1], ACT.Ln, bias=eps[:, :]))
            A.activation(ctx_rstd[:, :], ctx_rstd[:, :], ACT.Exp, scale=-0.5).then_inc(sem("ctx_rstd"), 1)

        def normalise_context_pool():
            G.wait_ge(sem("ctx_rstd"), 1)
            c = ctx1[:, :, 0:C]
            pool_then(G.tensor_tensor(c, c, ctx_mv[:, :, 0:1].to_broadcast([128, NC, C]), ALU.subtract))
            G.tensor_tensor(c, c, ctx_rstd[:, :].unsqueeze(2).to_broadcast([128, NC, C]), ALU.mult)\
                .then_inc(sem("ctx_norm"), 1)

        def moe0_dve():
            V.wait_ge(sem("m0_gate"), 1)
            dve_then(V.tensor_copy(lw[:, 0:8], bank(6)[:, 0:8]))
            top_k(8, 2, sel[:, 0:8])
            V.sem_inc(sem("m0_sel"), 1)
            stats = v3[:, 0, 0:6 * NC].rearrange("p (c i) -> p c i", c=NC)
            for e in range(8):
                for c in range(4 * (e % 4), 4 * (e % 4) + 4):
                    i = V.bn_stats(stats[:, c, :], ctx1[:, c, 0:C]) if e < 4 else \
                        V.bn_aggr(ctx_mv[:, c, :], stats[:, c, :])
                dve_then(i)
                V.wait_ge(sem("m0_down"), e + 1)
                V.scalar_tensor_tensor(x[:, :], bank(2 + e % 2)[:, 0:128], sel[:, e:e + 1], x[:, :],
                                       ALU.mult, ALU.add).then_inc(sem("m0_acc"), 1)
                V.wait_ge(sem("m0_acc"), e + 1)
            V.sem_inc(sem("ctx_stats"), 1)
            V.wait_ge(sem("m0_selT"), 1)
            V.tensor_copy(selT[:, :], bank(4)[0:8, 0:128]).then_inc(sem("m0_selTe"), 1)
            V.wait_ge(sem("m0_selT"), 2)
            dve_then(V.tensor_tensor(x[:, :], bank(5)[:, 0:128], x[:, :], ALU.add))

        KR = ks_region
        dA = KR[:, 0:4096].rearrange("p (c n t) -> p c n t", c=2, n=16)
        xB = KR[:, 4096:8192].rearrange("p (c n t) -> p c n t", c=2, n=16)
        hs = KR[:, 8192:12288].rearrange("p (c n t) -> p c n t", c=2, n=16)
        bc = KR[0:96, 12288:12416].bitcast(BF16)
        bc_rest = KR[0:96, 12800:13056]
        bc_w = KR[:, 12416:12800].rearrange("p (k c r i) -> p k c r i", k=2, c=2, r=3)
        mamba = pbuf[:, :, :].rearrange("p a b -> p (a b)")

        def mw(i):
            return mamba[:, 256 * i:256 * i + 256]
        xc, sz, t1, t2, dt_, z_, y_, yc = (mw(i) for i in range(8))
        dtrep = mw(8)
        xpad = mamba[:, 2304:2304 + 2 * (T + 3)].rearrange("p (c t) -> p c t", c=2)
        negA = sb("negA", [128, 32])

        def c2(ap):
            return ap.rearrange("p (c t) -> p c t", c=2)

        def mamba_pe():
            for c in range(4):
                mm = PE.matmul(bank(0)[:, 128 * c:128 * c + 128], w("l1", "inT")[:, 128 * c:128 * c + 128],
                               xnT[:, :], start=True, stop=True)
            mm.then_inc(sem("mb_mm"), 1)
            keys_pe(1, first=4)
            PE.wait_ge(sem("mb_dve"), 1)
            for c in range(2):
                mm = PE.matmul(bank(1)[:, 0:128], c2(dtrep)[:, c, :], c2(xc)[:, c, :], start=(c == 0), stop=(c == 1))
            mm.then_inc(sem("mb_mm"), 1)
            PE.wait_ge(sem("mb_w"), 1)
            for k in range(2):
                for c in range(2):
                    mm = PE.matmul(bank(2)[0:96, 128 * k:128 * k + 128],
                                   bc_w[:, k, c, :, :].rearrange("p r i -> p (r i)"), c2(xc)[:, c, :],
                                   start=(c == 0), stop=(c == 1))
            mm.then_inc(sem("mb_mm"), 1)
            PE.wait_ge(sem("mb_dve"), 2)
            for k in range(2):
                if k == 1:
                    PE.wait_ge(sem("k_ev"), 2)
                for n in range(16):
                    mm = PE.matmul(bank(4 * k + n // 4)[:, 128 * (n % 4):128 * (n % 4) + 128],
                                   sel32[0:96, n:n + 1].to_broadcast([96, 128]), bc[:, 128 * k:128 * k + 128],
                                   start=True, stop=True)
                mm.then_inc(sem("mb_mm"), 1)
            PE.wait_ge(sem("mb_dve"), 3)
            for c in range(2):
                mm = PE.matmul(bank(0)[:, 0:128], c256[:, :], c2(y_)[:, c, :], start=(c == 0), stop=(c == 1))
            mm.then_inc(sem("mb_mm"), 1)
            PE.wait_ge(sem("mb_dve"), 4)
            for c in range(2):
                mm = PE.matmul(bank(1)[:, 0:128], c256[:, :], c2(t1)[:, c, :], start=(c == 0), stop=(c == 1))
            mm.then_inc(sem("mb_mm"), 1)
            PE.wait_ge(sem("mb_dve"), 5)
            for c in range(2):
                mm = PE.matmul(bank(2)[:, 0:128], c2(yc)[:, c, :], w("l1", "outT")[:, 128 * c:128 * c + 128],
                               start=(c == 0), stop=(c == 1))
            mm.then_inc(sem("mb_mm"), 1)

        def sigmoid(dst, src, signal):
            act_then(A.activation(dst, src, ACT.Exp, scale=-1.0))
            act_then(A.activation(dst, dst, ACT.Ln, bias=one[:, :]))
            A.activation(dst, dst, ACT.Exp, scale=-1.0).then_inc(signal, 1)

        def mamba_act():
            A.wait_ge(sem("mb_mm"), 1)
            A.wait_ge(sem("mb_xin"), 1)
            A.activation(negA[:, :], w("l1", "alog"), ACT.Exp).then_inc(sem("mb_negA"), 1)
            sigmoid(sz, bank(0)[:, 256:512], sem("mb_act"))
            A.wait_ge(sem("mb_conv"), 1)
            sigmoid(t1, xc, sem("mb_act"))
            keys3_act()
            A.wait_ge(sem("mb_conv"), 2)
            act_then(A.activation(t2, t1, ACT.Exp))
            A.activation(t2, t2, ACT.Ln, bias=one[:, :]).then_inc(sem("mb_act"), 1)
            A.wait_ge(sem("mb_conv"), 3)
            for c in range(2):
                for n in range(16):
                    i = A.activation(dA[:, c, n, :], c2(dt_)[:, c, :], ACT.Exp,
                                     scale=negA[:, 16 * c + n:16 * c + n + 1])
                i.then_inc(sem("mb_act"), 1)
            A.wait_ge(sem("mb_mm"), 7)
            act_then(A.activation(r1[:, :], bank(1)[:, 0:128], ACT.Ln, bias=eps[:, :]))
            A.activation(r1[:, :], r1[:, :], ACT.Exp, scale=-0.5).then_inc(sem("mb_act"), 1)

        def mamba_dve():
            cw, cb = w("l1", "convw"), w("l1", "convb")
            dve_then(V.memset(xpad[:, :, 0:3], 0.0))
            V.wait_ge(sem("mb_mm"), 1)
            V.tensor_copy(xpad[:, :, 3:T + 3], bank(0)[:, 0:256].rearrange("p (c t) -> p c t", c=2))\
                .then_inc(sem("mb_xin"), 1)
            V.wait_ge(sem("mb_xin"), 1)
            for c in range(2):
                dve_then(V.tensor_scalar(c2(xc)[:, c, :], xpad[:, c, 0:T], cw[:, 4 * c:4 * c + 1], cb[:, c:c + 1],
                                         ALU.mult, ALU.add))
                for k in range(1, 4):
                    dve_then(V.scalar_tensor_tensor(c2(xc)[:, c, :], xpad[:, c, k:k + T],
                                                    cw[:, 4 * c + k:4 * c + k + 1], c2(xc)[:, c, :],
                                                    ALU.mult, ALU.add))
            V.sem_inc(sem("mb_conv"), 1)
            V.wait_ge(sem("mb_act"), 1)
            dve_then(V.tensor_tensor(sz, bank(0)[:, 256:512], sz, ALU.mult))
            dve_then(V.tensor_copy(c2(dtrep), c2(w("l1", "xpT"))[:, :, 0:1].to_broadcast([128, 2, 128])))
            V.wait_ge(sem("mb_negA"), 1)
            dve_then(V.tensor_scalar(negA[:, :], negA[:, :], -1.0, None, ALU.mult))
            V.wait_ge(sem("mb_act"), 2)
            V.tensor_tensor(xc, xc, t1, ALU.mult).then_inc(sem("mb_dve"), 1)
            V.wait_ge(sem("mb_dve"), 1)
            V.wait_ge(sem("mb_mm"), 2)
            for c in range(2):
                dve_then(V.tensor_scalar(c2(z_)[:, c, :], bank(1)[:, 0:128], w("l1", "dtw")[:, c:c + 1],
                                         w("l1", "dtb")[:, c:c + 1], ALU.mult, ALU.add))
            dve_then(V.scalar_tensor_tensor(t1, z_, -1.0, z_, ALU.mult, ALU.min))
            V.sem_inc(sem("mb_conv"), 1)
            V.wait_ge(sem("mb_mm"), 3)
            dve_then(V.tensor_copy(bc, bank(2)[0:96, 0:256]))
            dve_then(V.tensor_tensor(bc_rest, bank(2)[0:96, 0:256], bc, ALU.subtract))
            V.tensor_copy(bc[32:64, :], bc_rest[32:64, :])
            dve_then(V.tensor_copy(bc[64:96, :], bc_rest[64:96, :]))
            dve_then(V.tensor_tensor(bc_rest[64:96, :], bc_rest[64:96, :], bc[64:96, :], ALU.subtract))
            V.tensor_copy(bc[64:96, :], bc_rest[64:96, :]).then_inc(sem("mb_dve"), 1)
            V.wait_ge(sem("mb_act"), 3)
            dve_then(V.scalar_tensor_tensor(dt_, z_, 0.0, t2, ALU.max, ALU.add))
            V.sem_inc(sem("mb_conv"), 1)
            dve_then(V.tensor_tensor(t1, xc, dt_, ALU.mult))
            V.wait_ge(sem("mb_mm"), 4)
            for c in range(2):
                dve_then(V.tensor_tensor(xB[:, c, :, :], bank(0, 4).rearrange("p (n t) -> p n t", n=16),
                                         c2(t1)[:, c, :].unsqueeze(1).to_broadcast([128, 16, T]), ALU.mult))
            for c in range(2):
                V.wait_ge(sem("mb_act"), 4 + c)
                dve_then(V.memset(dA[:, c, :, 0:1], 0.0))
                flat = [v[:, c, :, :].rearrange("p n t -> p (n t)") for v in (hs, dA, xB)]
                dve_then(V.tensor_tensor_scan(flat[0], flat[1], flat[2], 0.0, ALU.mult, ALU.add))
                if c == 0:
                    V.wait_ge(sem("mb_mm"), 5)
                dve_then(V.tensor_tensor(hs[:, c, :, :], bank(4, 4).rearrange("p (n t) -> p n t", n=16),
                                         hs[:, c, :, :], ALU.mult))
                dve_then(V.tensor_reduce(c2(y_)[:, c, :], hs[:, c, :, :].rearrange("p n t -> p t n"), AX.X, ALU.add))
                dve_then(V.scalar_tensor_tensor(c2(y_)[:, c, :], c2(xc)[:, c, :], w("l1", "dpar")[:, c:c + 1],
                                                c2(y_)[:, c, :], ALU.mult, ALU.add))
            V.sem_inc(sem("mb_dve"), 1)
            V.wait_ge(sem("mb_mm"), 6)
            dve_then(V.tensor_tensor(c2(yc), c2(y_), bank(0)[:, 0:128].unsqueeze(1).to_broadcast([128, 2, T]),
                                     ALU.subtract))
            V.tensor_tensor(t1, yc, yc, ALU.mult).then_inc(sem("mb_dve"), 1)
            V.wait_ge(sem("mb_act"), 6)
            dve_then(V.tensor_tensor(c2(yc), c2(yc), r1[:, :].unsqueeze(1).to_broadcast([128, 2, T]), ALU.mult))
            for c in range(2):
                dve_then(V.tensor_scalar(c2(yc)[:, c, :], c2(yc)[:, c, :], w("l1", "lng")[:, c:c + 1],
                                         w("l1", "lnb")[:, c:c + 1], ALU.mult, ALU.add))
            V.tensor_tensor(yc, yc, sz, ALU.mult).then_inc(sem("mb_dve"), 1)
            V.wait_ge(sem("mb_mm"), 8)
            dve_then(V.tensor_tensor(x[:, :], bank(2)[:, 0:128], x[:, :], ALU.add))

        egT, euT = r32[:, 0:4096], r32[:, 4096:8192]
        edT = w32[:, 0:4096].rearrange("p (m n) -> p m n", m=32)

        shared_e, shared_h = scr[:, 2048:2176], scr[:, 2176:2304]

        def moe1_pe():
            PE.matmul(bank(6)[:, 128:192], xnT[:, :], w("l1", "gateT"), start=True, stop=True)\
                .then_inc(sem("m1_gate"), 1)
            PE.matmul(bank(4)[:, 0:128], w("l1", "sgT"), xnT[:, :], start=True, stop=True)
            PE.matmul(bank(5)[:, 0:128], w("l1", "suT"), xnT[:, :], start=True, stop=True)\
                .then_inc(sem("m1_up"), 1)
            PE.wait_ge(sem("d_eg"), 48)

            def up(u):
                b = 2 * (u % 2)
                for t, wt in ((0, egT), (1, euT)):
                    for m in range(4 * u, 4 * u + 4):
                        mm = PE.matmul(bank(b + t)[:, 128 * (m % 4):128 * (m % 4) + 128], wt[:, 128 * m:128 * m + 128],
                                       xnT[:, :], start=True, stop=True)
                mm.then_inc(sem("m1_up"), 1)

            def down(u):
                PE.wait_ge(sem("m1_h"), u + 2)
                for m in range(4 * u, 4 * u + 4):
                    mm = PE.matmul(bank(6)[:, 0:128], scr[:, 1024 + 512 * (u % 2) + 128 * (m % 4):
                                                        1152 + 512 * (u % 2) + 128 * (m % 4)], edT[:, m, :],
                                   start=False, stop=(m == 31), skip_group_check=True)
                mm.then_inc(sem("m1_down"), 1)

            up(0)
            up(1)
            PE.wait_ge(sem("m1_comb"), 1)
            PE.transpose(bank(7)[:, 0:128], att[:, :], ident[:, :]).then_inc(sem("m1_combT"), 1)
            PE.wait_ge(sem("m1_h"), 1)
            PE.matmul(bank(6)[:, 0:128], shared_h, w("l1", "sdT"), start=True, stop=False,
                      skip_group_check=True)
            for u in range(8):
                context_turn_pe(u)
                if 1 <= u < 7:
                    PE.wait_ge(sem("m1_h"), u + 1)
                    up(u + 1)
                if u >= 1:
                    down(u - 1)
                context_keys_pe(u)
            down(7)

        def moe1_act():
            A.wait_ge(sem("m1_gate"), 1)
            A.activation(lr[:, 0:64], bank(6)[:, 128:192], ACT.Exp, scale=-1.0).then_inc(sem("m1_sig"), 1)
            A.wait_ge(sem("m1_up"), 1)
            sigmoid(shared_e, bank(4)[:, 0:128], sem("m1_sig"))
            for u in range(9):
                if u < 8:
                    A.wait_ge(sem("m1_up"), u + 2)
                    if u >= 2:
                        A.wait_ge(sem("m1_h"), u)
                    sigmoid(scr[:, 512 * (u % 2):512 * (u % 2) + 512], bank(2 * (u % 2)), sem("m1_sig"))
                if u:
                    context_act(u - 1)

        def moe1_dve():
            V.wait_ge(sem("m1_sig"), 1)
            V.wait_ge(sem("d_gb"), 16)
            dve_then(V.tensor_scalar(lr[:, 0:64], lr[:, 0:64], 1.0, None, ALU.add))
            dve_then(V.reciprocal(lr[:, 0:64], lr[:, 0:64]))
            dve_then(V.tensor_tensor(sm[:, :], lr[:, 0:64], gbias[:, :], ALU.add))
            dve_then(V.tensor_reduce(lw[:, 0:8], sm[:, :].rearrange("p (g e) -> p g e", g=8), AX.X, ALU.max))
            top_k(8, 4, sel[:, 0:8])
            dve_then(V.tensor_tensor(sm[:, :].rearrange("p (g e) -> p g e", g=8),
                                     sm[:, :].rearrange("p (g e) -> p g e", g=8),
                                     sel[:, 0:8].unsqueeze(2).to_broadcast([128, 8, 8]), ALU.mult))
            dve_then(V.tensor_copy(lw[:, 0:64], sm[:, :]))
            top_k(64, 6, sel[:, :])
            dve_then(V.tensor_tensor(sm[:, :], sm[:, :], sel[:, :], ALU.mult))
            dve_then(V.tensor_reduce(sc1[:, :], sm[:, :], AX.X, ALU.add))
            dve_then(V.tensor_scalar(sc1[:, :], sc1[:, :], 1e-8, None, ALU.add))
            dve_then(V.reciprocal(sc1[:, :], sc1[:, :]))
            V.tensor_scalar(att[:, :].rearrange("p (i e) -> p i e", i=2),
                            sm[:, :].unsqueeze(1).to_broadcast([128, 2, 64]), sc1[:, :], None, ALU.mult)\
                .then_inc(sem("m1_comb"), 1)
            V.wait_ge(sem("m1_combT"), 1)
            dve_then(V.tensor_copy(attT[:, :], bank(7)[:, 0:128]))
            V.wait_ge(sem("m1_sig"), 2)
            dve_then(V.tensor_tensor(shared_e, bank(4)[:, 0:128], shared_e, ALU.mult))
            V.tensor_tensor(shared_h, bank(5)[:, 0:128], shared_e, ALU.mult).then_inc(sem("m1_h"), 1)
            for u in range(8):
                b = 2 * (u % 2)
                e = scr[:, 512 * (u % 2):512 * (u % 2) + 512]
                context_first_dve(u)
                V.wait_ge(sem("m1_sig"), u + 3)
                dve_then(V.tensor_tensor(e, bank(b), e, ALU.mult))
                dve_then(V.tensor_tensor(e, bank(b + 1), e, ALU.mult))
                if u >= 2:
                    V.wait_ge(sem("m1_down"), u - 1)
                V.tensor_tensor(scr[:, 1024 + 512 * (u % 2):1536 + 512 * (u % 2)]
                                .rearrange("p (m t) -> p m t", m=4),
                                e.rearrange("p (m t) -> p m t", m=4),
                                attT[:, :].unsqueeze(1).to_broadcast([128, 4, T]), ALU.mult)\
                    .then_inc(sem("m1_h"), 1)
                context_rest_dve(u)
            V.wait_ge(sem("m1_down"), 8)
            dve_then(V.tensor_tensor(x[:, :], bank(6)[:, 0:128], x[:, :], ALU.add))

        KL = S + T
        KQ = KL + T
        kq2 = KR[:, 0:KQ]
        aux = KR[:, 2304:2304 + KQ]
        vv = KR[:, 4608:4608 + 17 * D].rearrange("p (c d) -> p c d", c=17)
        pp = KR[:, 6784:6784 + KL]
        ppT = KR[:, 8960:8960 + 17 * D].rearrange("p (c q) -> p c q", c=17)
        xcn = KR[0:C, 11136:13184]
        kt3 = KR[:, 13312:13312 + S]
        onesb = ones[0:1, :].bitcast(BF16).rearrange("p (n i) -> p n i", i=2)[:, :, 1]
        mask3u = KR[:, 15872:15872 + 512].bitcast(U8)
        sums = rec
        mrow8 = KR[0:1, 15360:15360 + 512].bitcast(U8)
        l2s = pbuf[:, :, :].rearrange("p a b -> p (a b)")
        mrow = l2s[0:1, 1024:1024 + KL // 2].bitcast(BF16)
        lnT, qm = l2s[:, 0:128], l2s[:, 128:384].rearrange("p (h q) -> p h q", h=2)

        CJ = 4

        def chunk(j, n=512):
            return slice(512 * j, 512 * j + n)

        def context_turn_pe(u):
            if u >= CJ:
                return
            if u == 0:
                PE.wait_ge(sem("ctx_norm"), 1)
            else:
                PE.wait_ge(sem("xa_ctx"), u)
            if u >= 3:
                PE.wait_ge(sem("xa_clamped"), u - 2)
            for c in range(4 * u, 4 * u + 4):
                mm = PE.transpose(bank(4)[0:C, 128 * (c % 4):128 * (c % 4) + 128], ctx1[:, c, 0:C], ident[:, :])
            mm.then_inc(sem("xa_turned"), 1)

        def context_keys_pe(u):
            j = u - 1
            if 0 <= j < CJ:
                PE.wait_ge(sem("xa_ctx"), j + 1)
                if j:
                    PE.wait_ge(sem("xa_key_out"), j)
                PE.matmul(bank(5), w("l2", "wkvT")[:, 0:128], xcn[:, chunk(j)], start=True, stop=True)\
                    .then_inc(sem("xa_key"), 1)
                if j:
                    PE.wait_ge(sem("xa_value_out"), j)
                for c in range(4 * j, 4 * j + 4):
                    mm = PE.matmul(bank(7)[:, 128 * (c % 4):128 * (c % 4) + 128], xcn[:, 128 * c:128 * c + 128],
                                   w("l2", "wkvT")[:, 128:256], start=True, stop=True)
                mm.then_inc(sem("xa_value"), 1)
            j = u - 2
            if 0 <= j < CJ:
                PE.wait_ge(sem("xa_key_square"), j + 1)
                PE.wait_ge(sem("xa_ctx"), min(u + 1, CJ))
                if j:
                    PE.wait_ge(sem("xa_clamped"), j)
                PE.matmul(bank(4), half64[:, :], aux[:, chunk(j)], start=True, stop=True)\
                    .then_inc(sem("xa_length"), 1)

        def context_act(u):
            if u < CJ:
                A.wait_ge(sem("xa_turned"), u + 1)
                A.activation(xcn[:, chunk(u)], bank(4)[0:C, :], ACT.Identity, bias=w("l2", "lxb"),
                             scale=w("l2", "lxg")).then_inc(sem("xa_ctx"), 1)
            j = u - 1
            if 0 <= j < CJ:
                A.wait_ge(sem("xa_key"), j + 1)
                A.activation(kq2[:, chunk(j)], bank(5), ACT.Copy).then_inc(sem("xa_key_out"), 1)
                A.wait_ge(sem("xa_key_out"), j + 1)
                A.activation(aux[:, chunk(j)], kq2[:, chunk(j)], ACT.Square).then_inc(sem("xa_key_square"), 1)
            j = u - 2
            if 0 <= j < CJ:
                A.wait_ge(sem("xa_clamped"), j + 1)
                act_then(A.activation(aux[:, chunk(j)], aux[:, chunk(j)], ACT.Ln))
                A.activation(aux[:, chunk(j)], aux[:, chunk(j)], ACT.Exp, scale=-0.5)\
                    .then_inc(sem("xa_key_rstd"), 1)

        def context_first_dve(u):
            j = u - 3
            if 0 <= j < CJ:
                V.wait_ge(sem("xa_key_rstd"), j + 1)
                V.scalar_tensor_tensor(kq2[:, chunk(j)], kq2[:, chunk(j)], w("l2", "kng"), aux[:, chunk(j)],
                                       ALU.mult, ALU.mult)

        def context_rest_dve(u):
            j = u - 1
            if 0 <= j < CJ:
                V.wait_ge(sem("xa_value"), j + 1)
                V.tensor_copy(vv[:, 4 * j:4 * j + 4, :].rearrange("p c d -> p (c d)"), bank(7))\
                    .then_inc(sem("xa_value_out"), 1)
            j = u - 2
            if 0 <= j < CJ:
                V.wait_ge(sem("xa_length"), j + 1)
                V.tensor_scalar(aux[:, chunk(j)], bank(4), 1e-16, None, ALU.max).then_inc(sem("xa_clamped"), 1)

        SJ = 5

        def x2_scores_pe(h, j):
            n = min(512, KL - 512 * j)
            PE.matmul(bank(j)[:, 0:n], qm[:, h, :], kq2[:, chunk(j, n)], start=True, stop=False)
            return PE.matmul(bank(j)[:, 0:n], onesb, mrow[:, chunk(j, n)], start=False, stop=True)

        def x2_turn_pe(h, i):
            PE.wait_ge(sem("x2_exp"), SJ * h + i + 1)
            if i >= 2 or h == 1:
                PE.wait_ge(sem("x2_te"), SJ * h + i - 1)
            if h == 1 and i == 1:
                PE.wait_ge(sem("x2_te"), SJ)
            for c in range(4 * i, min(4 * i + 4, 17)):
                mm = PE.transpose(bank(5 + i % 2)[:, 128 * (c % 4):128 * (c % 4) + 128],
                                  pp[:, 128 * c:128 * c + 128], ident[:, :])
            mm.then_inc(sem("x2_t"), 1)

        def x2_products_pe(h, i):
            PE.wait_ge(sem("x2_te"), SJ * h + i + 1)
            for c in range(4 * i, min(4 * i + 4, 17)):
                mm = PE.matmul(bank(7)[:, 64 * h:64 * h + 64], ppT[:, c, :], vv[:, c, 64 * h:64 * h + 64],
                               start=(c == 0), stop=(c == 16))
            if i == SJ - 1:
                mm.then_inc(sem("x2_mm"), 1)

        def x2_pe():
            values3_pe(0)
            PE.wait_ge(sem("x2_dve"), 1)
            PE.transpose(bank(4)[:, 0:128], att[:, :], ident[:, :]).then_inc(sem("x2_mm"), 1)
            PE.wait_ge(sem("x2_dve"), 2)
            PE.matmul(bank(4)[:, 128:256], w("l2", "wlT")[:, 0:128], lnT, start=True, stop=True)
            PE.matmul(bank(4)[:, 256:384], w("l2", "wqT"), lnT, start=True, stop=True)
            PE.matmul(bank(4)[:, 384:512], lnT, w("l2", "wlT")[:, 128:256], start=True, stop=True)\
                .then_inc(sem("x2_mm"), 1)
            PE.wait_ge(sem("x2_square"), 1)
            PE.matmul(bank(5)[:, 0:256], half64[:, :], aux[:, S:KQ], start=True, stop=True)\
                .then_inc(sem("x2_mm"), 1)
            PE.wait_ge(sem("v3_ev"), 1)
            values3_pe(1)
            PE.wait_ge(sem("x2_mask"), 1)
            PE.wait_ge(sem("x2_dve"), 3)
            for j in range(SJ):
                mm = x2_scores_pe(0, j)
                if j in (1, 3, 4):
                    mm.then_inc(sem("x2_s"), 1)
            values3_pe(2)
            PE.wait_ge(sem("v3_ev"), 3)
            for j in range(SJ):
                PE.wait_ge(sem("x2_exp"), j + 1)
                mm = x2_scores_pe(1, j)
                if j in (1, 3, 4):
                    mm.then_inc(sem("x2_s"), 1)
                x2_turn_pe(0, j)
            for j in range(SJ):
                x2_products_pe(0, j)
            for j in range(SJ):
                x2_turn_pe(1, j)
                if j:
                    x2_products_pe(1, j - 1)
            x2_products_pe(1, SJ - 1)
            PE.wait_ge(sem("x2_dve"), 5)
            PE.transpose(bank(0)[:, 0:128], att[:, :], ident[:, :]).then_inc(sem("x2_mm"), 1)
            PE.wait_ge(sem("x2_dve"), 6)
            PE.matmul(bank(1)[:, 0:128], attT[:, :], w("l2", "woT"), start=True, stop=False)
            PE.matmul(bank(1)[:, 0:128], ones[0:1, :], w("l2", "bo"), start=False, stop=True)\
                .then_inc(sem("x2_mm"), 1)

        def x2_act():
            A.wait_ge(sem("x2_ls"), 1)
            act_then(A.activation(lnv[:, :], mv[:, 1:2], ACT.Ln, bias=eps[:, :]))
            A.activation(rstd[:, :], lnv[:, :], ACT.Exp, scale=-0.5).then_inc(sem("x2_r"), 1)
            A.wait_ge(sem("k3_masked"), 1)
            values3_act(0)
            A.wait_ge(sem("x2_lat"), 1)
            A.activation(aux[:, S:KQ], kq2[:, S:KQ], ACT.Square).then_inc(sem("x2_square"), 1)
            A.wait_ge(sem("x2_lat"), 2)
            act_then(A.activation(aux[:, S:KQ], aux[:, S:KQ], ACT.Ln))
            A.activation(aux[:, S:KQ], aux[:, S:KQ], ACT.Exp, scale=-0.5).then_inc(sem("x2_r"), 1)
            values3_act(1)
            values3_act(2)
            for h in range(2):
                A.wait_ge(sem("x2_m"), h + 1)
                for j in range(SJ):
                    n = min(512, KL - 512 * j)
                    if h == 1:
                        A.wait_ge(sem("x2_t"), j + 1)
                    A.activation(pp[:, chunk(j, n)], bank(j)[:, 0:n], ACT.Exp, bias=nm[:, h:h + 1],
                                 accum_out=sums[:, SJ * h + j:SJ * h + j + 1]).then_inc(sem("x2_exp"), 1)

        def x2_dve():
            dve_then(V.bn_stats(st[:, :], xn[:, :]))
            V.bn_aggr(mv[:, :], st[:, :]).then_inc(sem("x2_ls"), 1)
            V.wait_ge(sem("x2_r"), 1)
            V.wait_ge(sem("x2_ls"), 1)
            V.tensor_scalar(att[:, :], xn[:, :], mv[:, 0:1], rstd[:, :], ALU.subtract, ALU.mult)\
                .then_inc(sem("x2_dve"), 1)
            V.wait_ge(sem("x2_mm"), 1)
            V.tensor_scalar(lnT, bank(4)[:, 0:128], w("l2", "llg"), w("l2", "llb"), ALU.mult, ALU.add)\
                .then_inc(sem("x2_dve"), 1)
            V.wait_ge(sem("x2_mm"), 2)
            V.tensor_copy(kq2[:, S:KQ], bank(4)[:, 128:384]).then_inc(sem("x2_lat"), 1)
            dve_then(V.tensor_copy(vv[:, 16, :], bank(4)[:, 384:512]))
            V.wait_ge(sem("x2_mm"), 3)
            V.tensor_scalar(aux[:, S:KQ], bank(5)[:, 0:256], 1e-16, None, ALU.max).then_inc(sem("x2_lat"), 1)
            V.wait_ge(sem("x2_r"), 2)
            dve_then(V.scalar_tensor_tensor(kq2[:, S:KL], kq2[:, S:KL], w("l2", "kng"), aux[:, S:KL],
                                            ALU.mult, ALU.mult))
            dve_then(V.scalar_tensor_tensor(kq2[:, KL:KQ], kq2[:, KL:KQ], w("l2", "qng"), aux[:, KL:KQ],
                                            ALU.mult, ALU.mult))
            for h in range(2):
                dve_then(V.tensor_scalar(qm[:, h, :], kq2[:, KL:KQ], mh[:, h:h + 1], 64 ** -0.5,
                                         ALU.mult, ALU.mult))
            V.sem_inc(sem("x2_dve"), 1)
            V.wait_ge(sem("d_m3"), 16)
            V.tensor_scalar(mrow3, mask3u[0:1, :], -1.0, BIG, ALU.add, ALU.mult).then_inc(sem("mrow3"), 1)

            def largest(h, part):
                V.wait_ge(sem("x2_s"), 3 * h + part + 1)
                dve_then(V.tensor_reduce(pm[:, part:part + 1], ps[:, 1024 * part:min(1024 * part + 1024, KL)], AX.X,
                                         ALU.max, negate=True))
                if part == 2:
                    V.tensor_reduce(nm[:, h:h + 1], pm[:, 0:3], AX.X, ALU.min).then_inc(sem("x2_m"), 1)

            for part in range(3):
                largest(0, part)
            for h in range(2):
                for i in range(SJ):
                    V.wait_ge(sem("x2_t"), SJ * h + i + 1)
                    if h == 1 and i == 0:
                        V.wait_ge(sem("x2_mm"), 4)
                    n = min(4, 17 - 4 * i)
                    V.tensor_copy(ppT[:, 4 * i:4 * i + n, :].rearrange("p c q -> p (c q)"),
                                  bank(5 + i % 2)[:, 0:128 * n]).then_inc(sem("x2_te"), 1)
                    if h == 0 and i in (1, 3, 4):
                        largest(1, i // 2)
                V.wait_ge(sem("x2_mm"), 4 + h)
                V.wait_ge(sem("x2_exp"), SJ * h + SJ)
                dve_then(V.tensor_reduce(sc1[:, :], sums[:, SJ * h:SJ * h + SJ], AX.X, ALU.add))
                dve_then(V.reciprocal(sc1[:, :], sc1[:, :]))
                V.tensor_scalar(att[:, 64 * h:64 * h + 64], bank(7)[:, 64 * h:64 * h + 64], sc1[:, :], None,
                                ALU.mult).then_inc(sem("x2_dve"), 1)
            V.wait_ge(sem("x2_mm"), 6)
            V.tensor_copy(attT[:, :], bank(0)[:, 0:128]).then_inc(sem("x2_dve"), 1)
            V.wait_ge(sem("x2_mm"), 7)
            dve_then(V.tensor_tensor(x[:, :], bank(1)[:, 0:128], x[:, :], ALU.add))

        fk, fq, ve, fe = (l2s[:, 512 + 256 * i:768 + 256 * i] for i in range(4))
        kvm = l2s[:, 1536:1536 + 144]

        def lin_pe():
            PE.matmul(bank(0)[:, 0:128], w("l2", "aq"), xnT[:, :], start=True, stop=True)
            PE.matmul(bank(1)[:, 0:128], xnT[:, :], w("l2", "ak"), start=True, stop=False)
            PE.matmul(bank(1)[:, 0:128], ones[0:1, :], w("l2", "abk"), start=False, stop=True)\
                .then_inc(sem("li_mm"), 1)
            PE.matmul(bank(2)[:, 0:128], xnT[:, :], w("l2", "av"), start=True, stop=False)
            PE.matmul(bank(2)[:, 0:128], ones[0:1, :], w("l2", "abv"), start=False, stop=True)\
                .then_inc(sem("li_mm"), 1)
            PE.wait_ge(sem("li_dve"), 3)
            PE.matmul(bank(3)[:, 0:129], fk[:, 0:128], ve[:, 0:129], start=True, stop=True)\
                .then_inc(sem("li_mm"), 1)
            PE.wait_ge(sem("li_dve"), 4)
            PE.matmul(bank(4)[:, 0:144], fq[:, 0:128], kvm, start=True, stop=True)\
                .then_inc(sem("li_mm"), 1)
            PE.wait_ge(sem("li_dve"), 5)
            PE.transpose(bank(5)[:, 0:128], att[:, :], ident[:, :]).then_inc(sem("li_mm"), 1)
            PE.wait_ge(sem("li_dve"), 6)
            PE.matmul(bank(6)[:, 0:128], attT[:, :], w("l2", "ao"), start=True, stop=False)
            PE.matmul(bank(6)[:, 0:128], ones[0:1, :], w("l2", "abo"), start=False, stop=True)\
                .then_inc(sem("li_mm"), 1)

        def lin_act():
            A.wait_ge(sem("li_dve"), 1)
            A.activation(fe[:, 0:128], fe[:, 0:128], ACT.Exp).then_inc(sem("li_act"), 1)
            A.wait_ge(sem("li_dve"), 2)
            A.activation(fe[:, 128:256], fe[:, 128:256], ACT.Exp).then_inc(sem("li_act"), 1)

        def lin_dve():
            V.wait_ge(sem("li_mm"), 1)
            dve_then(V.tensor_scalar(fq[:, 128:256], bank(0)[:, 0:128], w("l2", "abq"), None, ALU.add))
            V.tensor_scalar(fe[:, 0:128], fq[:, 128:256], 0.0, None, ALU.min).then_inc(sem("li_dve"), 1)
            V.tensor_scalar(fe[:, 128:256], bank(1)[:, 0:128], 0.0, None, ALU.min).then_inc(sem("li_dve"), 1)
            dve_then(V.memset(ve[:, 128:129], 1.0))
            V.wait_ge(sem("li_mm"), 2)
            dve_then(V.tensor_copy(ve[:, 0:128], bank(2)[:, 0:128]))
            V.wait_ge(sem("li_act"), 1)
            dve_then(V.scalar_tensor_tensor(fq[:, 0:128], fq[:, 128:256], 0.0, fe[:, 0:128], ALU.max, ALU.add))
            V.wait_ge(sem("li_act"), 2)
            V.scalar_tensor_tensor(fk[:, 0:128], bank(1)[:, 0:128], 0.0, fe[:, 128:256], ALU.max, ALU.add)\
                .then_inc(sem("li_dve"), 1)
            V.wait_ge(sem("li_mm"), 3)
            dve_then(V.tensor_tensor(kvm[:, 0:128].rearrange("p (h d) -> p h d", h=H),
                                     bank(3)[:, 0:128].rearrange("p (h d) -> p h d", h=H),
                                     m8[:, :].unsqueeze(2).to_broadcast([128, H, HD]), ALU.mult))
            dve_then(V.tensor_copy(sc1[:, :], bank(3)[:, 128:129]))
            V.tensor_scalar(kvm[:, 128:144], m8[:, :], sc1[:, :], None, ALU.mult).then_inc(sem("li_dve"), 1)
            V.wait_ge(sem("li_mm"), 4)
            dve_then(V.tensor_scalar(rec[:, :], bank(4)[:, 128:144], 1e-6, None, ALU.max))
            dve_then(V.reciprocal(rec[:, :], rec[:, :]))
            V.tensor_tensor(att[:, :].rearrange("p (h d) -> p h d", h=H),
                            bank(4)[:, 0:128].rearrange("p (h d) -> p h d", h=H),
                            rec[:, :].unsqueeze(2).to_broadcast([128, H, HD]), ALU.mult)\
                .then_inc(sem("li_dve"), 1)
            V.wait_ge(sem("li_mm"), 5)
            V.tensor_copy(attT[:, :], bank(5)[:, 0:128]).then_inc(sem("li_dve"), 1)
            V.wait_ge(sem("li_mm"), 6)
            dve_then(V.tensor_tensor(x[:, :], bank(6)[:, 0:128], x[:, :], ALU.add))

        ew = w32[:, 4096:8192]

        def moe2_pe():
            PE.matmul(bank(7)[:, 128:160], xnT[:, :], w("l2", "rwT"), start=True, stop=True)\
                .then_inc(sem("m2_gate"), 1)
            PE.wait_ge(sem("d_ew"), 16)
            for u in range(8):
                if u >= 4:
                    PE.wait_ge(sem("m2_acc"), 4 * (u - 3))
                PE.matmul(bank(u % 4), xnT[:, :], ew[:, 512 * u:512 * u + 512], start=True, stop=True)\
                    .then_inc(sem("m2_mm"), 1)

        def moe2_act():
            A.wait_ge(sem("m2_s"), 1)
            A.activation(sm[:, 0:32], bank(7)[:, 128:160], ACT.Exp, bias=nm[:, 0:1], accum_out=sc1[:, :])\
                .then_inc(sem("m2_e"), 1)

        def moe2_dve():
            V.wait_ge(sem("m2_gate"), 1)
            V.tensor_reduce(nm[:, 0:1], bank(7)[:, 128:160], AX.X, ALU.max, negate=True).then_inc(sem("m2_s"), 1)
            V.wait_ge(sem("m2_e"), 1)
            dve_then(V.reciprocal(sc1[:, :], sc1[:, :]))
            dve_then(V.tensor_scalar(lw[:, 0:32], sm[:, 0:32], sc1[:, :], None, ALU.mult))
            top_k(32, 2, sel[:, 0:32])
            dve_then(V.tensor_tensor(sel[:, 0:32], sel[:, 0:32], lw[:, 0:32], ALU.mult))
            for e in range(32):
                if e % 4 == 0:
                    V.wait_ge(sem("m2_mm"), e // 4 + 1)
                if e >= 2:
                    V.wait_ge(sem("m2_acc"), e - 1)
                y, acc = bank(e // 4 % 4)[:, 128 * (e % 4):128 * (e % 4) + 128], (x, att)[e % 2]
                if e == 1:
                    V.tensor_scalar(acc[:, :], y, sel[:, e:e + 1], None, ALU.mult).then_inc(sem("m2_acc"), 1)
                else:
                    V.scalar_tensor_tensor(acc[:, :], y, sel[:, e:e + 1], acc[:, :], ALU.mult, ALU.add)\
                        .then_inc(sem("m2_acc"), 1)
            V.wait_ge(sem("m2_acc"), 32)
            dve_then(V.tensor_tensor(x[:, :], x[:, :], att[:, :], ALU.add))

        q3 = l2s[:, 0:128]
        v3s = l2s[:, 128:128 + H * (HD + 1)].rearrange("p (h d) -> p h d", h=H)
        kbd = r32[:, 0:2048]
        s3 = r32[:, 2048:4096]
        p3T = r32[:, 4096:6144]

        def self_pe():
            PE.matmul(bank(0)[:, 0:128], w("l3", "sqT"), xnT[:, :], start=True, stop=True)
            PE.matmul(bank(1)[:, 0:128], w("l3", "skT"), xnT[:, :], start=True, stop=True)
            PE.matmul(bank(2)[:, 0:128], xnT[:, :], w("l3", "svT"), start=True, stop=True)\
                .then_inc(sem("sa_mm"), 1)
            for g in range(4):
                PE.wait_ge(sem("sa_k"), g + 1)
                PE.matmul(bank(4 + g), q3, kbd[:, chunk(g)], start=True, stop=True).then_inc(sem("sa_s"), 1)

            def turn(g):
                PE.wait_ge(sem("sa_exp"), g + 1)
                for h in range(4 * g, 4 * g + 4):
                    mm = PE.transpose(bank(g)[:, 128 * (h % 4):128 * (h % 4) + 128],
                                      s3[:, 128 * h:128 * h + 128], ident[:, :])
                mm.then_inc(sem("sa_t"), 1)

            turn(0)
            for g in range(4):
                if g < 3:
                    turn(g + 1)
                PE.wait_ge(sem("sa_te"), g + 1)
                for h in range(4 * g, 4 * g + 4):
                    mm = PE.matmul(bank(4)[:, 9 * h:9 * h + 9], p3T[:, 128 * h:128 * h + 128],
                                   v3s[:, h, :], start=True, stop=True)
            mm.then_inc(sem("sa_mm"), 1)

        def self_act():
            for g in range(4):
                A.wait_ge(sem("sa_less"), g + 1)
                A.activation(s3[:, chunk(g)], s3[:, chunk(g)], ACT.Exp).then_inc(sem("sa_exp"), 1)
                if g:
                    A.wait_ge(sem("sa_t"), g)
                    A.activation(p3T[:, chunk(g - 1)], bank(g - 1), ACT.Copy).then_inc(sem("sa_te"), 1)
            A.wait_ge(sem("sa_t"), 4)
            A.activation(p3T[:, chunk(3)], bank(3), ACT.Copy).then_inc(sem("sa_te"), 1)

        def self_dve():
            V.wait_ge(sem("sa_mm"), 1)
            dve_then(V.tensor_scalar(q3, bank(0)[:, 0:128], HD ** -0.5, None, ALU.mult))

            def heads(t):
                return t.rearrange("p (h k) -> p h k", h=QH)

            def own_keys(g):
                V.tensor_tensor(heads(kbd[:, chunk(g)]), bank(1)[:, 0:128].unsqueeze(1).to_broadcast([128, QH, 128]),
                                m8[:, QH * g:QH * g + QH].unsqueeze(2).to_broadcast([128, QH, 128]), ALU.mult)\
                    .then_inc(sem("sa_k"), 1)

            def less_maxima(g):
                V.wait_ge(sem("sa_s"), g + 1)
                q = slice(QH * g, QH * g + QH)
                dve_then(V.tensor_reduce(nm[:, q], heads(bank(4 + g)), AX.X, ALU.max))
                V.tensor_tensor(heads(s3[:, chunk(g)]), heads(bank(4 + g)),
                                nm[:, q].unsqueeze(2).to_broadcast([128, QH, 128]), ALU.subtract)\
                    .then_inc(sem("sa_less"), 1)

            own_keys(0)
            own_keys(1)
            V.tensor_copy(v3s[:, :, 0:HD], bank(2)[:, 0:128].rearrange("p (h d) -> p h d", h=H))
            dve_then(V.memset(v3s[:, :, HD:HD + 1], 1.0))
            own_keys(2)
            less_maxima(0)
            own_keys(3)
            for g in range(1, 4):
                less_maxima(g)
            V.wait_ge(sem("sa_mm"), 2)
            o = bank(4)[:, 0:H * (HD + 1)].rearrange("p (h d) -> p h d", h=H)
            dve_then(V.reciprocal(rec[:, :], o[:, :, HD]))
            dve_then(V.tensor_tensor(att[:, :].rearrange("p (h d) -> p h d", h=H), o[:, :, 0:HD],
                                     rec[:, :].unsqueeze(2).to_broadcast([128, H, HD]), ALU.mult))
            dve_then(V.tensor_tensor(x[:, :], att[:, :], x[:, :], ALU.add))

        f8 = sb("f8", [128, 128], FP8)
        fb = sb("fb", [128, 128], BF16)
        fy = sb("fy", [128, 128], BF16)
        fout = sb("fout", [128, 128], BF16)
        u8m = attT[:, :].bitcast(mybir.dt.uint32)

        def quantise(src, dst):
            dve_then(V.tensor_scalar(r1[:, :], src, 240.0, -240.0, ALU.min, ALU.max))
            dve_then(V.tensor_copy(f8[:, :], r1[:, :], saturate=False))
            dve_then(V.tensor_copy(dst, f8[:, :]))
            dve_then(V.tensor_scalar(r1[:, :], src, 0.5, 240.0, ALU.mult, ALU.min))
            dve_then(V.tensor_scalar(r1[:, :], r1[:, :], -240.0, None, ALU.max))
            dve_then(V.tensor_copy(f8[:, :], r1[:, :], saturate=False))
            dve_then(V.tensor_scalar(r1[:, :], f8[:, :], 2.0, None, ALU.mult))
            dve_then(V.tensor_tensor(r2[:, :], r1[:, :], r1[:, :], ALU.mult))
            dve_then(V.tensor_scalar(r2[:, :], r2[:, :], 480.0 ** 2, 3e38, ALU.is_ge, ALU.mult))
            dve_then(V.tensor_scalar(r2[:, :], r2[:, :], 3e38, None, ALU.mult))
            dve_then(V.tensor_tensor(r1[:, :], r1[:, :], r2[:, :], ALU.add))
            dve_then(V.tensor_tensor(r1[:, :], r1[:, :], r2[:, :], ALU.subtract))
            dve_then(V.tensor_tensor(r2[:, :], src, src, ALU.mult))
            dve_then(V.tensor_scalar(u8m[:, :], r2[:, :], 240.0 ** 2, None, ALU.is_gt))
            dve_then(V.tensor_copy(fb[:, :], r1[:, :]))
            dve_then(V.copy_predicated(dst, u8m[:, :], fb[:, :]))

        def fp8_pe():
            PE.wait_ge(sem("f_q"), 1)
            PE.transpose(bank(0).bitcast(BF16)[:, 0:128], fy[:, :], identb[:, :]).then_inc(sem("f_mm"), 1)
            PE.wait_ge(sem("f_q"), 2)
            PE.matmul(bank(1)[:, 0:128], fout[:, :], kq[:, :], start=True, stop=True).then_inc(sem("f_mm"), 1)

        def fp8_weights_dve():
            V.wait_ge(sem("d_f"), 64)
            dve_then(V.reciprocal(sc1[:, :], skk[:, :]))
            dve_then(V.tensor_scalar(kq32[:, :], kq[:, :], sc1[:, :], None, ALU.mult))
            quantise(kq32[:, :], kq[:, :])
            dve_then(V.reciprocal(inv_in[:, :], sin[:, :]))
            dve_then(V.tensor_tensor(skk[:, :], skk[:, :], sin[:, :], ALU.mult))

        def fp8_dve():
            dve_then(V.tensor_copy(fb[:, :], xn[:, :]))
            dve_then(V.tensor_scalar(kq32[:, :], fb[:, :], inv_in[:, :], None, ALU.mult))
            quantise(kq32[:, :], fy[:, :])
            V.sem_inc(sem("f_q"), 1)
            V.wait_ge(sem("f_mm"), 1)
            V.tensor_copy(fout[:, :], bank(0).bitcast(BF16)[:, 0:128]).then_inc(sem("f_q"), 1)
            V.wait_ge(sem("f_mm"), 2)
            dve_then(V.tensor_scalar(fb[:, :], bank(1)[:, 0:128], skk[:, :], None, ALU.mult))
            dve_then(V.tensor_tensor(fy[:, :], fb[:, :], fbias[:, :], ALU.add))
            V.tensor_tensor(x[:, :], x[:, :], fy[:, :], ALU.add).then_inc(sem("x_done"), 1)

        mrow3 = w32[0:1, 2560:3584].bitcast(BF16)
        mrow3h = mrow3.unsqueeze(1).to_broadcast([1, H, S])

        @block.sync
        def _(sy):
            load(sy, x[:, :], a["x"], "x")
            load(sy, ctxT[0:C, :], a["ctxT"], "ctxT")
            load(sy, packs["ctx"][:, :], a["pack_ctx"], "ctx")
            load(sy, r32[:, 0:H * DH0], a["pack_x0"][:, 0:H * DH0], "x0")
            load(sy, r32[:, H * DH0:lay["x0"][1]], a["pack_x0"][:, H * DH0:], "x0r")
            load(sy, ctx1[:, :, 0:C], a["ctx"].rearrange("(c p) n -> p c n", p=128), "ctx1")
            load(sy, packs["l0"][:, :], a["pack_l0"], "l0")
            load(sy, packs["l1"][:, :], a["pack_l1"], "l1")
            load(sy, packs["l2"][:, :], a["pack_l2"], "l2")
            load(sy, packs["l3"][:, :], a["pack_l3"], "l3")
            load(sy, gbias[:, :], a["gbias"].to_broadcast([128, 64]), "gb")
            load(sy, kq[:, :], a["kernel"], "f")
            load(sy, fbias[:, :], a["fbias"].to_broadcast([128, 128]), "f")
            load(sy, sin[:, :], a["s_in"].to_broadcast([128, 1]), "f")
            load(sy, skk[:, :], a["s_k"].to_broadcast([128, 1]), "f")
            store_keys_sync(0)
            load(sy, w32[:, 0:4096], a["w1"], "w12")
            load(sy, w32[:, 4096:8192], a["w2"], "w12")
            sy.wait_ge(sem("x0_done"), 1)
            stack_keys_sync(0)
            load(sy, egT, a["eg"], "eg")
            load(sy, euT, a["eu"], "eg")
            sy.wait_ge(sem("m0_selT"), 2)
            load(sy, w32[:, 0:4096], a["ed"], "eg")
            load(sy, ew, a["ew"], "ew")
            sy.wait_ge(sem("mamba_done"), 1)
            load(sy, mrow8, a["mask2"], "m8")
            load(sy, mask3u, a["mask3"].to_broadcast([128, S]), "m3")
            store_keys_sync(1)
            stack_keys_sync(1)
            sy.wait_ge(sem("mrow3"), 1)
            sy.dma_start(KS[KROWS:KROWS + 1, :, :], mrow3h).then_inc(sem("d_mask3"), 16)
            sy.wait_ge(sem("ks_ones"), 2)
            sy.dma_start(qs[KROWS:KROWS + 1, :], KS[0:1, 0, 0:H * T]).then_inc(sem("d_mask3"), 16)
            sy.wait_ge(sem("x_done"), 1)
            sy.dma_start(out, x[:, :]).then_inc(sem("d_out"), 16)
            sy.wait_ge(sem("d_out"), 16)

        @block.gpsimd
        def _(g):
            pool_then(G.memset(ident[:, :], 0.0))
            pool_then(G.affine_select(out=ident[:, :], in_=ident[:, :], compare_op=ALU.not_equal, fill=1.0,
                                      base=0, pattern=[[-1, 128]], channel_multiplier=1))
            pool_then(G.memset(one[:, :], 1.0))
            pool_then(G.memset(eps[:, :], EPS))
            G.sem_inc(sem("consts"), 1)
            pool_then(G.memset(identb[:, :], 0.0))
            pool_then(G.affine_select(out=identb[:, :], in_=identb[:, :], compare_op=ALU.not_equal, fill=1.0,
                                      base=0, pattern=[[-1, 128]], channel_multiplier=1))
            pool_then(G.memset(ones[:, :], 1.0))
            pool_then(G.memset(c256[:, :], 1.0 / 256))
            pool_then(G.memset(ctx1[:, :, C:C + 1], 1.0))
            pool_then(G.memset(nmx[:, :], 0.0))
            pool_then(G.memset(nclamp[:, :], -CLAMP))
            pool_then(G.memset(npart[:, :, :], 0.0))
            pool_then(G.memset(m16[:, :], 0.0))
            for b in (0, 16, 32, 96):
                pool_then(G.affine_select(out=m16[:, :], in_=m16[:, :], compare_op=ALU.not_equal, fill=1.0,
                                          base=-b, pattern=[[-1, H]], channel_multiplier=1))
            for t, wd, n, v, inner in ((m8, HD, H, 1.0, 1), (mh, 64, 2, 1.0, 1), (half64, 64, 2, 1.0 / 64, 64)):
                pool_then(G.memset(t[:, :], v))
                view = t[:, :].rearrange("p (h i) -> p h i", h=n)
                pool_then(G.affine_select(out=view, in_=view, compare_op=ALU.is_ge, fill=0.0, base=0,
                                          pattern=[[-wd, n], [0, inner]], channel_multiplier=1))
                pool_then(G.affine_select(out=view, in_=view, compare_op=ALU.is_ge, fill=0.0, base=wd - 1,
                                          pattern=[[wd, n], [0, inner]], channel_multiplier=-1))
            G.sem_inc(sem("consts"), 1)
            pool_then(G.memset(ctxR[C:C + H, :].bitcast(F32), 1.0))
            G.wait_ge(sem("ctxR"), 1)
            G.tensor_tensor(ctxL[:, :], ctxT[0:C, :], ctxR[0:C, :].bitcast(F32), ALU.subtract).then_inc(sem("x0_low"), 1)
            for g in range(4):
                quad = slice(512 * g, 512 * g + 512)
                G.wait_ge(sem("x0_qkR"), g + 1)
                G.tensor_tensor(qkL[:, quad], QK[0:C, quad], qkR[0:C, quad].bitcast(F32), ALU.subtract)\
                    .then_inc(sem("x0_low"), 1)
            split_keys_pool(0)
            G.wait_ge(sem("x0_done"), 1)
            pool_then(G.memset(ks_region[0:SHIFT, :], TWO_ONES))
            G.sem_inc(sem("ks_ones"), 1)
            normalise_context_pool()
            G.wait_ge(sem("n_att"), 1)
            pool_then(G.memset(KR[:, 12416:12800], 0.0))
            for k in range(2):
                pool_then(G.tensor_copy(bc_w[:, k, :, :, 0:16],
                                        c2(w("l1", "xpT"))[:, :, 1 + 16 * k:17 + 16 * k].unsqueeze(2)
                                        .to_broadcast([128, 2, 3, 16])))
            G.sem_inc(sem("mb_w"), 1)
            mask_keys3_pool()
            G.wait_ge(sem("moe1_done"), 1)
            G.wait_ge(sem("d_m8"), 16)
            pool_then(G.memset(mrow[:, S:KL], 0.0))
            pool_then(G.tensor_scalar(mrow[:, 0:S], mrow8, -1.0, BIG, ALU.add, ALU.mult))
            G.sem_inc(sem("x2_mask"), 1)
            split_keys_pool(1)
            G.wait_ge(sem("k_parts"), 2)
            G.wait_ge(sem("x2_done"), 1)
            pool_then(G.memset(ks_region[0:SHIFT, :], TWO_ONES))
            G.sem_inc(sem("ks_ones"), 1)

        @block.scalar
        def _(act):
            A.preload_act_table_set("natural_log_exp_and_others")
            A.wait_ge(sem("consts"), 1)
            norm_act(0)
            A.wait_ge(sem("d_ctx"), 16)
            x0_act()
            norm_act(1)
            rec_act()
            norm_act(2)
            A.wait_ge(sem("v1_mm"), 3)
            values_act(v1, 6, range(12, NC), "v1_ev")
            moe0_act()
            norm_act(3)
            context_rstd_act()
            narrow_act(0)
            norm_act(4)
            mamba_act()
            norm_act(5)
            moe1_act()
            norm_act(6)
            x2_act()
            norm_act(7)
            lin_act()
            norm_act(8)
            moe2_act()
            norm_act(9)
            narrow_act(1)
            norm_act(10)
            self_act()
            norm_act(11)

        @block.vector
        def _(dve):
            V.wait_ge(sem("consts"), 1)
            V.wait_ge(sem("d_x"), 16)
            norm_dve(0)
            V.wait_ge(sem("d_ctxT"), 16)
            V.tensor_copy(ctxR[0:C, :], ctxT[0:C, :]).then_inc(sem("ctxR"), 1)
            x0_dve()
            V.sem_inc(sem("x0_done"), 1)
            norm_dve(1)
            rec_dve()
            norm_dve(2)
            moe0_dve()
            norm_dve(3)
            V.wait_ge(sem("d_l1"), 16)
            narrow_dve(0)
            norm_dve(4)
            mamba_dve()
            V.sem_inc(sem("mamba_done"), 1)
            norm_dve(5)
            V.wait_ge(sem("d_l2"), 16)
            moe1_dve()
            V.sem_inc(sem("moe1_done"), 1)
            norm_dve(6)
            x2_dve()
            V.sem_inc(sem("x2_done"), 1)
            norm_dve(7)
            lin_dve()
            norm_dve(8)
            moe2_dve()
            norm_dve(9)
            narrow_dve(1)
            norm_dve(10)
            self_dve()
            norm_dve(11)
            fp8_dve()

        @block.tensor
        def _(pe):
            PE.wait_ge(sem("consts"), 1)
            norm_pe(0)
            PE.wait_ge(sem("d_ctx"), 16)
            PE.wait_ge(sem("d_ctxT"), 16)
            x0_pe()
            norm_pe(1)
            rec_pe()
            norm_pe(2)
            moe0_pe()
            norm_pe(3)
            PE.wait_ge(sem("d_l1"), 16)
            narrow_pe(0)
            norm_pe(4)
            mamba_pe()
            norm_pe(5)
            PE.wait_ge(sem("d_l2"), 16)
            moe1_pe()
            PE.wait_ge(sem("d_l3"), 16)
            PE.wait_ge(sem("moe1_done"), 1)
            x2_pe()
            norm_pe(7)
            lin_pe()
            norm_pe(8)
            moe2_pe()
            norm_pe(9)
            narrow_pe(1)
            norm_pe(10)
            self_pe()
            norm_pe(11)
            fp8_pe()


def _packed(np, spec, parts):
    at = sum(cols for _, _, cols in spec)
    out = np.zeros((128, at), np.float32)
    at = 0
    for name, rows, cols in spec:
        out[0:rows, at:at + cols] = parts[name].reshape(rows, cols)
        at += cols
    return out


def kernel(**inputs):
    import numpy as np
    import concourse.bacc as _bacc
    from concourse import mybir as _mybir
    from concourse.bass_utils import run_bass_kernel_spmd as _run

    i = {k: np.asarray(v) for k, v in inputs.items()}

    def col(v, n=1):
        return v.reshape(n, -1).T

    cw = i["L1_attn_conv_w"].reshape(2, 128, 4).transpose(1, 0, 2)
    ar = {
        "x": i["x"].reshape(T, D),
        "ctx": i["ctx_768"].reshape(S, C),
        "ctxT": i["ctx_768"].reshape(S, C).T,
        "pack_ctx": _packed(np, SPEC_CTX, {
            "wk1": i["L1_xattn_Wk"], "wv1": i["L1_xattn_Wv"], "bk1": i["L1_xattn_bk"]}),
        "pack_x0": _packed(np, SPEC_X0, {
            "wq": i["L0_xattn_Wq"],
            "wkT": i["L0_xattn_Wk"].reshape(C, H, DH0).transpose(2, 1, 0),
            "wv": i["L0_xattn_Wv"],
            "wo": i["L0_xattn_Wo"].reshape(H, DH0, D).transpose(1, 0, 2),
            "bo": i["L0_xattn_bo"]}),
        "pack_l0": _packed(np, SPEC_L0, {
            "waT": i["L0_attn_Wa_w"].T, "wab": i["L0_attn_Wa_b"], "bT": i["L0_attn_B_w"].T,
            "cT": i["L0_attn_C_w"].T, "dT": i["L0_attn_D_w"].T, "gw": i["L0_ffn_gate_w"],
            "gb": i["L0_ffn_gate_b"], "b1": i["L0_ffn_b1"].reshape(8, 4, 128).transpose(2, 0, 1),
            "b2": i["L0_ffn_b2"]}),
        "pack_l1": _packed(np, SPEC_L1, {
            "wq": i["L1_xattn_Wq"], "bq": i["L1_xattn_bq"], "bv": i["L1_xattn_bv"], "wo": i["L1_xattn_Wo"],
            "bo": i["L1_xattn_bo"], "inT": i["L1_attn_in_proj_w"].T, "convw": cw,
            "convb": col(i["L1_attn_conv_b"], 2),
            "xpT": i["L1_attn_x_proj_w"].reshape(33, 2, 128).transpose(2, 1, 0),
            "alog": i["L1_attn_A_log"].reshape(2, 128, 16).transpose(1, 0, 2),
            "dpar": col(i["L1_attn_D_param"], 2), "dtw": col(i["L1_attn_dt_w"], 2),
            "dtb": col(i["L1_attn_dt_b"], 2),
            "outT": i["L1_attn_out_w"].reshape(D, 2, 128).transpose(2, 1, 0),
            "lng": col(i["L1_attn_ln_g"], 2), "lnb": col(i["L1_attn_ln_b"], 2),
            "gateT": i["L1_ffn_gate_w"].T, "sgT": i["L1_ffn_sg_w"].T, "suT": i["L1_ffn_su_w"].T,
            "sdT": i["L1_ffn_sd_w"].T}),
        "pack_l2": _packed(np, SPEC_L2, {
            "wkvT": i["L2_xattn_Wkv"].T, "wqT": i["L2_xattn_Wq"].T, "wlT": i["L2_xattn_Wlkv"].T,
            "woT": i["L2_xattn_Wo"].T, "bo": i["L2_xattn_bo"], "lxg": i["L2_xattn_ln_x_g"],
            "lxb": i["L2_xattn_ln_x_b"], "llg": i["L2_xattn_ln_l_g"], "llb": i["L2_xattn_ln_l_b"],
            "qng": np.concatenate([i["L2_xattn_qn_g"]] * 2), "kng": np.concatenate([i["L2_xattn_kn_g"]] * 2),
            "aq": i["L2_attn_Wq"], "ak": i["L2_attn_Wk"], "av": i["L2_attn_Wv"], "ao": i["L2_attn_Wo"],
            "abq": i["L2_attn_bq"], "abk": i["L2_attn_bk"], "abv": i["L2_attn_bv"], "abo": i["L2_attn_bo"],
            "rwT": i["L2_ffn_router_w"].T}),
        "pack_l3": _packed(np, SPEC_L3, {
            "wq": i["L3_xattn_Wq"], "wk": i["L3_xattn_Wk"], "wv": i["L3_xattn_Wv"], "wo": i["L3_xattn_Wo"],
            "sqT": i["L3_attn_Wq"].T, "skT": i["L3_attn_Wk"].T, "svT": i["L3_attn_Wv"].T}),
        "w1": i["L0_ffn_w1"].transpose(1, 0, 2).reshape(D, 4096),
        "w2": i["L0_ffn_w2"].reshape(8, 4, 128, D).transpose(2, 0, 1, 3).reshape(128, 4096),
        "eg": i["L1_ffn_eg_w"].transpose(2, 1, 0).reshape(D, 4096),
        "eu": i["L1_ffn_eu_w"].transpose(2, 1, 0).reshape(D, 4096),
        "ed": i["L1_ffn_ed_w"].transpose(2, 0, 1).reshape(32, 128, D).transpose(1, 0, 2).reshape(128, 4096),
        "ew": i["L2_ffn_expert_weights"].transpose(1, 0, 2).reshape(D, 4096),
        "gbias": i["L1_ffn_gate_bias"].reshape(1, 64),
        "kernel": i["L3_ffn_kernel"],
        "fbias": i["L3_ffn_bias"].reshape(1, D),
        "s_in": i["L3_ffn_input_scale"].reshape(1, 1),
        "s_k": i["L3_ffn_kernel_scale"].reshape(1, 1),
        "mask2": i["mask_BxS2_bk0"].reshape(1, S),
        "mask3": i["mask_BxS2_bf1"].reshape(1, S),
    }
    nc = _bacc.Bacc("TRN2", target_bir_lowering=False, num_devices=1)
    arrays, aps = {}, {}
    for name, v in ar.items():
        v = np.ascontiguousarray(v)
        arrays["in_" + name] = v
        aps[name] = nc.dram_tensor("in_" + name, v.shape, _mybir.dt.from_np(v.dtype), kind="ExternalInput").ap()
    res = nc.dram_tensor("out_0", (T, D), _mybir.dt.float32, kind="ExternalOutput").ap()
    perceiver(nc, aps, res)
    r = _run(nc, [arrays], core_ids=[0])
    return r.results[0]["out_0"].reshape(1, T, D)
```
